# Optimizing a Trainium2 kernel written in Bass

```python
import numpy as np
import jax
import jax.numpy as jnp

def _softmax(x, axis=-1):
    return jax.nn.softmax(x, axis=axis)

def _gelu(x):
    return jax.nn.gelu(x, approximate=True)

def _silu(x):
    return jax.nn.silu(x)

def _sigmoid(x):
    return jax.nn.sigmoid(x)

def _layernorm(x, axis=-1, eps=1e-05):
    m = jnp.mean(x, axis=axis, keepdims=True)
    v = jnp.var(x, axis=axis, keepdims=True)
    return (x - m) / jnp.sqrt(v + eps)

def _scatter_add(tgt, idx, src, axis=0):
    return tgt.at[idx].add(src)

def _segment_sum(src, seg, n):
    return jax.ops.segment_sum(src, seg, n)
kernel_name = 'mk_hybrid_d1_jaxref_r8_67a14b'

def setup_inputs(seed: int=0):
    np.random.seed(seed)
    _w = jnp.asarray

    def _L0_attn_a_setup():
        import jax, jax.numpy as jnp
        import numpy as np
        D_MODEL = 128
        D_STATE = 128
        HEAD_DIM = 64
        EXPAND = 2
        K = 4
        N_GROUPS = 1
        D_INNER = EXPAND * D_MODEL
        N_HEADS = D_INNER // HEAD_DIM
        D_PROJ = 2 * D_INNER + 2 * N_GROUPS * D_STATE + N_HEADS
        EPS = 1e-06

        def _rmsnorm(x, w):
            return x * jax.lax.rsqrt(jnp.mean(x * x, axis=-1, keepdims=True) + EPS) * w
        key = jax.random.key(seed)
        ks = jax.random.split(key, 8)
        B, L = (2, 256)
        x = jax.random.normal(ks[0], (B, L, D_MODEL), jnp.float32)
        norm_w = jnp.ones((D_MODEL,), jnp.float32)
        in_proj_w = jax.random.normal(ks[1], (D_PROJ, D_MODEL), jnp.float32) / np.sqrt(D_MODEL).astype(np.float32)
        conv_w = jax.random.normal(ks[2], (D_INNER, K), jnp.float32) / np.sqrt(K).astype(np.float32)
        conv_b = jnp.zeros((D_INNER,), jnp.float32)
        A_log = jnp.log(jax.random.uniform(ks[3], (N_HEADS,), jnp.float32) * 15.0 + 1.0)
        D = jnp.ones((N_HEADS,), jnp.float32)
        dt_bias = jnp.log(jax.random.uniform(ks[4], (N_HEADS,), jnp.float32) * 0.099 + 0.001)
        out_proj_w = jax.random.normal(ks[5], (D_MODEL, D_INNER), jnp.float32) / np.sqrt(D_INNER).astype(np.float32)
        return dict(x=x, norm_w=norm_w, in_proj_w=in_proj_w, conv_w=conv_w, conv_b=conv_b, A_log=A_log, D=D, dt_bias=dt_bias, out_proj_w=out_proj_w)
    _L0_attn_a_in = _L0_attn_a_setup()

    def _L0_attn_b_setup():
        import jax, jax.numpy as jnp
        import numpy as np
        EPS = 1e-08

        def elu_feature_map(x):
            return jax.nn.elu(x) + 1.0
        key = jax.random.key(seed)
        ks = jax.random.split(key, 5)
        B, S, D = (2, 512, 128)
        scale = 1.0 / np.sqrt(D).astype(np.float32)
        x = jax.random.normal(ks[0], (B, S, D), dtype=jnp.float32)
        Wq = jax.random.normal(ks[1], (D, D), dtype=jnp.float32) * scale
        Wk = jax.random.normal(ks[2], (D, D), dtype=jnp.float32) * scale
        Wv = jax.random.normal(ks[3], (D, D), dtype=jnp.float32) * scale
        Wo = jax.random.normal(ks[4], (D, D), dtype=jnp.float32) * scale
        return {'x': x, 'Wq': Wq, 'Wk': Wk, 'Wv': Wv, 'Wo': Wo}
    _L0_attn_b_in = _L0_attn_b_setup()

    def _L0_ffn_setup():
        import jax, jax.numpy as jnp
        import numpy as np
        B, N, D = (4, 512, 128)
        E, S, F = (16, 64, 256)
        DO = 128
        EPS = 1e-05

        def _layernorm(x, g, b):
            mu = jnp.mean(x, axis=-1, keepdims=True)
            var = jnp.mean(jnp.square(x - mu), axis=-1, keepdims=True)
            return (x - mu) * jax.lax.rsqrt(var + EPS) * g + b
        key = jax.random.key(seed)
        ks = jax.random.split(key, 8)
        d = {'x': jax.random.normal(ks[0], (B, N, D), dtype=jnp.float32), 'norm_g': jnp.ones((D,), jnp.float32), 'norm_b': jnp.zeros((D,), jnp.float32), 'slot_g': jnp.ones((D,), jnp.float32), 'slot_b': jnp.zeros((D,), jnp.float32), 'scale': jnp.ones((1,), jnp.float32), 'slot_embeds': jax.random.normal(ks[1], (E, S, D), jnp.float32) / np.sqrt(D), 'Wg': jax.random.normal(ks[2], (E, D, F), jnp.float32) * np.sqrt(2.0 / (D + F)), 'bg': jnp.zeros((E, F), jnp.float32), 'Wu': jax.random.normal(ks[3], (E, D, F), jnp.float32) * np.sqrt(2.0 / (D + F)), 'bu': jnp.zeros((E, F), jnp.float32), 'Wd': jax.random.normal(ks[4], (E, F, DO), jnp.float32) * np.sqrt(2.0 / (F + DO)), 'bd': jnp.zeros((E, DO), jnp.float32)}
        return d
    _L0_ffn_in = _L0_ffn_setup()
    _d = {'L0_attn_a_x': _L0_attn_a_in['x'], 'L0_attn_a_norm_w': _L0_attn_a_in['norm_w'], 'L0_attn_a_in_proj_w': _L0_attn_a_in['in_proj_w'], 'L0_attn_a_conv_w': _L0_attn_a_in['conv_w'], 'L0_attn_a_conv_b': _L0_attn_a_in['conv_b'], 'L0_attn_a_A_log': _L0_attn_a_in['A_log'], 'L0_attn_a_D': _L0_attn_a_in['D'], 'L0_attn_a_dt_bias': _L0_attn_a_in['dt_bias'], 'L0_attn_a_out_proj_w': _L0_attn_a_in['out_proj_w'], 'L0_attn_b_Wq': _L0_attn_b_in['Wq'], 'L0_attn_b_Wk': _L0_attn_b_in['Wk'], 'L0_attn_b_Wv': _L0_attn_b_in['Wv'], 'L0_attn_b_Wo': _L0_attn_b_in['Wo'], 'L0_ffn_norm_g': _L0_ffn_in['norm_g'], 'L0_ffn_norm_b': _L0_ffn_in['norm_b'], 'L0_ffn_slot_g': _L0_ffn_in['slot_g'], 'L0_ffn_slot_b': _L0_ffn_in['slot_b'], 'L0_ffn_scale': _L0_ffn_in['scale'], 'L0_ffn_slot_embeds': _L0_ffn_in['slot_embeds'], 'L0_ffn_Wg': _L0_ffn_in['Wg'], 'L0_ffn_bg': _L0_ffn_in['bg'], 'L0_ffn_Wu': _L0_ffn_in['Wu'], 'L0_ffn_bu': _L0_ffn_in['bu'], 'L0_ffn_Wd': _L0_ffn_in['Wd'], 'L0_ffn_bd': _L0_ffn_in['bd']}
    _x0 = _d['L0_attn_a_x']
    _d['L0_attn_a_x'] = jax.random.normal(jax.random.fold_in(jax.random.key(seed), 1), (2, 2048, 128), dtype=_x0.dtype)
    del _x0
    return _d

def reference(L0_attn_a_x, L0_attn_a_norm_w, L0_attn_a_in_proj_w, L0_attn_a_conv_w, L0_attn_a_conv_b, L0_attn_a_A_log, L0_attn_a_D, L0_attn_a_dt_bias, L0_attn_a_out_proj_w, L0_attn_b_Wq, L0_attn_b_Wk, L0_attn_b_Wv, L0_attn_b_Wo, L0_ffn_norm_g, L0_ffn_norm_b, L0_ffn_slot_g, L0_ffn_slot_b, L0_ffn_scale, L0_ffn_slot_embeds, L0_ffn_Wg, L0_ffn_bg, L0_ffn_Wu, L0_ffn_bu, L0_ffn_Wd, L0_ffn_bd):

    def _L0_attn_a_ref(x, norm_w, in_proj_w, conv_w, conv_b, A_log, D, dt_bias, out_proj_w):
        import jax, jax.numpy as jnp
        import numpy as np
        D_MODEL = 128
        D_STATE = 128
        HEAD_DIM = 64
        EXPAND = 2
        K = 4
        N_GROUPS = 1
        D_INNER = EXPAND * D_MODEL
        N_HEADS = D_INNER // HEAD_DIM
        D_PROJ = 2 * D_INNER + 2 * N_GROUPS * D_STATE + N_HEADS
        EPS = 1e-06

        def _rmsnorm(x, w):
            return x * jax.lax.rsqrt(jnp.mean(x * x, axis=-1, keepdims=True) + EPS) * w
        batch, L, _ = x.shape
        residual = x
        xn = _rmsnorm(x, norm_w)
        proj = jnp.einsum('bld,pd->blp', xn, in_proj_w)
        i = 0
        z = proj[:, :, i:i + D_INNER]
        i += D_INNER
        x_ssm = proj[:, :, i:i + D_INNER]
        i += D_INNER
        bc = N_GROUPS * D_STATE
        Bm = proj[:, :, i:i + bc].reshape(batch, L, N_GROUPS, D_STATE)
        i += bc
        Cm = proj[:, :, i:i + bc].reshape(batch, L, N_GROUPS, D_STATE)
        i += bc
        dt_raw = proj[:, :, i:i + N_HEADS]
        xp = jnp.pad(x_ssm, ((0, 0), (K - 1, 0), (0, 0)))
        x_conv = conv_b
        for k in range(K):
            x_conv = x_conv + xp[:, k:k + L, :] * conv_w[:, k]
        x_conv = jax.nn.silu(x_conv)
        xh = x_conv.reshape(batch, L, N_HEADS, HEAD_DIM)
        dt = jax.nn.softplus(dt_raw + dt_bias)
        dA = jnp.exp(-jnp.exp(A_log) * dt)
        dtx = dt[..., None] * xh
        gidx = jnp.arange(N_HEADS) // (N_HEADS // N_GROUPS)
        Bg = Bm[:, :, gidx, :]
        Cg = Cm[:, :, gidx, :]

        def step(h, inp):
            dA_t, dtx_t, B_t, C_t = inp
            h = h * dA_t[:, :, None, None] + dtx_t[..., None] * B_t[:, :, None, :]
            y_t = jnp.einsum('bhpn,bhn->bhp', h, C_t)
            return (h, y_t)
        h0 = jnp.zeros((batch, N_HEADS, HEAD_DIM, D_STATE), jnp.float32)
        xs = (jnp.swapaxes(dA, 0, 1), jnp.swapaxes(dtx, 0, 1), jnp.swapaxes(Bg, 0, 1), jnp.swapaxes(Cg, 0, 1))
        _, ys = jax.lax.scan(step, h0, xs)
        y = jnp.swapaxes(ys, 0, 1) + D[None, None, :, None] * xh
        y = y.reshape(batch, L, D_INNER) * jax.nn.silu(z)
        return residual + jnp.einsum('bli,di->bld', y, out_proj_w)

    def _L0_attn_b_ref(x, Wq, Wk, Wv, Wo):
        import jax, jax.numpy as jnp
        import numpy as np
        EPS = 1e-08

        def elu_feature_map(x):
            return jax.nn.elu(x) + 1.0
        B, S, D = x.shape
        H = 16
        Dh = D // H

        def proj(W):
            return (x @ W.T).reshape(B, S, H, Dh)
        q = elu_feature_map(proj(Wq))
        k = elu_feature_map(proj(Wk))
        v = proj(Wv)
        q_t = jnp.moveaxis(q, 1, 0)
        k_t = jnp.moveaxis(k, 1, 0)
        v_t = jnp.moveaxis(v, 1, 0)

        def step(carry, qkv):
            kv_sum, k_sum = carry
            q_i, k_i, v_i = qkv
            kv_sum = kv_sum + jnp.einsum('bhd,bhe->bhde', k_i, v_i)
            k_sum = k_sum + k_i
            num = jnp.einsum('bhd,bhde->bhe', q_i, kv_sum)
            den = jnp.sum(q_i * k_sum, axis=-1, keepdims=True)
            out_i = num / (den + EPS)
            return ((kv_sum, k_sum), out_i)
        kv0 = jnp.zeros((B, H, Dh, Dh), dtype=x.dtype)
        ks0 = jnp.zeros((B, H, Dh), dtype=x.dtype)
        _, out = jax.lax.scan(step, (kv0, ks0), (q_t, k_t, v_t))
        out = jnp.moveaxis(out, 0, 1).reshape(B, S, D)
        return out @ Wo.T

    def _L0_ffn_ref(x, norm_g, norm_b, slot_g, slot_b, scale, slot_embeds, Wg, bg, Wu, bu, Wd, bd):
        import jax, jax.numpy as jnp
        import numpy as np
        B, N, D = (4, 512, 128)
        E, S, F = (16, 64, 256)
        DO = 128
        EPS = 1e-05

        def _layernorm(x, g, b):
            mu = jnp.mean(x, axis=-1, keepdims=True)
            var = jnp.mean(jnp.square(x - mu), axis=-1, keepdims=True)
            return (x - mu) * jax.lax.rsqrt(var + EPS) * g + b
        x = _layernorm(x, norm_g, norm_b)
        se = _layernorm(slot_embeds, slot_g, slot_b) * scale
        logits = jnp.einsum('bnd,esd->bnes', x, se)
        dispatch = jax.nn.softmax(logits, axis=1)
        combine = jax.nn.softmax(logits.reshape(x.shape[0], x.shape[1], -1), axis=-1)
        slots = jnp.einsum('bnd,bnes->besd', x, dispatch)
        gate = jax.nn.gelu(jnp.einsum('besd,edf->besf', slots, Wg) + bg[None, :, None, :], approximate=False)
        up = jnp.einsum('besd,edf->besf', slots, Wu) + bu[None, :, None, :]
        eout = jnp.einsum('besf,efo->beso', gate * up, Wd) + bd[None, :, None, :]
        eout = eout.reshape(eout.shape[0], -1, eout.shape[-1])
        return jnp.einsum('bns,bso->bno', combine, eout)
    x = L0_attn_a_x
    x = x + _L0_attn_a_ref(_layernorm(x, axis=-1), L0_attn_a_norm_w, L0_attn_a_in_proj_w, L0_attn_a_conv_w, L0_attn_a_conv_b, L0_attn_a_A_log, L0_attn_a_D, L0_attn_a_dt_bias, L0_attn_a_out_proj_w)
    x = x + _L0_ffn_ref(_layernorm(x, axis=-1), L0_ffn_norm_g, L0_ffn_norm_b, L0_ffn_slot_g, L0_ffn_slot_b, L0_ffn_scale, L0_ffn_slot_embeds, L0_ffn_Wg, L0_ffn_bg, L0_ffn_Wu, L0_ffn_bu, L0_ffn_Wd, L0_ffn_bd)
    x = x + _L0_attn_b_ref(_layernorm(x, axis=-1), L0_attn_b_Wq, L0_attn_b_Wk, L0_attn_b_Wv, L0_attn_b_Wo)
    x = x + _L0_ffn_ref(_layernorm(x, axis=-1), L0_ffn_norm_g, L0_ffn_norm_b, L0_ffn_slot_g, L0_ffn_slot_b, L0_ffn_scale, L0_ffn_slot_embeds, L0_ffn_Wg, L0_ffn_bg, L0_ffn_Wu, L0_ffn_bu, L0_ffn_Wd, L0_ffn_bd)
    return x

_drawn_inputs = setup_inputs


def setup_inputs(seed=0):
    import zlib

    import numpy as np

    out = dict(_drawn_inputs(seed))
    spreads = {'L0_attn_a_norm_w': (1.0, 0.2),
     'L0_attn_a_conv_b': (0.0, 0.1),
     'L0_attn_a_D': (1.0, 0.6),
     'L0_ffn_norm_g': (1.0, 0.2),
     'L0_ffn_norm_b': (0.0, 0.1),
     'L0_ffn_slot_g': (1.0, 0.2),
     'L0_ffn_slot_b': (0.0, 0.1),
     'L0_ffn_bg': (0.0, 0.1),
     'L0_ffn_bu': (0.0, 0.1),
     'L0_ffn_bd': (0.0, 0.1)}
    factors = {'L0_attn_b_Wq': 6.767, 'L0_attn_b_Wk': 3.672}
    for name, (base, spread) in spreads.items():
        noise = np.random.default_rng([zlib.crc32(name.encode()), seed]).standard_normal(out[name].shape)
        drawn = base * np.exp(spread * noise) if base else spread * noise
        out[name] = jnp.asarray(drawn.astype(out[name].dtype))
    for name, factor in factors.items():
        out[name] = (out[name] * factor).astype(out[name].dtype)
    return out
```

```python
import concourse.bass as bass
from concourse import mybir
from contextlib import ExitStack

F32 = mybir.dt.float32
F16 = mybir.dt.float16
ACT = mybir.ActivationFunctionType
ALU = mybir.AluOpType
AX = mybir.AxisListType

P = 128
BATCH, SEQ, DM = 2, 2048, 128
TILES = SEQ // P
NT = BATCH * TILES
LN_EPS, RMS_EPS, ATT_EPS = 1e-5, 1e-6, 1e-8
CH = 256
NH, HD = 4, 64
TAPS = 4
PROJ = 2 * CH + 2 * P
NE, SLOTS, FF = 16, 64, 256
NS = NE * SLOTS
SB = NS // P
AH, AD = 16, 8
AE = AD + 1


def wait(eng, sem, value):
    if isinstance(value, int) and value <= 0:
        return
    eng.wait_ge(sem, value)


def chain(eng, sem, ins, value):
    ins.then_inc(sem, 1)
    eng.wait_ge(sem, value)


class Core:
    pass


def prepare(nc, c):
    with ExitStack() as ctx:
        def sb(name, shape, dt=F32):
            return ctx.enter_context(nc.sbuf_tensor(name, shape, dt))

        def sem(name):
            return nc.alloc_semaphore(name)

        wp_nat = sb("wp_nat", [P, PROJ // P, DM])
        wdt_nat = sb("wdt_nat", [NH, DM])
        wout_nat = sb("wout_nat", [DM, CH])
        wa_nat = sb("wa_nat", [P, 4, DM])
        se_nat = sb("se_nat", [P, SB, DM])
        b_nat = sb("b_nat", [NE, 2, FF])
        se_st = sb("se_st", [P, SB, 6])
        cols = sb("cols", [P, 8])
        se32 = sb("se32", [P, NS])
        dskip = sb("dskip", [P, 2])
        tb = [ctx.enter_context(nc.psum_tensor(f"prep_ps{i}", [P, 512], F32)) for i in range(8)]

        x_in = sem("x_in")
        w_in = sem("w_in")
        cols_in = sem("cols_in")
        se_in = sem("se_in")
        masks_zero = sem("masks_zero")
        masks_ready = sem("masks_ready")
        se_dve = sem("se_dve")
        se_pow = sem("se_pow")
        se_var = sem("se_var")
        se_scaled = sem("se_scaled")
        tr_done = sem("tr_done")
        ev_act = sem("ev_act")
        ev_dve = sem("ev_dve")
        se_hi = sem("se_hi")

        jobs = []
        for k in range(PROJ // P):
            jobs.append((wp_nat[:, k, :], P, c.wpT[:, k * P:(k + 1) * P], "norm"))
        jobs.append((wdt_nat[:, :], NH, c.wpT[:, PROJ:PROJ + NH], "norm"))
        for k in range(2):
            jobs.append((wout_nat[:, k * P:(k + 1) * P], P, c.woutT[:, k, :], "half"))
        for k in range(3):
            jobs.append((wa_nat[:, k, :], P, c.wqkvT[:, k * P:(k + 1) * P], "copy"))
        jobs.append((wa_nat[:, 3, :], P, c.waoT[:, :], "copy"))
        for which, dst in ((0, c.bgT), (1, c.buT)):
            for k in range(2):
                jobs.append((b_nat[:, which, k * P:(k + 1) * P], NE, dst[:, k, :], "copy"))
        for j in range(SB):
            jobs.append((se_nat[:, j, :], P, se32[:, j * P:(j + 1) * P], "slot"))
        first_se = len(jobs) - SB
        by_act = [n % 2 == 1 and job[3] != "slot" for n, job in enumerate(jobs)]

        block = ctx.enter_context(nc.Block())

        @block.sync
        def _(sp):
            for b in range(BATCH):
                sp.dma_start(c.x[:, b, :, :], c.x_dram[b].rearrange("(t p) d -> p t d", p=P)).then_inc(x_in, 16)
            sp.dma_start(wp_nat[:, :, :], c.in_proj_w[0:PROJ, :].rearrange("(k p) d -> p k d", p=P)).then_inc(w_in, 16)
            sp.dma_start(wdt_nat[:, :], c.in_proj_w[PROJ:PROJ + NH, :]).then_inc(w_in, 16)
            sp.dma_start(wout_nat[:, :], c.out_proj_w).then_inc(w_in, 16)
            for k, w in enumerate((c.Wq, c.Wk, c.Wv, c.Wo)):
                sp.dma_start(wa_nat[:, k, :], w).then_inc(w_in, 16)
            sp.dma_start(b_nat[:, 0, :], c.bg).then_inc(w_in, 16)
            sp.dma_start(b_nat[:, 1, :], c.bu).then_inc(w_in, 16)
            for e2 in range(2):
                src = c.bd.rearrange("(j e) o -> e j o", e=2)[e2:e2 + 1, :, :]
                sp.dma_start(c.bdb[e2 * SLOTS:(e2 + 1) * SLOTS, :, :],
                             src.broadcast_to([SLOTS, SB, DM])).then_inc(w_in, 16)
            sp.wait_ge(x_in, 16 * BATCH)

        @block.scalar
        def _(act):
            act.dma_start(se_nat[:, :, :], c.slot_embeds.rearrange("e s d -> (e s) d")
                          .rearrange("(j p) d -> p j d", p=P)).then_inc(se_in, 16)
            for k, v in enumerate((c.norm_w, c.slot_g, c.slot_b)):
                act.dma_start(cols[:, k:k + 1], v.rearrange("(p a) -> p a", a=1)).then_inc(cols_in, 16)
            act.dma_start(cols[:, 3:4], c.scale.rearrange("(p a) -> p a", a=1).broadcast_to([P, 1])).then_inc(cols_in, 16)
            for dst, v in ((c.gcol, c.norm_g), (c.bcol, c.norm_b)):
                act.dma_start(dst[:, :], v.rearrange("(p a) -> p a", a=1)).then_inc(cols_in, 16)
            act.dma_start(c.convw[:, :, :], c.conv_w.rearrange("(k p) t -> p k t", p=P)).then_inc(cols_in, 16)
            act.dma_start(c.convb[:, :], c.conv_b.rearrange("(k p) -> p k", p=P),
                          allow_slow_non_contiguous=True).then_inc(cols_in, 16)
            act.dma_start(c.alog[:, :], c.A_log.rearrange("(a h) -> a h", a=1).broadcast_to([P, NH])).then_inc(cols_in, 16)
            act.dma_start(c.dtb[:, :], c.dt_bias.rearrange("(a h) -> a h", a=1).broadcast_to([P, NH])).then_inc(cols_in, 16)
            for h in range(2):
                src = c.D_skip.rearrange("(k h) -> h k", h=2)[h:h + 1, :]
                act.dma_start(dskip[h * HD:(h + 1) * HD, :], src.broadcast_to([HD, 2]),
                              allow_slow_non_contiguous=True).then_inc(cols_in, 16)
            for n, (src, rows, dst, how) in enumerate(jobs):
                if not by_act[n]:
                    continue
                act.wait_ge(tr_done, n + 1)
                if n == 1:
                    act.wait_ge(cols_in, 16 * 12)
                ps = tb[n % 8][:, 0:rows]
                if how == "norm":
                    nc.scalar.activation(dst, ps, ACT.Copy, scale=cols[:, 0:1]).then_inc(ev_act, 1)
                elif how == "half":
                    nc.scalar.activation(dst, ps, ACT.Copy, scale=0.5).then_inc(ev_act, 1)
                else:
                    nc.scalar.copy(dst, ps).then_inc(ev_act, 1)

        @block.gpsimd
        def _(pool):
            nc.gpsimd.memset(c.ident[:, :], 0.0).then_inc(masks_zero, 1)
            nc.gpsimd.memset(c.ones[:, :], 1.0).then_inc(masks_zero, 1)
            nc.gpsimd.memset(c.mhalf[:, :], -0.5).then_inc(masks_zero, 1)
            nc.gpsimd.memset(c.mask_blk[:, :, :], 1.0).then_inc(masks_zero, 1)
            pool.wait_ge(masks_zero, 4)
            nc.gpsimd.affine_select(out=c.ident[:, :], in_=c.ident[:, :], compare_op=ALU.not_equal, fill=1.0,
                                    base=0, pattern=[[-1, P]], channel_multiplier=1).then_inc(masks_ready, 1)
            nc.gpsimd.affine_select(out=c.upto[:, :], in_=c.ones[:, :], compare_op=ALU.is_ge, fill=0.0,
                                    base=0, pattern=[[1, P]], channel_multiplier=-1).then_inc(masks_ready, 1)
            nc.gpsimd.affine_select(out=c.after[:, :], in_=c.ones[:, :], compare_op=ALU.is_gt, fill=0.0,
                                    base=0, pattern=[[-1, P]], channel_multiplier=1).then_inc(masks_ready, 1)
            nc.gpsimd.affine_select(out=c.mask_blk[:, :, :], in_=c.mask_blk[:, :, :], compare_op=ALU.is_ge, fill=0.0,
                                    base=0, pattern=[[-AD, AH], [0, AE]], channel_multiplier=1).then_inc(masks_zero, 1)
            pool.wait_ge(masks_zero, 5)
            nc.gpsimd.affine_select(out=c.mask_blk[:, :, :], in_=c.mask_blk[:, :, :], compare_op=ALU.is_ge, fill=0.0,
                                    base=AD - 1, pattern=[[AD, AH], [0, AE]], channel_multiplier=-1).then_inc(masks_ready, 1)
            pool.wait_ge(se_var, 1)
            nc.gpsimd.tensor_tensor(se_st[:, :, 3], se_st[:, :, 1], c.mhalf[:, 0:SB], ALU.pow).then_inc(se_pow, 1)

        @block.vector
        def _(dve):
            dve.wait_ge(se_in, 16)
            for j in range(SB):
                last = nc.vector.bn_stats(se_st[:, j, :], se_nat[:, j, :])
            chain(dve, se_dve, last, 1)
            n = stats_tail(nc, dve, se_st, se_dve, 1, LN_EPS)
            nc.vector.tensor_scalar(se_st[:, :, 1], se_st[:, :, 1], 1.0, None, ALU.mult).then_inc(se_var, 1)
            dve.wait_ge(se_pow, 1)
            for j in range(SB):
                nc.vector.tensor_scalar(se_nat[:, j, :], se_nat[:, j, :], se_st[:, j, 0:1], se_st[:, j, 3:4],
                                        ALU.subtract, ALU.mult).then_inc(se_scaled, 1)
            dve.wait_ge(cols_in, 16 * 12)
            nc.vector.tensor_scalar(cols[:, 4:6], cols[:, 1:3], cols[:, 3:4], None, ALU.mult).then_inc(se_dve, 1)
            dve.wait_ge(se_dve, n + 1)
            nc.vector.tensor_scalar(c.dcol[:, :], dskip[:, :], 0.5, None, ALU.mult)
            for m, (src, rows, dst, how) in enumerate(jobs):
                if by_act[m]:
                    continue
                dve.wait_ge(tr_done, m + 1)
                ps = tb[m % 8][:, 0:rows]
                if how == "slot":
                    nc.vector.tensor_scalar(dst, ps, cols[:, 4:5], cols[:, 5:6], ALU.mult, ALU.add).then_inc(ev_dve, 1)
                elif how == "norm":
                    nc.vector.tensor_scalar(dst, ps, cols[:, 0:1], None, ALU.mult).then_inc(ev_dve, 1)
                elif how == "half":
                    nc.vector.tensor_scalar(dst, ps, 0.5, None, ALU.mult).then_inc(ev_dve, 1)
                else:
                    nc.vector.tensor_copy(dst, ps).then_inc(ev_dve, 1)
            dve.wait_ge(ev_dve, len(jobs) - sum(by_act))
            nc.vector.tensor_copy(c.seh[:, :], se32[:, :]).then_inc(se_hi, 1)
            dve.wait_ge(se_hi, 1)
            nc.vector.tensor_tensor(c.sel[:, :], se32[:, :], c.seh[:, :], ALU.subtract).then_inc(se_hi, 1)

        @block.tensor
        def _(pe):
            pe.wait_ge(masks_ready, 1)
            pe.wait_ge(w_in, 16 * 11)
            for n, (src, rows, dst, how) in enumerate(jobs):
                if n >= 8:
                    m = n - 8
                    pe.wait_ge(ev_act if by_act[m] else ev_dve,
                               sum(a == by_act[m] for a in by_act[:m + 1]))
                if how == "slot":
                    pe.wait_ge(se_scaled, n - first_se + 1)
                nc.tensor.transpose(tb[n % 8][:, 0:rows], src, c.ident[0:rows, 0:rows]).then_inc(tr_done, 1)



def stats_tail(nc, dve, st, sem, n, eps):
    nc.vector.tensor_tensor(st[:, :, 0], st[:, :, 1], st[:, :, 4], ALU.add)
    chain(dve, sem, nc.vector.tensor_tensor(st[:, :, 3], st[:, :, 1], st[:, :, 4], ALU.subtract), n + 1)
    nc.vector.tensor_scalar(st[:, :, 0], st[:, :, 0], 0.5, None, ALU.mult)
    nc.vector.tensor_tensor(st[:, :, 4], st[:, :, 2], st[:, :, 5], ALU.add)
    chain(dve, sem, nc.vector.tensor_tensor(st[:, :, 3], st[:, :, 3], st[:, :, 3], ALU.mult), n + 2)
    nc.vector.tensor_scalar(st[:, :, 4], st[:, :, 4], 1.0 / DM, None, ALU.mult)
    chain(dve, sem, nc.vector.tensor_scalar(st[:, :, 3], st[:, :, 3], 0.25, None, ALU.mult), n + 3)
    chain(dve, sem, nc.vector.tensor_tensor(st[:, :, 4], st[:, :, 4], st[:, :, 3], ALU.add), n + 4)
    chain(dve, sem, nc.vector.tensor_scalar(st[:, :, 1], st[:, :, 4], eps, None, ALU.add), n + 5)
    return n + 5


def row_stats(nc, c, name, second_eps):
    with ExitStack() as ctx:
        st = ctx.enter_context(nc.sbuf_tensor(f"{name}_st", [P, NT, 6], F32))
        stats_done = nc.alloc_semaphore(f"{name}_stats_done")
        dve_step = nc.alloc_semaphore(f"{name}_dve_step")
        var_ready = nc.alloc_semaphore(f"{name}_var_ready")
        pow_ready = nc.alloc_semaphore(f"{name}_pow_ready")
        xf = c.x[:, :, :, :].rearrange("p b t d -> p (b t) d")
        block = ctx.enter_context(nc.Block(no_gpsimd_drain=True))

        @block.vector
        def _(dve):
            with dve.Fori(0, NT // 4) as r:
                t = 4 * r
                for q in range(4):
                    last = nc.vector.bn_stats(st[:, bass.ds(t + q, 1), :], xf[:, bass.ds(t + q, 1), :])
                last.then_inc(stats_done, 1)
            dve.wait_ge(stats_done, NT // 4)
            n = stats_tail(nc, dve, st, dve_step, 0, LN_EPS)
            nc.vector.tensor_copy(c.mean[:, :], st[:, :, 0]).then_inc(dve_step, 1)
            nc.vector.tensor_copy(c.var[:, :], st[:, :, 1]).then_inc(var_ready, 1)
            if second_eps is not None:
                dve.wait_ge(pow_ready, 1)
                chain(dve, dve_step, nc.vector.tensor_tensor(st[:, :, 2], c.r1[:, :], c.r1[:, :], ALU.mult), n + 2)
                chain(dve, dve_step, nc.vector.tensor_tensor(st[:, :, 3], st[:, :, 2], st[:, :, 4], ALU.mult), n + 3)
                nc.vector.tensor_scalar(c.var[:, :], st[:, :, 3], second_eps, None, ALU.add).then_inc(var_ready, 1)
                dve.wait_ge(pow_ready, 2)
                nc.vector.tensor_tensor(c.s[:, :], c.r1[:, :], c.r2[:, :], ALU.mult)

        @block.gpsimd
        def _(pool):
            pool.wait_ge(var_ready, 1)
            nc.gpsimd.tensor_tensor(c.r1[:, :], c.var[:, :], c.mhalf[:, :], ALU.pow).then_inc(pow_ready, 1)
            if second_eps is not None:
                pool.wait_ge(var_ready, 2)
                nc.gpsimd.tensor_tensor(c.r2[:, :], c.var[:, :], c.mhalf[:, :], ALU.pow).then_inc(pow_ready, 1)


def moe_normalise(nc, c, name, xh, xT):
    with ExitStack() as ctx:
        def sem(what):
            return nc.alloc_semaphore(f"{name}_{what}")

        G = 4
        xn = ctx.enter_context(nc.sbuf_tensor(f"{name}_xn", [P, 2, G, DM], F32))
        xa = ctx.enter_context(nc.sbuf_tensor(f"{name}_xa", [P, 2, G * P], F32))
        ps = [ctx.enter_context(nc.psum_tensor(f"{name}_nps{i}", [P, G * P], F32)) for i in range(2)]
        xn_ready, xn_hi, xn_split = sem("xn_ready"), sem("xn_hi"), sem("xn_split")
        transposed, affine, xa_hi, xa_split = sem("transposed"), sem("affine"), sem("xa_hi"), sem("xa_split")
        xf = c.x[:, :, :, :].rearrange("p b t d -> p (b t) d")
        block = ctx.enter_context(nc.Block(no_gpsimd_drain=True))
        NG = NT // G

        @block.vector
        def _(dve):
            def normalise(g, pp):
                wait(dve, transposed, g - 1)
                wait(dve, xn_split, g - 1)
                for q in range(G):
                    t = bass.ds(g * G + q, 1)
                    last = nc.vector.tensor_scalar(xn[:, pp, q, :], xf[:, t, :], c.mean[:, t], c.s[:, t],
                                                   ALU.subtract, ALU.mult)
                last.then_inc(xn_ready, 1)

            def split(g, pp):
                dve.wait_ge(affine, g + 1)
                cols = bass.ds(g * (G * P), G * P)
                nc.vector.tensor_copy(xT[:, 0, cols], xa[:, pp, :]).then_inc(xa_hi, 1)
                dve.wait_ge(xa_hi, g + 1)
                nc.vector.tensor_tensor(xT[:, 1, cols], xa[:, pp, :], xT[:, 0, cols], ALU.subtract).then_inc(xa_split, 1)

            normalise(0, 0)
            normalise(1, 1)
            split(0, 0)
            with dve.Fori(0, NG // 2 - 1) as r:
                g = 2 * r + 1
                for q in range(2):
                    normalise(g + q + 1, q % 2)
                    split(g + q, (q + 1) % 2)
            split(NG - 1, 1)

        @block.gpsimd
        def _(pool):
            def split(g, pp):
                pool.wait_ge(xn_ready, g + 1)
                t = bass.ds(g * G, G)
                nc.gpsimd.tensor_copy(xh[:, t, 0, :], xn[:, pp, :, :]).then_inc(xn_hi, 1)
                pool.wait_ge(xn_hi, g + 1)
                nc.gpsimd.tensor_tensor(xh[:, t, 1, :], xn[:, pp, :, :], xh[:, t, 0, :], ALU.subtract)\
                    .then_inc(xn_split, 1)

            with pool.Fori(0, NG // 2) as r:
                g = 2 * r
                for q in range(2):
                    split(g + q, q)
            pool.wait_ge(xn_split, NG)

        @block.tensor
        def _(pe):
            def transpose(g, pp):
                pe.wait_ge(xn_ready, g + 1)
                wait(pe, affine, g - 1)
                for q in range(G):
                    last = nc.tensor.transpose(ps[pp][:, q * P:(q + 1) * P], xn[:, pp, q, :], c.ident[:, :])
                last.then_inc(transposed, 1)

            transpose(0, 0)
            transpose(1, 1)
            with pe.Fori(1, NG // 2) as r:
                g = 2 * r
                for q in range(2):
                    transpose(g + q, q)

        @block.scalar
        def _(act):
            def apply(g, pp):
                act.wait_ge(transposed, g + 1)
                wait(act, xa_split, g - 1)
                nc.scalar.activation(xa[:, pp, :], ps[pp][:, :], ACT.Identity, scale=c.gcol[:, 0:1],
                                     bias=c.bcol[:, 0:1]).then_inc(affine, 1)

            apply(0, 0)
            apply(1, 1)
            with act.Fori(1, NG // 2) as r:
                g = 2 * r
                for q in range(2):
                    apply(g + q, q)


def moe_dispatch(nc, c, name, xh, xT, sT):
    with ExitStack() as ctx:
        def sem(what):
            return nc.alloc_semaphore(f"{name}_{what}")

        NK = SEQ // 512
        RING = 4
        e32 = ctx.enter_context(nc.sbuf_tensor(f"{name}_e32", [P, 2, SEQ], F32))
        eh = ctx.enter_context(nc.sbuf_tensor(f"{name}_eh", [P, RING, 4, P], F16))
        el = ctx.enter_context(nc.sbuf_tensor(f"{name}_el", [P, RING, 4, P], F16))
        mx = ctx.enter_context(nc.sbuf_tensor(f"{name}_mx", [P, 2, NK], F32))
        nmx = ctx.enter_context(nc.sbuf_tensor(f"{name}_nmx", [P, 2], F32))
        sums = ctx.enter_context(nc.sbuf_tensor(f"{name}_sums", [P, 2, NK], F32))
        rs = ctx.enter_context(nc.sbuf_tensor(f"{name}_rs", [P, 2, 2], F32))
        part = ctx.enter_context(nc.sbuf_tensor(f"{name}_part", [P, P], F32))
        slots = ctx.enter_context(nc.sbuf_tensor(f"{name}_slots", [P, 2, P], F32))
        LB = [ctx.enter_context(nc.psum_tensor(f"{name}_L{i}", [P, 512], F32)) for i in range(NK)]
        TB = [ctx.enter_context(nc.psum_tensor(f"{name}_T{i}", [P, 4, P], F32)) for i in range(2)]
        SL = [ctx.enter_context(nc.psum_tensor(f"{name}_S{i}", [P, 512], F32)) for i in range(2)]
        logits, maxed, max_parts, exped = sem("logits"), sem("maxed"), sem("max_parts"), sem("exped")
        transposed, hi_ready, lo_ready, summed = sem("transposed"), sem("hi_ready"), sem("lo_ready"), sem("summed")
        total_ready, inverse_ready, part_ready = sem("total_ready"), sem("inverse_ready"), sem("part_ready")
        slots_ready = sem("slots_ready")
        slots_transposed, slots_out = sem("slots_transposed"), sem("slots_out")
        block = ctx.enter_context(nc.Block(no_gpsimd_drain=True))
        STEPS = 2 * SB

        def step(r, q):
            return 2 * r + q, r + q // 2, q % 2

        @block.tensor
        def _(pe):
            def logit(r, q):
                i, j, b = step(r, q)
                jj = bass.ds(j * P, P)
                for k in range(NK):
                    wait(pe, exped, 4 * i - 3 + k)
                    cols = slice(b * SEQ + k * 512, b * SEQ + (k + 1) * 512)
                    nc.tensor.matmul(LB[k][:, :], c.seh[:, jj], xT[:, 0, cols], start=True, stop=False)
                    nc.tensor.matmul(LB[k][:, :], c.seh[:, jj], xT[:, 1, cols], start=False, stop=False)
                    nc.tensor.matmul(LB[k][:, :], c.sel[:, jj], xT[:, 0, cols], start=False, stop=True)\
                        .then_inc(logits, 1)

            def transpose(r, q, g):
                i, j, b = step(r, q)
                pe.wait_ge(exped, 4 * i + g + 1)
                wait(pe, lo_ready, 4 * i + g - 1)
                for k in range(4):
                    col = (4 * g + k) * P
                    last = nc.tensor.transpose(TB[g % 2][:, k, :], e32[:, b, col:col + P], c.ident[:, :])
                last.then_inc(transposed, 1)

            def collect(r, q, g):
                i, j, b = step(r, q)
                pe.wait_ge(lo_ready, 4 * i + g + 1)
                if g == 0:
                    wait(pe, slots_out, i - 1)
                for k in range(4):
                    t = b * TILES + 4 * g + k
                    first, final = g == 0 and k == 0, g == NK - 1 and k == 3
                    nc.tensor.matmul(SL[b][:, 0:2 * P], eh[:, g, k, :],
                                     xh[:, t, :, :].rearrange("p h d -> p (h d)"),
                                     start=first, stop=False, skip_group_check=True)
                    last = nc.tensor.matmul(SL[b][:, 0:P], el[:, g, k, :], xh[:, t, 0, :],
                                            start=False, stop=final, skip_group_check=True)
                last.then_inc(summed, 1)

            def slot_transpose(r, q):
                i, j, b = step(r, q)
                pe.wait_ge(slots_ready, i + 1)
                nc.tensor.transpose(SL[b][:, 2 * P:3 * P], slots[:, b, :], c.ident[:, :]).then_inc(slots_transposed, 1)

            def body(r, q, first=False, final=False):
                if not final:
                    logit(r, q + 1)
                transpose(r, q, 0)
                transpose(r, q, 1)
                if not first:
                    collect(r, q - 1, 2)
                    collect(r, q - 1, 3)
                transpose(r, q, 2)
                collect(r, q, 0)
                if not first:
                    slot_transpose(r, q - 1)
                transpose(r, q, 3)
                collect(r, q, 1)

            logit(0, 0)
            body(0, 0, first=True)
            body(0, 1)
            body(0, 2)
            with pe.Fori(1, SB - 1) as r:
                body(r, 1)
                body(r, 2)
            body(SB - 1, 1, final=True)
            collect(SB - 1, 1, 2)
            collect(SB - 1, 1, 3)
            slot_transpose(SB - 1, 1)

        @block.vector
        def _(dve):
            def peak(r, q):
                i, j, b = step(r, q)
                for k in range(NK):
                    dve.wait_ge(logits, 4 * i + k + 1)
                    last = nc.vector.tensor_reduce(mx[:, b, k:k + 1], LB[k][:, :], AX.X, ALU.max)
                chain(dve, max_parts, last, i + 1)
                nc.vector.tensor_reduce(nmx[:, b:b + 1], mx[:, b, :], AX.X, ALU.max, negate=True).then_inc(maxed, 1)

            def low(r, q, g):
                i, j, b = step(r, q)
                dve.wait_ge(hi_ready, 4 * i + g + 1)
                nc.vector.tensor_tensor(el[:, g, :, :], TB[g % 2][:, :, :], eh[:, g, :, :], ALU.subtract)\
                    .then_inc(lo_ready, 1)

            def inverse(r, q):
                i, j, b = step(r, q)
                dve.wait_ge(exped, 4 * i + 4)
                chain(dve, total_ready, nc.vector.tensor_reduce(rs[:, b, 0:1], sums[:, b, :], AX.X, ALU.add), i + 1)
                chain(dve, inverse_ready, nc.vector.reciprocal(rs[:, b, 1:2], rs[:, b, 0:1]), i + 1)

            def normalise(r, q):
                i, j, b = step(r, q)
                dve.wait_ge(summed, 4 * i + 4)
                chain(dve, part_ready, nc.vector.tensor_scalar(part[:, :], SL[b][:, P:2 * P], rs[:, b, 1:2], None,
                                                               ALU.mult), i + 1)
                nc.vector.scalar_tensor_tensor(out=slots[:, b, :], in0=SL[b][:, 0:P], scalar=rs[:, b, 1:2],
                                               in1=part[:, :], op0=ALU.mult, op1=ALU.add).then_inc(slots_ready, 1)

            def body(r, q, first=False, final=False):
                if not final:
                    peak(r, q + 1)
                inverse(r, q)
                low(r, q, 0)
                low(r, q, 1)
                if not first:
                    normalise(r, q - 1)
                low(r, q, 2)
                low(r, q, 3)

            peak(0, 0)
            body(0, 0, first=True)
            with dve.Fori(0, SB - 1) as r:
                body(r, 1)
                body(r, 2)
            body(SB - 1, 1, final=True)
            normalise(SB - 1, 1)

        @block.scalar
        def _(act):
            def exponential(r, q):
                i, j, b = step(r, q)
                act.wait_ge(maxed, i + 1)
                wait(act, transposed, 4 * i - 4)
                wait(act, total_ready, i - 1)
                for k in range(NK):
                    nc.scalar.activation(e32[:, b, k * 512:(k + 1) * 512], LB[k][:, :], ACT.Exp,
                                         bias=nmx[:, b:b + 1], accum_out=sums[:, b, k:k + 1]).then_inc(exped, 1)

            def high(r, q, g):
                i, j, b = step(r, q)
                act.wait_ge(transposed, 4 * i + g + 1)
                wait(act, summed, 4 * i + g - 3)
                nc.scalar.copy(eh[:, g, :, :], TB[g % 2][:, :, :]).then_inc(hi_ready, 1)

            def affine(r, q):
                i, j, b = step(r, q)
                act.wait_ge(slots_transposed, i + 1)
                nc.scalar.activation(sT[:, bass.ds(j, 1), b, :], SL[b][:, 2 * P:3 * P], ACT.Identity,
                                     scale=c.gcol[:, 0:1], bias=c.bcol[:, 0:1]).then_inc(slots_out, 1)

            def body(r, q, first=False, final=False):
                high(r, q, 0)
                high(r, q, 1)
                if not final:
                    exponential(r, q + 1)
                high(r, q, 2)
                if not first:
                    affine(r, q - 1)
                high(r, q, 3)

            exponential(0, 0)
            body(0, 0, first=True)
            body(0, 1)
            body(0, 2)
            with act.Fori(1, SB - 1) as r:
                body(r, 1)
                body(r, 2)
            body(SB - 1, 1, final=True)
            affine(SB - 1, 1)


def moe_experts(nc, c, name, sT, eo):
    with ExitStack() as ctx:
        def sem(what):
            return nc.alloc_semaphore(f"{name}_{what}")

        FB = FF // P
        wg = ctx.enter_context(nc.sbuf_tensor(f"{name}_wg", [P, 2, FF], F32))
        wu = ctx.enter_context(nc.sbuf_tensor(f"{name}_wu", [P, 2, FF], F32))
        wd = ctx.enter_context(nc.sbuf_tensor(f"{name}_wd", [P, 2, FB, DM], F32))
        gate = ctx.enter_context(nc.sbuf_tensor(f"{name}_gate", [P, 2, FB, P], F32))
        hid = ctx.enter_context(nc.sbuf_tensor(f"{name}_hid", [P, 2, FB, P], F32))
        o32 = ctx.enter_context(nc.sbuf_tensor(f"{name}_o32", [P, 2, BATCH, DM], F32))
        HB = [ctx.enter_context(nc.psum_tensor(f"{name}_H{i}", [P, 2, FB, P], F32)) for i in range(2)]
        OB = [ctx.enter_context(nc.psum_tensor(f"{name}_O{i}", [P, BATCH, DM], F32)) for i in range(2)]
        w_in = [sem("w_in0"), sem("w_in1")]
        up_done, gate_ready, hid_ready, down_done = sem("up_done"), sem("gate_ready"), sem("hid_ready"), sem("down_done")
        biased, out_hi, out_lo = sem("biased"), sem("out_hi"), sem("out_lo")
        block = ctx.enter_context(nc.Block(no_gpsimd_drain=True))

        @block.sync
        def _(sp):
            def load(j, e2):
                wait(sp, down_done, 2 * j + e2 - 1)
                e = bass.ds(2 * j + e2, 1)
                sp.dma_start(wg[:, e2, :], c.Wg[e, :, :].rearrange("a d f -> d (a f)")).then_inc(w_in[e2], 16)
                sp.dma_start(wu[:, e2, :], c.Wu[e, :, :].rearrange("a d f -> d (a f)")).then_inc(w_in[e2], 16)
                sp.dma_start(wd[:, e2, :, :], c.Wd[e, :, :].rearrange("a (k p) o -> p (a k) o", p=P))\
                    .then_inc(w_in[e2], 16)

            load(0, 0)
            load(0, 1)
            with sp.Fori(1, SB) as j:
                load(j, 0)
                load(j, 1)

        @block.tensor
        def _(pe):
            def up(j, e2):
                e = 2 * j + e2
                pe.wait_ge(w_in[e2], 48 * j + 48)
                wait(pe, hid_ready, e - 1)
                rows = sT[:, bass.ds(j, 1), :, e2 * SLOTS:(e2 + 1) * SLOTS]
                for which, w in enumerate((wg, wu)):
                    for k in range(FB):
                        last = nc.tensor.matmul(HB[e2][:, which, k, :], w[:, e2, k * P:(k + 1) * P], rows,
                                                start=True, stop=True)
                last.then_inc(up_done, 1)

            def down(j, e2, pj):
                e = 2 * j + e2
                pe.wait_ge(hid_ready, e + 1)
                if e2 == 0:
                    wait(pe, biased, j - 1)
                for b in range(BATCH):
                    for k in range(FB):
                        last = nc.tensor.matmul(OB[pj][e2 * SLOTS:(e2 + 1) * SLOTS, b, :],
                                                hid[:, e2, k, b * SLOTS:(b + 1) * SLOTS], wd[:, e2, k, :],
                                                start=(k == 0), stop=(k == FB - 1))
                last.then_inc(down_done, 1)

            def pair(j, pj, final=False):
                up(j, 1)
                down(j, 0, pj)
                if not final:
                    up(j + 1, 0)
                down(j, 1, pj)

            up(0, 0)
            pair(0, 0)
            pair(1, 1)
            pair(2, 0)
            with pe.Fori(1, SB // 2 - 1) as r:
                j = 2 * r + 1
                pair(j, 1)
                pair(j + 1, 0)
            pair(SB - 1, 1, final=True)

        @block.scalar
        def _(act):
            def expert(j, e2):
                e = 2 * j + e2
                act.wait_ge(up_done, e + 1)
                wait(act, hid_ready, e - 1)
                for k in range(FB):
                    last = nc.scalar.activation(gate[:, e2, k, :], HB[e2][:, 0, k, :], ACT.Gelu,
                                                bias=c.bgT[:, k, bass.ds(e, 1)])
                last.then_inc(gate_ready, 1)

            def split(j, pj):
                act.wait_ge(biased, j + 1)
                nc.scalar.copy(eo[:, :, bass.ds(j, 1), 0, :], o32[:, pj, :, :]).then_inc(out_hi, 1)

            expert(0, 0)
            expert(0, 1)
            with act.Fori(0, SB // 2 - 1) as r:
                j = 2 * r + 1
                for q in range(2):
                    expert(j + q, 0)
                    split(j + q - 1, q)
                    expert(j + q, 1)
            expert(SB - 1, 0)
            split(SB - 2, 0)
            expert(SB - 1, 1)
            split(SB - 1, 1)

        @block.vector
        def _(dve):
            def expert(j, e2):
                e = 2 * j + e2
                dve.wait_ge(gate_ready, e + 1)
                wait(dve, down_done, e - 1)
                for k in range(FB):
                    last = nc.vector.scalar_tensor_tensor(out=hid[:, e2, k, :], in0=HB[e2][:, 1, k, :],
                                                          scalar=c.buT[:, k, bass.ds(e, 1)], in1=gate[:, e2, k, :],
                                                          op0=ALU.add, op1=ALU.mult)
                last.then_inc(hid_ready, 1)

            def bias(j, pj):
                dve.wait_ge(down_done, 2 * j + 2)
                wait(dve, out_lo, j - 1)
                nc.vector.tensor_tensor(o32[:, pj, :, :], OB[pj][:, :, :],
                                        c.bdb[:, bass.ds(j, 1), :].broadcast_to([P, BATCH, DM]), ALU.add)\
                    .then_inc(biased, 1)

            def split(j, pj):
                dve.wait_ge(out_hi, j + 1)
                nc.vector.tensor_tensor(eo[:, :, bass.ds(j, 1), 1, :], o32[:, pj, :, :],
                                        eo[:, :, bass.ds(j, 1), 0, :], ALU.subtract).then_inc(out_lo, 1)

            def step(j, q):
                expert(j, 0)
                bias(j - 1, q)
                expert(j, 1)
                split(j - 1, q)

            expert(0, 0)
            expert(0, 1)
            for q in range(2):
                step(1 + q, q)
            with dve.Fori(1, SB // 2 - 1) as r:
                j = 2 * r + 1
                for q in range(2):
                    step(j + q, q)
            expert(SB - 1, 0)
            bias(SB - 2, 0)
            expert(SB - 1, 1)
            split(SB - 2, 0)
            bias(SB - 1, 1)
            split(SB - 1, 1)


def moe_combine(nc, c, name, xT, eo, store):
    with ExitStack() as ctx:
        def sem(what):
            return nc.alloc_semaphore(f"{name}_{what}")

        NK = NS // 512
        e32 = ctx.enter_context(nc.sbuf_tensor(f"{name}_e32", [P, 2, NS], F32))
        eh = ctx.enter_context(nc.sbuf_tensor(f"{name}_eh", [P, 2, SB, P], F16))
        el = ctx.enter_context(nc.sbuf_tensor(f"{name}_el", [P, 2, SB, P], F16))
        nmx = ctx.enter_context(nc.sbuf_tensor(f"{name}_nmx", [P, 2], F32))
        rs = ctx.enter_context(nc.sbuf_tensor(f"{name}_rs", [P, 2, 2], F32))
        part = ctx.enter_context(nc.sbuf_tensor(f"{name}_part", [P, P], F32))
        LB = [ctx.enter_context(nc.psum_tensor(f"{name}_L{i}", [P, NS], F32)) for i in range(2)]
        TB = [ctx.enter_context(nc.psum_tensor(f"{name}_T{i}", [P, 4, P], F32)) for i in range(2)]
        OB = [ctx.enter_context(nc.psum_tensor(f"{name}_O{i}", [P, 512], F32)) for i in range(2)]
        logits, maxed, exped, transposed = sem("logits"), sem("maxed"), sem("exped"), sem("transposed")
        hi_ready, lo_ready, summed = sem("hi_ready"), sem("lo_ready"), sem("summed")
        inverse_ready, part_ready, x_ready, stored = sem("inverse_ready"), sem("part_ready"), sem("x_ready"), sem("stored")
        block = ctx.enter_context(nc.Block())
        STEPS = 2 * TILES

        def step(r, q):
            return 2 * r + q, r + q // 2, q % 2

        @block.tensor
        def _(pe):
            def logit(r, q):
                i, t, b = step(r, q)
                wait(pe, exped, i - 1)
                tok = bass.ds(b * SEQ + t * P, P)
                for k in range(NK):
                    out, sl = LB[b][:, k * 512:(k + 1) * 512], slice(k * 512, (k + 1) * 512)
                    nc.tensor.matmul(out, xT[:, 0, tok], c.seh[:, sl], start=True, stop=False)
                    nc.tensor.matmul(out, xT[:, 0, tok], c.sel[:, sl], start=False, stop=False)
                    last = nc.tensor.matmul(out, xT[:, 1, tok], c.seh[:, sl], start=False, stop=True)
                last.then_inc(logits, 1)

            def transpose(r, q):
                i, t, b = step(r, q)
                pe.wait_ge(exped, i + 1)
                for g in range(2):
                    wait(pe, lo_ready, 2 * i + g - 1)
                    for k in range(4):
                        col = (4 * g + k) * P
                        last = nc.tensor.transpose(TB[g][:, k, :], e32[:, b, col:col + P], c.ident[:, :])
                    last.then_inc(transposed, 1)

            def collect(r, q):
                i, t, b = step(r, q)
                wait(pe, x_ready, i - 1)
                for k in range(SB):
                    if k % 4 == 0:
                        pe.wait_ge(lo_ready, 2 * i + k // 4 + 1)
                    nc.tensor.matmul(OB[b][:, 0:2 * P], eh[:, b, k, :], eo[:, b, k, :, :].rearrange("p h d -> p (h d)"),
                                     start=(k == 0), stop=False, skip_group_check=True)
                    last = nc.tensor.matmul(OB[b][:, 0:P], el[:, b, k, :], eo[:, b, k, 0, :],
                                            start=False, stop=(k == SB - 1), skip_group_check=True)
                last.then_inc(summed, 1)

            def body(r, q, first=False, final=False):
                if not final:
                    logit(r, q + 1)
                transpose(r, q)
                if not first:
                    collect(r, q - 1)

            logit(0, 0)
            body(0, 0, first=True)
            body(0, 1)
            body(0, 2)
            with pe.Fori(1, TILES - 1) as r:
                body(r, 1)
                body(r, 2)
            body(TILES - 1, 1, final=True)
            collect(TILES - 1, 1)

        @block.vector
        def _(dve):
            def peak(r, q):
                i, t, b = step(r, q)
                dve.wait_ge(logits, i + 1)
                nc.vector.tensor_reduce(nmx[:, b:b + 1], LB[b][:, :], AX.X, ALU.max, negate=True).then_inc(maxed, 1)

            def low(r, q, g):
                i, t, b = step(r, q)
                dve.wait_ge(hi_ready, 2 * i + g + 1)
                sl = slice(4 * g, 4 * g + 4)
                nc.vector.tensor_tensor(el[:, b, sl, :], TB[g][:, :, :], eh[:, b, sl, :], ALU.subtract)\
                    .then_inc(lo_ready, 1)

            def add(r, q):
                i, t, b = step(r, q)
                chain(dve, inverse_ready, nc.vector.reciprocal(rs[:, b, 1:2], rs[:, b, 0:1]), i + 1)
                dve.wait_ge(summed, i + 1)
                xt = c.x[:, b, bass.ds(t, 1), :]
                chain(dve, part_ready, nc.vector.scalar_tensor_tensor(
                    out=part[:, :], in0=OB[b][:, P:2 * P], scalar=rs[:, b, 1:2], in1=xt,
                    op0=ALU.mult, op1=ALU.add), i + 1)
                nc.vector.scalar_tensor_tensor(out=xt, in0=OB[b][:, 0:P], scalar=rs[:, b, 1:2], in1=part[:, :],
                                               op0=ALU.mult, op1=ALU.add).then_inc(x_ready, 1)

            def body(r, q, first=False, final=False):
                if not final:
                    peak(r, q + 1)
                low(r, q, 0)
                low(r, q, 1)
                if not first:
                    add(r, q - 1)

            peak(0, 0)
            body(0, 0, first=True)
            with dve.Fori(0, TILES - 1) as r:
                body(r, 1)
                body(r, 2)
            body(TILES - 1, 1, final=True)
            add(TILES - 1, 1)

        @block.scalar
        def _(act):
            def exponential(r, q):
                i, t, b = step(r, q)
                act.wait_ge(maxed, i + 1)
                wait(act, transposed, 2 * i - 2)
                wait(act, inverse_ready, i - 1)
                nc.scalar.activation(e32[:, b, :], LB[b][:, :], ACT.Exp, bias=nmx[:, b:b + 1],
                                     accum_out=rs[:, b, 0:1]).then_inc(exped, 1)

            def high(r, q, g):
                i, t, b = step(r, q)
                act.wait_ge(transposed, 2 * i + g + 1)
                wait(act, summed, i - 1)
                nc.scalar.copy(eh[:, b, 4 * g:4 * g + 4, :], TB[g][:, :, :]).then_inc(hi_ready, 1)

            def body(r, q, final=False):
                high(r, q, 0)
                high(r, q, 1)
                if not final:
                    exponential(r, q + 1)

            exponential(0, 0)
            body(0, 0)
            body(0, 1)
            body(0, 2)
            with act.Fori(1, TILES - 1) as r:
                body(r, 1)
                body(r, 2)
            body(TILES - 1, 1, final=True)

        if store:
            @block.sync
            def _(sp):
                def save(r, q):
                    i, t, b = step(r, q)
                    sp.wait_ge(x_ready, i + 1)
                    dst = c.out_dram[b].rearrange("(t p) d -> p t d", p=P)
                    sp.dma_start(dst[:, bass.ds(t, 1), :], c.x[:, b, bass.ds(t, 1), :]).then_inc(stored, 16)

                with sp.Fori(0, TILES) as r:
                    save(r, 0)
                    save(r, 1)
                sp.wait_ge(stored, 16 * STEPS)


def save_x(nc, c):
    with ExitStack() as ctx:
        stored = nc.alloc_semaphore("x_stored")
        block = ctx.enter_context(nc.Block())

        @block.sync
        def _(sp):
            for b in range(BATCH):
                sp.dma_start(c.out_dram[b].rearrange("(t p) d -> p t d", p=P), c.x[:, b, :, :]).then_inc(stored, 16)
            sp.wait_ge(stored, 16 * BATCH)


def moe(nc, c, name, store=False):
    row_stats(nc, c, f"{name}_rows", LN_EPS)
    with ExitStack() as ctx:
        xT = ctx.enter_context(nc.sbuf_tensor(f"{name}_xT", [P, 2, BATCH * SEQ], F16))
        sT = ctx.enter_context(nc.sbuf_tensor(f"{name}_sT", [P, SB, BATCH, P], F32))
        eo = ctx.enter_context(nc.sbuf_tensor(f"{name}_eo", [P, BATCH, SB, 2, DM], F16))
        with ExitStack() as tokens:
            xh = tokens.enter_context(nc.sbuf_tensor(f"{name}_xh", [P, NT, 2, DM], F16))
            moe_normalise(nc, c, f"{name}_norm", xh, xT)
            moe_dispatch(nc, c, f"{name}_disp", xh, xT, sT)
        moe_experts(nc, c, f"{name}_exp", sT, eo)
        moe_combine(nc, c, f"{name}_comb", xT, eo, store)


def ssm_inputs(nc, c, name, xT, dt_half, a, ecum, etot):
    with ExitStack() as ctx:
        def sem(what):
            return nc.alloc_semaphore(f"{name}_{what}")

        def sb(what, shape):
            return ctx.enter_context(nc.sbuf_tensor(f"{name}_{what}", shape, F32))

        G, NG = 4, NT // 4
        xn, xl, xa = sb("xn", [P, 2, G, DM]), sb("xl", [P, 2, G, DM]), sb("xa", [P, 2, G * P])
        raw, neg, ex, up, lg, rc = (sb(n, [P, NT, NH]) for n in ("raw", "neg", "ex", "up", "lg", "rc"))
        ea = sb("ea", [P, NH])
        ps = [ctx.enter_context(nc.psum_tensor(f"{name}_ps{i}", [P, G * P], F32)) for i in range(2)]
        DT = ctx.enter_context(nc.psum_tensor(f"{name}_DT", [P, 512], F32))
        CU = ctx.enter_context(nc.psum_tensor(f"{name}_CU", [P, 512], F32))
        xn_ready, xl_ready, x_added, transposed = sem("xn_ready"), sem("xl_ready"), sem("x_added"), sem("transposed")
        xa_ready, xT_ready, dt_done = sem("xa_ready"), sem("xT_ready"), sem("dt_done")
        dve_step, neg_ready, act_step, a_ready, sums_done = (
            sem("dve_step"), sem("neg_ready"), sem("act_step"), sem("a_ready"), sem("sums_done"))
        xf = c.x[:, :, :, :].rearrange("p b t d -> p (b t) d")
        dts = DT[:, 0:NT * NH].rearrange("p (t h) -> p t h", h=NH)
        block = ctx.enter_context(nc.Block(no_gpsimd_drain=True))

        @block.vector
        def _(dve):
            def normalise(g, pp):
                wait(dve, transposed, g - 1)
                wait(dve, x_added, g - 1)
                for q in range(G):
                    t = bass.ds(g * G + q, 1)
                    last = nc.vector.tensor_scalar(xn[:, pp, q, :], xf[:, t, :], c.mean[:, t], c.s[:, t],
                                                   ALU.subtract, ALU.mult)
                last.then_inc(xn_ready, 1)
                for q in range(G):
                    t = bass.ds(g * G + q, 1)
                    last = nc.vector.tensor_scalar(xl[:, pp, q, :], xf[:, t, :], c.mean[:, t], c.r1[:, t],
                                                   ALU.subtract, ALU.mult)
                last.then_inc(xl_ready, 1)

            def keep(g, pp):
                dve.wait_ge(xa_ready, g + 1)
                nc.vector.tensor_copy(xT[:, bass.ds(g * (G * P), G * P)], xa[:, pp, :]).then_inc(xT_ready, 1)

            normalise(0, 0)
            normalise(1, 1)
            keep(0, 0)
            with dve.Fori(0, NG // 2 - 1) as r:
                g = 2 * r + 1
                for q in range(2):
                    normalise(g + q + 1, q % 2)
                    keep(g + q, (q + 1) % 2)
            keep(NG - 1, 1)
            dve.wait_ge(dt_done, NG)
            bias = c.dtb[:, :].unsqueeze(1).broadcast_to([P, NT, NH])
            chain(dve, dve_step, nc.vector.tensor_tensor(raw[:, :, :], dts, bias, ALU.add), 1)
            nc.vector.scalar_tensor_tensor(out=neg[:, :, :], in0=raw[:, :, :], scalar=-1.0, in1=raw[:, :, :],
                                           op0=ALU.mult, op1=ALU.min).then_inc(neg_ready, 1)
            dve.wait_ge(act_step, 2)
            chain(dve, dve_step, nc.vector.tensor_scalar(up[:, :, :], ex[:, :, :], 1.0, None, ALU.add), 2)
            nc.vector.reciprocal(rc[:, :, :], up[:, :, :]).then_inc(neg_ready, 1)
            chain(dve, dve_step, nc.vector.tensor_scalar(neg[:, :, :], up[:, :, :], -1.0, None, ALU.add), 3)
            chain(dve, dve_step, nc.vector.tensor_tensor(ex[:, :, :], ex[:, :, :], neg[:, :, :], ALU.subtract), 4)
            chain(dve, dve_step, nc.vector.tensor_tensor(ex[:, :, :], ex[:, :, :], rc[:, :, :], ALU.mult), 5)
            dve.wait_ge(act_step, 3)
            chain(dve, dve_step, nc.vector.tensor_tensor(lg[:, :, :], lg[:, :, :], ex[:, :, :], ALU.add), 6)
            chain(dve, dve_step, nc.vector.scalar_tensor_tensor(out=raw[:, :, :], in0=raw[:, :, :], scalar=0.0,
                                                                in1=lg[:, :, :], op0=ALU.max, op1=ALU.add), 7)
            nc.vector.tensor_scalar(dt_half[:, :, :], raw[:, :, :], 0.5, None, ALU.mult)
            nc.vector.scalar_tensor_tensor(out=a[:, :, :], in0=raw[:, :, :], scalar=-1.0,
                                           in1=ea[:, :].unsqueeze(1).broadcast_to([P, NT, NH]),
                                           op0=ALU.mult, op1=ALU.mult).then_inc(a_ready, 1)

        @block.gpsimd
        def _(pool):
            def add(g, pp):
                pool.wait_ge(xl_ready, g + 1)
                t = bass.ds(g * G, G)
                nc.gpsimd.tensor_tensor(xf[:, t, :], xf[:, t, :], xl[:, pp, :, :], ALU.add).then_inc(x_added, 1)

            with pool.Fori(0, NG // 2) as r:
                add(2 * r, 0)
                add(2 * r + 1, 1)
            pool.wait_ge(x_added, NG)

        @block.tensor
        def _(pe):
            def transpose(g, pp):
                pe.wait_ge(xn_ready, g + 1)
                wait(pe, xa_ready, g - 1)
                for q in range(G):
                    last = nc.tensor.transpose(ps[pp][:, q * P:(q + 1) * P], xn[:, pp, q, :], c.ident[:, :])
                last.then_inc(transposed, 1)

            def project(g, pp):
                pe.wait_ge(xa_ready, g + 1)
                for q in range(G):
                    last = nc.tensor.matmul(DT[:, bass.ds((g * G + q) * NH, NH)], xa[:, pp, q * P:(q + 1) * P],
                                            c.wpT[:, PROJ:PROJ + NH], start=True, stop=True)
                last.then_inc(dt_done, 1)

            transpose(0, 0)
            transpose(1, 1)
            with pe.Fori(1, NG // 2) as r:
                for q in range(2):
                    project(2 * r + q - 2, q)
                    transpose(2 * r + q, q)
            project(NG - 2, 0)
            project(NG - 1, 1)
            pe.wait_ge(a_ready, 1)
            av = a[:, :, :].rearrange("p t h -> p (t h)")
            nc.tensor.matmul(CU[:, 0:P], c.upto[:, :], av, start=True, stop=True)
            nc.tensor.matmul(CU[:, P:2 * P], c.ones[:, :], av, start=True, stop=True).then_inc(sums_done, 1)

        @block.scalar
        def _(act):
            def evacuate(g, pp):
                act.wait_ge(transposed, g + 1)
                wait(act, xT_ready, g - 1)
                wait(act, dt_done, g - 1)
                nc.scalar.copy(xa[:, pp, :], ps[pp][:, :]).then_inc(xa_ready, 1)

            evacuate(0, 0)
            evacuate(1, 1)
            with act.Fori(1, NG // 2) as r:
                for q in range(2):
                    evacuate(2 * r + q, q)
            nc.scalar.activation(ea[:, :], c.alog[:, :], ACT.Exp).then_inc(act_step, 1)
            act.wait_ge(neg_ready, 1)
            nc.scalar.activation(ex[:, :, :], neg[:, :, :], ACT.Exp).then_inc(act_step, 1)
            act.wait_ge(neg_ready, 2)
            nc.scalar.activation(lg[:, :, :], up[:, :, :], ACT.Ln).then_inc(act_step, 1)
            act.wait_ge(sums_done, 1)
            nc.scalar.activation(ecum[:, :, :].rearrange("p t h -> p (t h)"), CU[:, 0:P], ACT.Exp)
            nc.scalar.activation(etot[:, :, :].rearrange("p t h -> p (t h)"), CU[:, P:2 * P], ACT.Exp)


def ssm_scan(nc, c, name, xT, dt_half, a, ecum, etot):
    with ExitStack() as ctx:
        def sem(what):
            return nc.alloc_semaphore(f"{name}_{what}")

        def sb(what, shape):
            return ctx.enter_context(nc.sbuf_tensor(f"{name}_{what}", shape, F32))

        HALO = TAPS - 1
        xs = sb("xs", [P, 2, 2, BATCH, HALO + P])
        bc = sb("bc", [P, 2, 2, BATCH, P])
        zt, zg = sb("zt", [P, 2, BATCH, P]), sb("zg", [P, 2, 2, BATCH, P])
        cv, th = sb("cv", [P, 2, BATCH, P]), sb("th", [P, 2, BATCH, P])
        xg = sb("xg", [P, 2, 2, BATCH, P])
        am, dd = sb("am", [P, BATCH, NH, P]), sb("dd", [P, BATCH, NH, P])
        gm, pr = sb("gm", [P, BATCH, P]), sb("pr", [P, BATCH, NH, P])
        xt, xw = sb("xt", [P, BATCH, NH, HD]), sb("xw", [P, BATCH, NH, HD])
        bt = sb("bt", [P, BATCH, P])
        st = sb("st", [P, BATCH, NH, HD])
        yo, y = sb("yo", [P, BATCH, NH, HD]), sb("y", [P, BATCH, CH])
        gd, gt = sb("gd", [P, 2, BATCH, P]), sb("gt", [P, 2, BATCH, P])

        def pb(what, shape):
            return ctx.enter_context(nc.psum_tensor(f"{name}_{what}", shape, F32))

        ZB, XB, CB = pb("ZB", [P, 2, BATCH, P]), pb("XB", [P, 2, BATCH, P]), pb("CB", [P, 2, BATCH, P])
        DB = [pb("DB0", [P, NH, P]), pb("DB1", [P, NH, P])]
        GB = pb("GB", [P, 512])
        TB = pb("TB", [P, 512])
        YB = pb("YB", [P, 512])
        x_proj, bc_proj, z_proj, decay_done = sem("x_proj"), sem("bc_proj"), sem("z_proj"), sem("decay_done")
        cb_done, xt_done, y_done, st_done = sem("cb_done"), sem("xt_done"), sem("y_done"), sem("st_done")
        yT_done, out_done = sem("yT_done"), sem("out_done")
        xs_ready, bc_ready, zt_ready, tap_ready = sem("xs_ready"), sem("bc_ready"), sem("zt_ready"), sem("tap_ready")
        th_ready, dd_ready, bt_ready = sem("th_ready"), sem("dd_ready"), sem("bt_ready")
        gm_ready, xt_ready, xw_ready, x_added = sem("gm_ready"), sem("xt_ready"), sem("xw_ready"), sem("x_added")
        tap_step, cv_ready, xg_ready, zg_ready = sem("tap_step"), sem("cv_ready"), sem("xg_ready"), sem("zg_ready")
        yo_ready, y_ready, st_step, st_ready = sem("yo_ready"), sem("y_ready"), sem("st_step"), sem("st_ready")
        gd_ready, gt_ready = sem("gd_ready"), sem("gt_ready")
        am_ready, pr_ready = sem("am_ready"), sem("pr_ready")
        zeroed = sem("zeroed")
        K = TILES
        xTb = xT[:, :].rearrange("p (b l) -> p b l", b=BATCH)

        def of_tile(v, k):
            return v[:, :, :].rearrange("p (b t) h -> p b t h", b=BATCH)[:, :, bass.ds(k, 1), :]\
                .rearrange("p b a h -> p (b a) h")

        block = ctx.enter_context(nc.Block(no_gpsimd_drain=True))

        def periods(eng, body):
            body(0, 0, first=True)
            body(1, 1)
            with eng.Fori(1, K // 2 - 1) as r:
                body(2 * r, 0)
                body(2 * r + 1, 1)
            body(K - 2, 0)
            body(K - 1, 1, final=True)

        @block.tensor
        def _(pe):
            def project(k, pp):
                tok = xTb[:, :, bass.ds(k * P, P)]
                for bank, col, free, done in ((XB, CH, xs_ready, x_proj), (CB, 2 * CH, bc_ready, bc_proj),
                                              (ZB, 0, zg_ready, z_proj)):
                    wait(pe, free, k)
                    for n in range(2):
                        last = nc.tensor.matmul(bank[:, n, :, :], c.wpT[:, col + n * P:col + (n + 1) * P], tok,
                                                start=True, stop=True)
                    last.then_inc(done, 1)

            def decay(k):
                pe.wait_ge(am_ready, k + 1)
                wait(pe, dd_ready, k)
                for b in range(BATCH):
                    last = nc.tensor.matmul(DB[b][:, :, :], c.after[:, :], am[:, b, :, :], start=True, stop=True)
                last.then_inc(decay_done, 1)

            def products(k, pp):
                pe.wait_ge(bc_ready, k + 1)
                wait(pe, y_ready, k)
                for b in range(BATCH):
                    nc.tensor.matmul(GB[:, b * P:(b + 1) * P], bc[:, pp, 0, b, :], bc[:, pp, 1, b, :],
                                     start=True, stop=True)
                for b in range(BATCH):
                    last = nc.tensor.transpose(GB[:, (2 + b) * P:(3 + b) * P], bc[:, pp, 0, b, :], c.ident[:, :])
                last.then_inc(cb_done, 1)
                pe.wait_ge(xg_ready, k + 1)
                wait(pe, st_ready, k)
                for b in range(BATCH):
                    for n in range(2):
                        last = nc.tensor.transpose(TB[:, (2 * b + n) * P:(2 * b + n + 1) * P], xg[:, pp, n, b, :],
                                                   c.ident[:, :])
                last.then_inc(xt_done, 1)

            def outputs(k, pp):
                pe.wait_ge(pr_ready, k + 1)
                pe.wait_ge(xt_ready, k + 1)
                wait(pe, x_added, k)
                for b in range(BATCH):
                    for h in range(NH):
                        col = b * CH + h * HD
                        nc.tensor.matmul(YB[:, col:col + HD], pr[:, b, h, :], xt[:, b, h, :], start=True, stop=True)
                pe.wait_ge(bt_ready, k + 1)
                wait(pe, st_ready, k)
                pe.wait_ge(zeroed, 2)
                for b in range(BATCH):
                    last = nc.tensor.matmul(GB[:, b * CH:(b + 1) * CH], bc[:, pp, 1, b, :], st[:, b, :, :],
                                            start=True, stop=True)
                last.then_inc(y_done, 1)
                pe.wait_ge(xw_ready, k + 1)
                for b in range(BATCH):
                    last = nc.tensor.matmul(TB[:, b * CH:(b + 1) * CH], bt[:, b, :], xw[:, b, :, :],
                                            start=True, stop=True)
                last.then_inc(st_done, 1)

            def y_transpose(k):
                pe.wait_ge(y_ready, k + 1)
                for n in range(2):
                    for b in range(BATCH):
                        last = nc.tensor.transpose(YB[:, (2 * n + b) * P:(2 * n + b + 1) * P],
                                                   y[:, b, n * P:(n + 1) * P], c.ident[:, :])
                last.then_inc(yT_done, 1)

            def project_out(k):
                pe.wait_ge(gt_ready, k + 1)
                for b in range(BATCH):
                    for n in range(2):
                        last = nc.tensor.matmul(YB[:, b * P:(b + 1) * P], gt[:, n, b, :], c.woutT[:, n, :],
                                                start=(n == 0), stop=(n == 1))
                last.then_inc(out_done, 1)

            def body(k, pp, first=False, final=False):
                products(k, pp)
                if not first:
                    project_out(k - 1)
                if not final:
                    project(k + 1, 1 - pp)
                outputs(k, pp)
                if not final:
                    decay(k + 1)
                y_transpose(k)

            project(0, 0)
            decay(0)
            periods(pe, body)
            project_out(K - 1)

        @block.scalar
        def _(act):
            def ahead(k, pp):
                act.wait_ge(x_proj, k + 1)
                wait(act, cv_ready, k - 1)
                if isinstance(k, int) and k == 0:
                    act.wait_ge(zeroed, 2)
                else:
                    nc.scalar.copy(xs[:, pp, :, :, 0:HALO], xs[:, 1 - pp, :, :, P:P + HALO])
                chain(act, xs_ready, nc.scalar.copy(xs[:, pp, :, :, HALO:HALO + P], XB[:, :, :, :]), k + 1)
                wait(act, xg_ready, k)
                for n in range(2):
                    last = nc.scalar.activation(cv[:, n, :, :], xs[:, pp, n, :, 0:P], ACT.Identity,
                                                scale=c.convw[:, n, 0:1], bias=c.convb[:, n:n + 1])
                last.then_inc(tap_ready, 1)
                act.wait_ge(bc_proj, k + 1)
                wait(act, y_done, k - 1)
                nc.scalar.copy(bc[:, pp, :, :, :], CB[:, :, :, :]).then_inc(bc_ready, 1)
                act.wait_ge(z_proj, k + 1)
                nc.scalar.activation(zt[:, :, :, :], ZB[:, :, :, :], ACT.Tanh, scale=0.5).then_inc(zt_ready, 1)
                act.wait_ge(cv_ready, k + 1)
                nc.scalar.activation(th[:, :, :, :], cv[:, :, :, :], ACT.Tanh, scale=0.5).then_inc(th_ready, 1)
                act.wait_ge(decay_done, k + 1)
                wait(act, pr_ready, k)
                wait(act, xw_ready, k)
                for b in range(BATCH):
                    last = nc.scalar.activation(dd[:, b, :, :], DB[b][:, :, :], ACT.Exp)
                last.then_inc(dd_ready, 1)

            def body(k, pp, first=False, final=False):
                act.wait_ge(gm_ready, k + 1)
                wait(act, st_done, k)
                nc.scalar.copy(bt[:, :, :].rearrange("p b n -> p (b n)"), GB[:, 2 * P:4 * P]).then_inc(bt_ready, 1)
                if not final:
                    ahead(k + 1, 1 - pp)

            ahead(0, 0)
            periods(act, body)

        @block.gpsimd
        def _(pool):
            def decays(k):
                wait(pool, decay_done, k)
                at = of_tile(a, k).unsqueeze(3).broadcast_to([P, BATCH, NH, P])
                upto = c.upto[:, :].unsqueeze(1).unsqueeze(1).broadcast_to([P, BATCH, NH, P])
                nc.gpsimd.tensor_tensor(am[:, :, :, :], upto, at, ALU.mult).then_inc(am_ready, 1)

            def masked(k):
                pool.wait_ge(dd_ready, k + 1)
                pool.wait_ge(gm_ready, k + 1)
                wait(pool, y_done, k)
                nc.gpsimd.tensor_tensor(pr[:, :, :, :], dd[:, :, :, :],
                                        gm[:, :, :].unsqueeze(2).broadcast_to([P, BATCH, NH, P]), ALU.mult)\
                    .then_inc(pr_ready, 1)

            def body(k, pp, first=False, final=False):
                masked(k)
                if not final:
                    decays(k + 1)

            nc.gpsimd.memset(xs[:, 0, :, :, 0:HALO], 0.0).then_inc(zeroed, 1)
            nc.gpsimd.memset(st[:, :, :, :], 0.0).then_inc(zeroed, 1)
            decays(0)
            periods(pool, body)
            pool.wait_ge(pr_ready, K)

        @block.vector
        def _(dve):
            def inside(k, pp):
                dve.wait_ge(cb_done, k + 1)
                wait(dve, pr_ready, k)
                nc.vector.tensor_tensor(gm[:, :, :], GB[:, 0:BATCH * P].rearrange("p (b t) -> p b t", b=BATCH),
                                        c.upto[:, :].unsqueeze(1).broadcast_to([P, BATCH, P]), ALU.mult)\
                    .then_inc(gm_ready, 1)
                dve.wait_ge(xt_done, k + 1)
                wait(dve, y_done, k)
                chain(dve, xt_ready, nc.vector.tensor_tensor(
                    xt[:, :, :, :], TB[:, :].rearrange("p (b h e) -> p b h e", b=BATCH, h=NH),
                    of_tile(dt_half, k).unsqueeze(3).broadcast_to([P, BATCH, NH, HD]), ALU.mult), k + 1)
                dve.wait_ge(dd_ready, k + 1)
                wait(dve, st_done, k)
                nc.vector.tensor_tensor(xw[:, :, :, :], xt[:, :, :, :],
                                        dd[:, :, :, P - 1:P].broadcast_to([P, BATCH, NH, HD]), ALU.mult)\
                    .then_inc(xw_ready, 1)

            def residual(k):
                dve.wait_ge(out_done, k + 1)
                xk = c.x[:, :, bass.ds(k, 1), :].rearrange("p b a d -> p (b a) d")
                nc.vector.tensor_tensor(xk, YB[:, 0:BATCH * P].rearrange("p (b d) -> p b d", b=BATCH), xk, ALU.add)\
                    .then_inc(x_added, 1)

            def ahead(k, pp):
                dve.wait_ge(tap_ready, k + 1)
                for tap in range(1, TAPS):
                    for n in range(2):
                        last = nc.vector.scalar_tensor_tensor(
                            out=cv[:, n, :, :], in0=xs[:, pp, n, :, tap:tap + P], scalar=c.convw[:, n, tap:tap + 1],
                            in1=cv[:, n, :, :], op0=ALU.mult, op1=ALU.add)
                    if tap < TAPS - 1:
                        chain(dve, tap_step, last, (TAPS - 2) * k + tap)
                last.then_inc(cv_ready, 1)
                dve.wait_ge(zt_ready, k + 1)
                nc.vector.scalar_tensor_tensor(out=zg[:, pp, :, :, :].rearrange("p n b t -> p (n b t)"),
                                               in0=zt[:, :, :, :].rearrange("p n b t -> p (n b t)"), scalar=1.0,
                                               in1=ZB[:, :, :, :].rearrange("p n b t -> p (n b t)"),
                                               op0=ALU.add, op1=ALU.mult).then_inc(zg_ready, 1)
                dve.wait_ge(th_ready, k + 1)
                wait(dve, xt_done, k - 1)
                nc.vector.scalar_tensor_tensor(out=xg[:, pp, :, :, :].rearrange("p n b t -> p (n b t)"),
                                               in0=th[:, :, :, :].rearrange("p n b t -> p (n b t)"), scalar=1.0,
                                               in1=cv[:, :, :, :].rearrange("p n b t -> p (n b t)"),
                                               op0=ALU.add, op1=ALU.mult).then_inc(xg_ready, 1)

            def combine(k, pp):
                dve.wait_ge(y_done, k + 1)
                wait(dve, yT_done, k)
                chain(dve, yo_ready, nc.vector.tensor_tensor(
                    yo[:, :, :, :], GB[:, :].rearrange("p (b h e) -> p b h e", b=BATCH, h=NH),
                    of_tile(ecum, k).unsqueeze(3).broadcast_to([P, BATCH, NH, HD]), ALU.mult), k + 1)
                nc.vector.tensor_tensor(y[:, :, :].rearrange("p b e -> p (b e)"), YB[:, :],
                                        yo[:, :, :, :].rearrange("p b h e -> p (b h e)"), ALU.add).then_inc(y_ready, 1)
                chain(dve, st_step, nc.vector.tensor_tensor(
                    st[:, :, :, :], st[:, :, :, :],
                    of_tile(etot, k).unsqueeze(3).broadcast_to([P, BATCH, NH, HD]), ALU.mult), k + 1)
                dve.wait_ge(st_done, k + 1)
                nc.vector.tensor_tensor(st[:, :, :, :].rearrange("p b h e -> p (b h e)"),
                                        st[:, :, :, :].rearrange("p b h e -> p (b h e)"), TB[:, :], ALU.add)\
                    .then_inc(st_ready, 1)
                dve.wait_ge(yT_done, k + 1)
                for n in range(2):
                    last = nc.vector.scalar_tensor_tensor(
                        out=gd[:, n, :, :].rearrange("p b t -> p (b t)"),
                        in0=xg[:, pp, n, :, :].rearrange("p b t -> p (b t)"), scalar=c.dcol[:, n:n + 1],
                        in1=YB[:, n * BATCH * P:(n + 1) * BATCH * P], op0=ALU.mult, op1=ALU.add)
                chain(dve, gd_ready, last, k + 1)
                wait(dve, out_done, k)
                nc.vector.tensor_tensor(gt[:, :, :, :], gd[:, :, :, :], zg[:, pp, :, :, :], ALU.mult)\
                    .then_inc(gt_ready, 1)

            def body(k, pp, first=False, final=False):
                inside(k, pp)
                if not first:
                    residual(k - 1)
                if not final:
                    ahead(k + 1, 1 - pp)
                combine(k, pp)

            dve.wait_ge(zeroed, 2)
            ahead(0, 0)
            periods(dve, body)
            residual(K - 1)


def ssm(nc, c):
    row_stats(nc, c, "ssm_rows", RMS_EPS)
    with ExitStack() as ctx:
        def sb(what, shape):
            return ctx.enter_context(nc.sbuf_tensor(f"ssm_{what}", shape, F32))

        xT = sb("xT", [P, BATCH * SEQ])
        tables = [sb(n, [P, NT, NH]) for n in ("dt_half", "a", "ecum", "etot")]
        ssm_inputs(nc, c, "ssm_in", xT, *tables)
        ssm_scan(nc, c, "ssm", xT, *tables)


def linear_attention(nc, c):
    row_stats(nc, c, "att_rows", None)
    with ExitStack() as ctx:
        def sem(what):
            return nc.alloc_semaphore(f"att_{what}")

        def sb(what, shape):
            return ctx.enter_context(nc.sbuf_tensor(f"att_{what}", shape, F32))

        KV = AH * AE * AD
        HE = AH * AE
        xn, xT = sb("xn", [P, 2, DM]), sb("xT", [P, 2, P])
        ex, qk = sb("ex", [P, 2, 2 * DM]), sb("qk", [P, 2, 2 * DM])
        neg = sb("neg", [P, 2 * DM])
        vx, kv = sb("vx", [P, 2, AH, AE]), sb("kv", [P, 2, KV])
        qT, st = sb("qT", [P, 2, P]), sb("st", [P, BATCH, HE])
        w, inter, num, inc = sb("w", [P, KV]), sb("inter", [P, HE]), sb("num", [P, AH, AE]), sb("inc", [P, HE])
        den, rden = sb("den", [P, AH]), sb("rden", [P, AH])
        o, oT = sb("o", [P, 2, DM]), sb("oT", [P, 2, P])

        def pb(what):
            return ctx.enter_context(nc.psum_tensor(f"att_{what}", [P, 512], F32))

        XB, QB, QT = pb("XB"), pb("QB"), pb("QT")
        CUM = ctx.enter_context(nc.psum_tensor("att_CUM", [P, 3 * 512], F32))
        SB_, OB = pb("SB"), pb("OB")
        xn_ready, x_transposed, xT_ready, qkv_done = sem("xn_ready"), sem("x_transposed"), sem("xT_ready"), sem("qkv_done")
        ex_ready, v_ready, negative_ready, qk_ready = sem("ex_ready"), sem("v_ready"), sem("negative_ready"), sem("qk_ready")
        kv_ready, q_transposed, qT_ready, inc_done = sem("kv_ready"), sem("q_transposed"), sem("qT_ready"), sem("inc_done")
        cum_done, w_ready, inter_ready, num_step = sem("cum_done"), sem("w_ready"), sem("inter_ready"), sem("num_step")
        o_ready, o_transposed, oT_ready, out_done = sem("o_ready"), sem("o_transposed"), sem("oT_ready"), sem("out_done")
        x_added, inc_masked, st_ready, zeroed = sem("x_added"), sem("inc_masked"), sem("st_ready"), sem("zeroed")
        STEPS = 2 * TILES
        block = ctx.enter_context(nc.Block(no_gpsimd_drain=True))

        def at(r, q):
            return 2 * r + q, r + q // 2, q % 2

        def exists(r, q):
            return not isinstance(r, int) or 0 <= 2 * r + q < STEPS

        def periods(eng, body):
            for i in range(-4, 4):
                body(0, i)
            with eng.Fori(2, TILES - 2) as r:
                body(r, 0)
                body(r, 1)
            for i in range(STEPS - 4, STEPS + 1):
                body(0, i)

        @block.tensor
        def _(pe):
            def x_transpose(r, q):
                i, t, b = at(r, q)
                pe.wait_ge(xn_ready, i + 1)
                wait(pe, xT_ready, i)
                nc.tensor.transpose(XB[:, 0:P], xn[:, b, :], c.ident[:, :]).then_inc(x_transposed, 1)

            def project(r, q):
                i, t, b = at(r, q)
                pe.wait_ge(xT_ready, i + 1)
                wait(pe, qk_ready, i)
                nc.tensor.matmul(QB[:, 0:3 * DM], xT[:, b, :], c.wqkvT[:, :], start=True, stop=True)\
                    .then_inc(qkv_done, 1)

            def q_transpose(r, q):
                i, t, b = at(r, q)
                pe.wait_ge(qk_ready, i + 1)
                wait(pe, qT_ready, i)
                nc.tensor.transpose(QT[:, 0:P], qk[:, b, 0:DM], c.ident[:, :]).then_inc(q_transposed, 1)

            def increment(r, q):
                i, t, b = at(r, q)
                pe.wait_ge(v_ready, i + 1)
                wait(pe, st_ready, i)
                nc.tensor.matmul(SB_[:, 0:HE], qk[:, b, DM:2 * DM], vx[:, b, :, :], start=True, stop=True)\
                    .then_inc(inc_done, 1)

            def add_up(r, q):
                i, t, b = at(r, q)
                pe.wait_ge(kv_ready, i + 1)
                wait(pe, inter_ready, i)
                for col in range(0, KV, 512):
                    end = min(KV, col + 512)
                    nc.tensor.matmul(CUM[:, col:end], c.upto[:, :], kv[:, b, col:end], start=True, stop=True)
                pe.wait_ge(qT_ready, i + 1)
                wait(pe, st_ready, i - 1)
                nc.tensor.matmul(CUM[:, KV:KV + HE], qT[:, b, :], st[:, b, :], start=True, stop=True)\
                    .then_inc(cum_done, 1)

            def o_transpose(r, q):
                i, t, b = at(r, q)
                pe.wait_ge(o_ready, i + 1)
                wait(pe, x_added, i)
                nc.tensor.transpose(OB[:, 0:P], o[:, b, :], c.ident[:, :]).then_inc(o_transposed, 1)

            def project_out(r, q):
                i, t, b = at(r, q)
                pe.wait_ge(oT_ready, i + 1)
                nc.tensor.matmul(OB[:, P:2 * P], oT[:, b, :], c.waoT[:, :], start=True, stop=True).then_inc(out_done, 1)

            def body(r, q):
                if exists(r, q - 1):
                    o_transpose(r, q - 1)
                if exists(r, q + 1):
                    add_up(r, q + 1)
                if exists(r, q - 1):
                    project_out(r, q - 1)
                if exists(r, q + 2):
                    q_transpose(r, q + 2)
                    increment(r, q + 2)
                if exists(r, q + 3):
                    x_transpose(r, q + 3)
                    project(r, q + 3)

            pe.wait_ge(zeroed, 2)
            periods(pe, body)

        @block.scalar
        def _(act):
            def o_copy(r, q):
                i, t, b = at(r, q)
                act.wait_ge(o_transposed, i + 1)
                wait(act, out_done, i - 1)
                nc.scalar.copy(oT[:, b, :], OB[:, 0:P]).then_inc(oT_ready, 1)

            def q_copy(r, q):
                i, t, b = at(r, q)
                act.wait_ge(q_transposed, i + 1)
                wait(act, cum_done, i - 1)
                nc.scalar.copy(qT[:, b, :], QT[:, 0:P]).then_inc(qT_ready, 1)

            def inputs(r, q):
                i, t, b = at(r, q)
                act.wait_ge(x_transposed, i + 1)
                wait(act, qkv_done, i - 1)
                nc.scalar.copy(xT[:, b, :], XB[:, 0:P]).then_inc(xT_ready, 1)
                act.wait_ge(qkv_done, i + 1)
                wait(act, qk_ready, i - 1)
                chain(act, negative_ready, nc.scalar.activation(neg[:, :], QB[:, 0:2 * DM], ACT.Relu, scale=-1.0), i + 1)
                nc.scalar.activation(ex[:, b, :], neg[:, :], ACT.Exp, scale=-1.0).then_inc(ex_ready, 1)
                wait(act, kv_ready, i - 1)
                wait(act, inc_done, i - 1)
                nc.scalar.copy(vx[:, b, :, 0:AD], QB[:, 2 * DM:3 * DM].rearrange("p (h e) -> p h e", e=AD))\
                    .then_inc(v_ready, 1)

            def body(r, q):
                if exists(r, q - 1):
                    o_copy(r, q - 1)
                if exists(r, q + 2):
                    q_copy(r, q + 2)
                if exists(r, q + 3):
                    inputs(r, q + 3)

            act.wait_ge(zeroed, 2)
            periods(act, body)

        @block.gpsimd
        def _(pool):
            def products(r, q):
                i, t, b = at(r, q)
                pool.wait_ge(qk_ready, i + 1)
                wait(pool, cum_done, i - 1)
                k = qk[:, b, DM:2 * DM].rearrange("p (h d) -> p h d", d=AD).unsqueeze(2)\
                    .broadcast_to([P, AH, AE, AD])
                v = vx[:, b, :, :].unsqueeze(3).broadcast_to([P, AH, AE, AD])
                nc.gpsimd.tensor_tensor(kv[:, b, :].rearrange("p (h e d) -> p h e d", h=AH, e=AE), k, v, ALU.mult)\
                    .then_inc(kv_ready, 1)

            def body(r, q):
                if exists(r, q + 2):
                    products(r, q + 2)

            nc.gpsimd.memset(vx[:, :, :, :], 1.0).then_inc(zeroed, 1)
            nc.gpsimd.memset(st[:, :, :], 0.0).then_inc(zeroed, 1)
            periods(pool, body)
            pool.wait_ge(kv_ready, STEPS)

        @block.vector
        def _(dve):
            mask = c.mask_blk[:, :, :].rearrange("p h e -> p (h e)")

            def normalise(r, q):
                i, t, b = at(r, q)
                wait(dve, x_transposed, i - 1)
                tt = bass.ds(b * TILES + t, 1)
                nc.vector.tensor_scalar(xn[:, b, :], c.x[:, b, bass.ds(t, 1), :].rearrange("p a d -> p (a d)"),
                                        c.mean[:, tt], c.r1[:, tt], ALU.subtract, ALU.mult).then_inc(xn_ready, 1)

            def features(r, q):
                i, t, b = at(r, q)
                dve.wait_ge(ex_ready, i + 1)
                dve.wait_ge(v_ready, i + 1)
                wait(dve, w_ready, i - 1)
                wait(dve, kv_ready, i - 1)
                wait(dve, inc_done, i - 1)
                wait(dve, q_transposed, i - 1)
                nc.vector.scalar_tensor_tensor(out=qk[:, b, :], in0=QB[:, 0:2 * DM], scalar=0.0, in1=ex[:, b, :],
                                               op0=ALU.max, op1=ALU.add).then_inc(qk_ready, 1)

            def read(r, q):
                i, t, b = at(r, q)
                dve.wait_ge(cum_done, i + 1)
                qb = qk[:, b, 0:DM].rearrange("p (h d) -> p h d", d=AD).unsqueeze(2).broadcast_to([P, AH, AE, AD])
                nc.vector.tensor_tensor(w[:, :].rearrange("p (h e d) -> p h e d", h=AH, e=AE),
                                        CUM[:, 0:KV].rearrange("p (h e d) -> p h e d", h=AH, e=AE), qb, ALU.mult)\
                    .then_inc(w_ready, 1)
                nc.vector.tensor_copy(inter[:, :], CUM[:, KV:KV + HE]).then_inc(inter_ready, 1)

            def finish(r, q):
                i, t, b = at(r, q)
                numf = num[:, :, :].rearrange("p h e -> p (h e)")
                dve.wait_ge(w_ready, i + 1)
                chain(dve, num_step, nc.vector.tensor_reduce(
                    numf, w[:, :].rearrange("p (m d) -> p m d", d=AD), AX.X, ALU.add), 4 * i + 1)
                chain(dve, num_step, nc.vector.tensor_tensor(numf, numf, inter[:, :], ALU.add), 4 * i + 2)
                chain(dve, num_step, nc.vector.tensor_scalar(den[:, :], num[:, :, AD], ATT_EPS, None, ALU.add), 4 * i + 3)
                chain(dve, num_step, nc.vector.reciprocal(rden[:, :], den[:, :]), 4 * i + 4)
                wait(dve, o_transposed, i - 1)
                nc.vector.tensor_tensor(o[:, b, :].rearrange("p (h e) -> p h e", e=AD), num[:, :, 0:AD],
                                        rden[:, :].unsqueeze(2).broadcast_to([P, AH, AD]), ALU.mult).then_inc(o_ready, 1)

            def update(r, q):
                i, t, b = at(r, q)
                dve.wait_ge(inc_done, i + 1)
                chain(dve, inc_masked, nc.vector.tensor_tensor(inc[:, :], SB_[:, 0:HE], mask, ALU.mult), i + 1)
                dve.wait_ge(cum_done, i + 1)
                nc.vector.tensor_tensor(st[:, b, :], st[:, b, :], inc[:, :], ALU.add).then_inc(st_ready, 1)

            def residual(r, q):
                i, t, b = at(r, q)
                dve.wait_ge(out_done, i + 1)
                xt = c.x[:, b, bass.ds(t, 1), :].rearrange("p a d -> p (a d)")
                nc.vector.tensor_tensor(xt, OB[:, P:2 * P], xt, ALU.add).then_inc(x_added, 1)

            def body(r, q):
                if exists(r, q):
                    read(r, q)
                if exists(r, q + 2):
                    features(r, q + 2)
                if exists(r, q):
                    finish(r, q)
                if exists(r, q + 1):
                    update(r, q + 1)
                if exists(r, q - 1):
                    residual(r, q - 1)
                if exists(r, q + 4):
                    normalise(r, q + 4)

            dve.wait_ge(zeroed, 2)
            periods(dve, body)


STAGES = [ssm, lambda nc, c: moe(nc, c, "moe1"), linear_attention, lambda nc, c: moe(nc, c, "moe2", store=True)]


def build(nc, c, stages):
    with ExitStack() as ctx:
        def sb(name, shape, dt=F32):
            return ctx.enter_context(nc.sbuf_tensor(name, shape, dt))

        c.x = sb("x_res", [P, BATCH, TILES, DM])
        c.ident, c.ones = sb("ident", [P, P]), sb("ones", [P, P])
        c.upto, c.after = sb("upto", [P, P]), sb("after", [P, P])
        c.mhalf = sb("mhalf", [P, NT])
        c.mask_blk = sb("mask_blk", [P, AH, AE])
        c.wpT, c.woutT = sb("wpT", [P, PROJ + NH]), sb("woutT", [P, 2, DM])
        c.wqkvT, c.waoT = sb("wqkvT", [P, 3 * DM]), sb("waoT", [P, DM])
        c.seh, c.sel = sb("seh", [P, NS], F16), sb("sel", [P, NS], F16)
        c.bgT, c.buT, c.bdb = sb("bgT", [P, 2, NE]), sb("buT", [P, 2, NE]), sb("bdb", [P, SB, DM])
        c.gcol, c.bcol = sb("gcol", [P, 1]), sb("bcol", [P, 1])
        c.convw, c.convb, c.dcol = sb("convw", [P, 2, TAPS]), sb("convb", [P, 2]), sb("dcol", [P, 2])
        c.alog, c.dtb = sb("alog", [P, NH]), sb("dtb", [P, NH])
        c.mean, c.var = sb("mean", [P, NT]), sb("var", [P, NT])
        c.r1, c.r2, c.s = sb("r1", [P, NT]), sb("r2", [P, NT]), sb("s", [P, NT])
        prepare(nc, c)
        for stage in stages[:-1]:
            with nc.cleanup_on_exit():
                stage(nc, c)
        stages[-1](nc, c)


NAMES = dict(L0_attn_a_x="x_dram", L0_attn_a_norm_w="norm_w", L0_attn_a_in_proj_w="in_proj_w",
             L0_attn_a_conv_w="conv_w", L0_attn_a_conv_b="conv_b", L0_attn_a_A_log="A_log", L0_attn_a_D="D_skip",
             L0_attn_a_dt_bias="dt_bias", L0_attn_a_out_proj_w="out_proj_w", L0_attn_b_Wq="Wq", L0_attn_b_Wk="Wk",
             L0_attn_b_Wv="Wv", L0_attn_b_Wo="Wo", L0_ffn_norm_g="norm_g", L0_ffn_norm_b="norm_b",
             L0_ffn_slot_g="slot_g", L0_ffn_slot_b="slot_b", L0_ffn_scale="scale", L0_ffn_slot_embeds="slot_embeds",
             L0_ffn_Wg="Wg", L0_ffn_bg="bg", L0_ffn_Wu="Wu", L0_ffn_bu="bu", L0_ffn_Wd="Wd", L0_ffn_bd="bd")


def kernel(**inputs):
    import numpy as _np
    import concourse.bacc as _bacc
    from concourse import mybir as _mybir
    from concourse.bass_utils import run_bass_kernel_spmd as _run

    nc = _bacc.Bacc("TRN2", target_bir_lowering=False, num_devices=1)
    core, arrays = Core(), {}
    args = {}
    for name, short in NAMES.items():
        a = _np.ascontiguousarray(inputs[name])
        arrays[f"in_{short}"] = a
        args[short] = nc.dram_tensor(f"in_{short}", a.shape, _mybir.dt.from_np(a.dtype), kind="ExternalInput").ap()
    core.__dict__.update(args)
    core.out_dram = nc.dram_tensor("out", (BATCH, SEQ, DM), _mybir.dt.float32, kind="ExternalOutput").ap()
    build(nc, core, STAGES)
    r = _run(nc, [arrays], core_ids=[0])
    return r.results[0]["out"]
```

```python
import concourse.bass as bass
from concourse import mybir
from contextlib import ExitStack

F32 = mybir.dt.float32
F16 = mybir.dt.float16
ACT = mybir.ActivationFunctionType
ALU = mybir.AluOpType
AX = mybir.AxisListType

P = 128
BATCH, SEQ, DM = 2, 2048, 128
TILES = SEQ // P
NT = BATCH * TILES
LN_EPS, RMS_EPS, ATT_EPS = 1e-5, 1e-6, 1e-8
CH = 256
NH, HD = 4, 64
TAPS = 4
PROJ = 2 * CH + 2 * P
NE, SLOTS, FF = 16, 64, 256
NS = NE * SLOTS
EW = 3 * FF
SB = NS // P
AH, AD = 16, 8
AE = AD + 1


def wait(eng, sem, value):
    if isinstance(value, int) and value <= 0:
        return
    eng.wait_ge(sem, value)


def chain(eng, sem, ins, value):
    ins.then_inc(sem, 1)
    eng.wait_ge(sem, value)


class Core:
    pass


def prepare(nc, c):
    with ExitStack() as ctx:
        def sb(name, shape, dt=F32):
            return ctx.enter_context(nc.sbuf_tensor(name, shape, dt))

        def sem(name):
            return nc.alloc_semaphore(name)

        wp_nat = sb("wp_nat", [P, PROJ // P, DM])
        wdt_nat = sb("wdt_nat", [NH, DM])
        wout_nat = sb("wout_nat", [DM, CH])
        wa_nat = sb("wa_nat", [P, 4, DM])
        se_nat = sb("se_nat", [P, SB, DM])
        b_nat = sb("b_nat", [NE, 2, FF])
        bd_nat = sb("bd_nat", [NE, DM])
        se_st = sb("se_st", [P, SB, 6])
        se_half = sb("se_half", [P, 4, SB])
        se_v, se_sd, se_y, se_t = (sb(f"se_{w}", [P, 1, SB]) for w in ("v", "sd", "y", "t"))
        se_mean, se_scale = sb("se_mean", [P, SB]), sb("se_scale", [P, SB])
        cols = sb("cols", [P, 8])
        se32 = sb("se32", [P, NS])
        dskip = sb("dskip", [P, 2])
        tb = [ctx.enter_context(nc.psum_tensor(f"prep_ps{i}", [P, 512], F32)) for i in range(8)]

        x_in = sem("x_in")
        w_in = sem("w_in")
        cols_in = sem("cols_in")
        se_in = sem("se_in")
        masks_zero = sem("masks_zero")
        masks_ready = sem("masks_ready")
        se_dve = sem("se_dve")
        se_root = sem("se_root")
        se_var = sem("se_var")
        se_scaled = sem("se_scaled")
        tr_done = sem("tr_done")
        ev_act = sem("ev_act")
        ev_dve = sem("ev_dve")
        se_hi = sem("se_hi")

        jobs = []
        for k in range(PROJ // P):
            jobs.append((wp_nat[:, k, :], P, c.wpT[:, k * P:(k + 1) * P], "norm"))
        jobs.append((wdt_nat[:, :], NH, c.wpT[:, PROJ:PROJ + NH], "norm"))
        for k in range(2):
            jobs.append((wout_nat[:, k * P:(k + 1) * P], P, c.woutT[:, k, :], "half"))
        for k in range(3):
            jobs.append((wa_nat[:, k, :], P, c.wqkvT[:, k * P:(k + 1) * P], "copy"))
        jobs.append((wa_nat[:, 3, :], P, c.waoT[:, :], "copy"))
        for which, dst in ((0, c.bgT), (1, c.buT)):
            for k in range(2):
                jobs.append((b_nat[:, which, k * P:(k + 1) * P], NE, dst[:, k, :], "copy"))
        jobs.append((bd_nat[:, :], NE, c.bdT[:, :], "copy"))
        for j in range(SB):
            jobs.append((se_nat[:, j, :], P, se32[:, j * P:(j + 1) * P], "slot"))
        first_se = len(jobs) - SB
        by_act = [n % 2 == 1 and job[3] != "slot" for n, job in enumerate(jobs)]

        xf = c.x[:, :, :, :].rearrange("p b t d -> p (b t) d")
        block = ctx.enter_context(nc.Block(no_gpsimd_drain=True))

        @block.sync
        def _(sp):
            sp.dma_start(wp_nat[:, :, :], c.in_proj_w[0:PROJ, :].rearrange("(k p) d -> p k d", p=P)).then_inc(w_in, 16)
            sp.dma_start(wdt_nat[:, :], c.in_proj_w[PROJ:PROJ + NH, :]).then_inc(w_in, 16)
            sp.dma_start(wout_nat[:, :], c.out_proj_w).then_inc(w_in, 16)
            for k, w in enumerate((c.Wq, c.Wk, c.Wv, c.Wo)):
                sp.dma_start(wa_nat[:, k, :], w).then_inc(w_in, 16)
            sp.dma_start(b_nat[:, 0, :], c.bg).then_inc(w_in, 16)
            sp.dma_start(b_nat[:, 1, :], c.bu).then_inc(w_in, 16)
            sp.dma_start(bd_nat[:, :], c.bd).then_inc(w_in, 16)
            for b in range(BATCH):
                sp.dma_start(c.x[:, b, :, :], c.x_dram[b].rearrange("(t p) d -> p t d", p=P)).then_inc(x_in, 16)

        @block.scalar
        def _(act):
            act.dma_start(se_nat[:, :, :], c.slot_embeds.rearrange("e s d -> (e s) d")
                          .rearrange("(j p) d -> p j d", p=P)).then_inc(se_in, 16)
            for k, v in enumerate((c.norm_w, c.slot_g, c.slot_b)):
                act.dma_start(cols[:, k:k + 1], v.rearrange("(p a) -> p a", a=1)).then_inc(cols_in, 16)
            act.dma_start(cols[:, 3:4], c.scale.rearrange("(p a) -> p a", a=1).broadcast_to([P, 1])).then_inc(cols_in, 16)
            for dst, v in ((c.gcol, c.norm_g), (c.bcol, c.norm_b)):
                act.dma_start(dst[:, :], v.rearrange("(p a) -> p a", a=1)).then_inc(cols_in, 16)
            act.dma_start(c.convw[:, :, :], c.conv_w.rearrange("(k p) t -> p k t", p=P)).then_inc(cols_in, 16)
            act.dma_start(c.convb[:, :], c.conv_b.rearrange("(k p) -> p k", p=P),
                          allow_slow_non_contiguous=True).then_inc(cols_in, 16)
            act.dma_start(c.alog[:, :], c.A_log.rearrange("(a h) -> a h", a=1).broadcast_to([P, NH])).then_inc(cols_in, 16)
            act.dma_start(c.dtb[:, :], c.dt_bias.rearrange("(a h) -> a h", a=1).broadcast_to([P, NH])).then_inc(cols_in, 16)
            for h in range(2):
                src = c.D_skip.rearrange("(k h) -> h k", h=2)[h:h + 1, :]
                act.dma_start(dskip[h * HD:(h + 1) * HD, :], src.broadcast_to([HD, 2]),
                              allow_slow_non_contiguous=True).then_inc(cols_in, 16)
            act.wait_ge(se_var, 1)
            nc.scalar.activation(se_sd[:, :, :], se_v[:, :, :], ACT.Sqrt).then_inc(se_root, 1)
            for n, (src, rows, dst, how) in enumerate(jobs):
                if not by_act[n]:
                    continue
                act.wait_ge(tr_done, n + 1)
                if n == 1:
                    act.wait_ge(cols_in, 16 * 12)
                ps = tb[n % 8][:, 0:rows]
                if how == "norm":
                    nc.scalar.activation(dst, ps, ACT.Copy, scale=cols[:, 0:1]).then_inc(ev_act, 1)
                elif how == "half":
                    nc.scalar.activation(dst, ps, ACT.Copy, scale=0.5).then_inc(ev_act, 1)
                else:
                    nc.scalar.copy(dst, ps).then_inc(ev_act, 1)

        @block.gpsimd
        def _(pool):
            nc.gpsimd.memset(c.ident[:, :], 0.0).then_inc(masks_zero, 1)
            nc.gpsimd.memset(c.ones[:, :], 1.0).then_inc(masks_zero, 1)
            nc.gpsimd.memset(c.mask_blk[:, :, :], 1.0).then_inc(masks_zero, 1)
            pool.wait_ge(masks_zero, 3)
            nc.gpsimd.affine_select(out=c.ident[:, :], in_=c.ident[:, :], compare_op=ALU.not_equal, fill=1.0,
                                    base=0, pattern=[[-1, P]], channel_multiplier=1).then_inc(masks_ready, 1)
            nc.gpsimd.affine_select(out=c.upto[:, :], in_=c.ones[:, :], compare_op=ALU.is_ge, fill=0.0,
                                    base=0, pattern=[[1, P]], channel_multiplier=-1).then_inc(masks_ready, 1)
            nc.gpsimd.affine_select(out=c.after[:, :], in_=c.ones[:, :], compare_op=ALU.is_gt, fill=0.0,
                                    base=0, pattern=[[-1, P]], channel_multiplier=1).then_inc(masks_ready, 1)
            nc.gpsimd.affine_select(out=c.mask_blk[:, :, :], in_=c.mask_blk[:, :, :], compare_op=ALU.is_ge, fill=0.0,
                                    base=0, pattern=[[-AD, AH], [0, AE]], channel_multiplier=1).then_inc(masks_zero, 1)
            pool.wait_ge(masks_zero, 4)
            nc.gpsimd.affine_select(out=c.mask_blk[:, :, :], in_=c.mask_blk[:, :, :], compare_op=ALU.is_ge, fill=0.0,
                                    base=AD - 1, pattern=[[AD, AH], [0, AE]], channel_multiplier=-1).then_inc(masks_ready, 1)
            pool.wait_ge(masks_ready, 4)

        @block.vector
        def _(dve):
            dve.wait_ge(se_in, 16)
            for j in range(SB):
                last = nc.vector.bn_stats(se_st[:, j, :], se_nat[:, j, :])
            chain(dve, se_dve, last, 1)
            variance(nc, dve, se_st, se_half, se_mean[:, :], se_dve, 1)
            nc.vector.tensor_scalar(se_v[:, 0, :], se_half[:, 3, :], LN_EPS, None, ALU.add).then_inc(se_var, 1)
            dve.wait_ge(se_root, 1)
            chain(dve, se_dve, inverse_root(nc, dve, se_v[:, :, :], se_sd[:, :, :], se_y[:, :, :], se_t[:, :, :],
                                            [(se_scale[:, :], 0)], se_dve, 4), 8)
            for j in range(SB):
                nc.vector.tensor_scalar(se_nat[:, j, :], se_nat[:, j, :], se_mean[:, j:j + 1], se_scale[:, j:j + 1],
                                        ALU.subtract, ALU.mult).then_inc(se_scaled, 1)
            dve.wait_ge(cols_in, 16 * 12)
            nc.vector.tensor_scalar(cols[:, 4:6], cols[:, 1:3], cols[:, 3:4], None, ALU.mult).then_inc(se_dve, 1)
            dve.wait_ge(se_dve, 9)
            nc.vector.tensor_scalar(c.dcol[:, :], dskip[:, :], 0.5, None, ALU.mult)
            for m, (src, rows, dst, how) in enumerate(jobs):
                if by_act[m]:
                    continue
                dve.wait_ge(tr_done, m + 1)
                ps = tb[m % 8][:, 0:rows]
                if how == "slot":
                    nc.vector.tensor_scalar(dst, ps, cols[:, 4:5], cols[:, 5:6], ALU.mult, ALU.add).then_inc(ev_dve, 1)
                elif how == "norm":
                    nc.vector.tensor_scalar(dst, ps, cols[:, 0:1], None, ALU.mult).then_inc(ev_dve, 1)
                elif how == "half":
                    nc.vector.tensor_scalar(dst, ps, 0.5, None, ALU.mult).then_inc(ev_dve, 1)
                else:
                    nc.vector.tensor_copy(dst, ps).then_inc(ev_dve, 1)
            dve.wait_ge(x_in, 16 * BATCH)
            with dve.Fori(0, NT // 4) as r:
                for q in range(4):
                    t = bass.ds(4 * r + q, 1)
                    nc.vector.bn_stats(c.st[:, t, :], xf[:, t, :])
            dve.wait_ge(ev_dve, len(jobs) - sum(by_act))
            nc.vector.tensor_copy(c.seh[:, :], se32[:, :]).then_inc(se_hi, 1)
            dve.wait_ge(se_hi, 1)
            nc.vector.tensor_tensor(c.sel[:, :], se32[:, :], c.seh[:, :], ALU.subtract).then_inc(se_hi, 1)

        @block.tensor
        def _(pe):
            pe.wait_ge(masks_ready, 1)
            pe.wait_ge(w_in, 16 * 10)
            for n, (src, rows, dst, how) in enumerate(jobs):
                if n >= 8:
                    m = n - 8
                    pe.wait_ge(ev_act if by_act[m] else ev_dve,
                               sum(a == by_act[m] for a in by_act[:m + 1]))
                if how == "slot":
                    pe.wait_ge(se_scaled, n - first_se + 1)
                nc.tensor.transpose(tb[n % 8][:, 0:rows], src, c.ident[0:rows, 0:rows]).then_inc(tr_done, 1)



def variance(nc, dve, st, tmp, mean, sem, n):
    nc.vector.tensor_tensor(tmp[:, 0, :], st[:, :, 1], st[:, :, 4], ALU.add)
    nc.vector.tensor_tensor(tmp[:, 2, :], st[:, :, 2], st[:, :, 5], ALU.add)
    chain(dve, sem, nc.vector.tensor_tensor(tmp[:, 1, :], st[:, :, 1], st[:, :, 4], ALU.subtract), n + 1)
    nc.vector.tensor_scalar(mean, tmp[:, 0, :], 0.5, None, ALU.mult)
    chain(dve, sem, nc.vector.scalar_tensor_tensor(out=tmp[:, 1, :], in0=tmp[:, 1, :], scalar=0.25,
                                                   in1=tmp[:, 1, :], op0=ALU.mult, op1=ALU.mult), n + 2)
    chain(dve, sem, nc.vector.scalar_tensor_tensor(out=tmp[:, 3, :], in0=tmp[:, 2, :], scalar=1.0 / DM,
                                                   in1=tmp[:, 1, :], op0=ALU.mult, op1=ALU.add), n + 3)


def inverse_root(nc, dve, v, sd, y, t, outs, sem, n):
    chain(dve, sem, nc.vector.reciprocal(y, sd), n + 1)
    chain(dve, sem, nc.vector.tensor_tensor(t, y, y, ALU.mult), n + 2)
    chain(dve, sem, nc.vector.scalar_tensor_tensor(out=t, in0=t, scalar=-0.5, in1=v, op0=ALU.mult, op1=ALU.mult), n + 3)
    for out, k in outs:
        last = nc.vector.scalar_tensor_tensor(out=out, in0=t[:, k, :], scalar=1.5, in1=y[:, k, :],
                                              op0=ALU.add, op1=ALU.mult)
    return last
def row_scales(nc, c, name, norms):
    with ExitStack() as ctx:
        n = len(norms)
        half = ctx.enter_context(nc.sbuf_tensor(f"{name}_half", [P, 4, NT], F32))
        v, sd, y, t = (ctx.enter_context(nc.sbuf_tensor(f"{name}_{w}", [P, n, NT], F32)) for w in ("v", "sd", "y", "t"))
        step = nc.alloc_semaphore(f"{name}_dve_step")
        var_ready = nc.alloc_semaphore(f"{name}_var_ready")
        root_ready = nc.alloc_semaphore(f"{name}_root_ready")
        block = ctx.enter_context(nc.Block(no_gpsimd_drain=True))

        @block.vector
        def _(dve):
            variance(nc, dve, c.st, half, c.mean[:, :], step, 0)
            for k, (out, a, b) in enumerate(norms):
                last = nc.vector.tensor_scalar(v[:, k, :], half[:, 3, :], a, b, ALU.mult, ALU.add)
            last.then_inc(var_ready, 1)
            dve.wait_ge(root_ready, 1)
            inverse_root(nc, dve, v[:, :, :], sd[:, :, :], y[:, :, :], t[:, :, :],
                         [(out[:, :], k) for k, (out, a, b) in enumerate(norms)], step, 3)

        @block.scalar
        def _(act):
            act.wait_ge(var_ready, 1)
            nc.scalar.activation(sd[:, :, :], v[:, :, :], ACT.Sqrt).then_inc(root_ready, 1)


def moe_normalise(nc, c, name, xh, xT):
    with ExitStack() as ctx:
        def sem(what):
            return nc.alloc_semaphore(f"{name}_{what}")

        G = 4
        xn = ctx.enter_context(nc.sbuf_tensor(f"{name}_xn", [P, 2, G, DM], F32))
        xa = ctx.enter_context(nc.sbuf_tensor(f"{name}_xa", [P, 2, G * P], F32))
        ps = [ctx.enter_context(nc.psum_tensor(f"{name}_nps{i}", [P, G * P], F32)) for i in range(2)]
        xn_ready, xn_hi, xn_split = sem("xn_ready"), sem("xn_hi"), sem("xn_split")
        transposed, affine, xa_split = sem("transposed"), sem("affine"), sem("xa_split")
        xf = c.x[:, :, :, :].rearrange("p b t d -> p (b t) d")
        block = ctx.enter_context(nc.Block(no_gpsimd_drain=True))
        NG = NT // G

        @block.vector
        def _(dve):
            def normalise(g, pp):
                wait(dve, transposed, g - 1)
                wait(dve, xn_split, g - 1)
                for q in range(G):
                    t = bass.ds(g * G + q, 1)
                    last = nc.vector.tensor_scalar(xn[:, pp, q, :], xf[:, t, :], c.mean[:, t], c.s[:, t],
                                                   ALU.subtract, ALU.mult)
                last.then_inc(xn_ready, 1)

            def low(g, pp):
                dve.wait_ge(affine, g + 1)
                cols = bass.ds(g * (G * P), G * P)
                nc.vector.tensor_tensor(xT[:, 1, cols], xa[:, pp, :], xT[:, 0, cols], ALU.subtract).then_inc(xa_split, 1)

            normalise(0, 0)
            normalise(1, 1)
            low(0, 0)
            with dve.Fori(0, NG // 2 - 1) as r:
                g = 2 * r + 1
                for q in range(2):
                    normalise(g + q + 1, q % 2)
                    low(g + q, (q + 1) % 2)
            low(NG - 1, 1)

        @block.gpsimd
        def _(pool):
            def low(g, pp):
                pool.wait_ge(xn_hi, g + 1)
                t = bass.ds(g * G, G)
                nc.gpsimd.tensor_tensor(xh[:, t, 1, :], xn[:, pp, :, :], xh[:, t, 0, :], ALU.subtract)\
                    .then_inc(xn_split, 1)

            with pool.Fori(0, NG // 2) as r:
                g = 2 * r
                for q in range(2):
                    low(g + q, q)
            pool.wait_ge(xn_split, NG)

        @block.tensor
        def _(pe):
            def transpose(g, pp):
                pe.wait_ge(xn_ready, g + 1)
                wait(pe, affine, g - 1)
                for q in range(G):
                    last = nc.tensor.transpose(ps[pp][:, q * P:(q + 1) * P], xn[:, pp, q, :], c.ident[:, :])
                last.then_inc(transposed, 1)

            transpose(0, 0)
            transpose(1, 1)
            with pe.Fori(1, NG // 2) as r:
                g = 2 * r
                for q in range(2):
                    transpose(g + q, q)

        @block.scalar
        def _(act):
            def apply(g, pp):
                act.wait_ge(xn_ready, g + 1)
                nc.scalar.copy(xh[:, bass.ds(g * G, G), 0, :], xn[:, pp, :, :]).then_inc(xn_hi, 1)
                act.wait_ge(transposed, g + 1)
                wait(act, xa_split, g - 1)
                nc.scalar.activation(xa[:, pp, :], ps[pp][:, :], ACT.Identity, scale=c.gcol[:, 0:1],
                                     bias=c.bcol[:, 0:1])
                nc.scalar.activation(xT[:, 0, bass.ds(g * (G * P), G * P)], ps[pp][:, :], ACT.Identity,
                                     scale=c.gcol[:, 0:1], bias=c.bcol[:, 0:1]).then_inc(affine, 1)

            apply(0, 0)
            apply(1, 1)
            with act.Fori(1, NG // 2) as r:
                g = 2 * r
                for q in range(2):
                    apply(g + q, q)


def moe_dispatch(nc, c, name, xh, xT, sT):
    with ExitStack() as ctx:
        def sem(what):
            return nc.alloc_semaphore(f"{name}_{what}")

        NK = SEQ // 512
        RING = 4
        e32 = ctx.enter_context(nc.sbuf_tensor(f"{name}_e32", [P, 2, SEQ], F32))
        eh = ctx.enter_context(nc.sbuf_tensor(f"{name}_eh", [P, RING, 4, P], F16))
        el = ctx.enter_context(nc.sbuf_tensor(f"{name}_el", [P, RING, 4, P], F16))
        mx = ctx.enter_context(nc.sbuf_tensor(f"{name}_mx", [P, 2, NK], F32))
        nmx = ctx.enter_context(nc.sbuf_tensor(f"{name}_nmx", [P, 2], F32))
        sums = ctx.enter_context(nc.sbuf_tensor(f"{name}_sums", [P, 2, NK], F32))
        rs = ctx.enter_context(nc.sbuf_tensor(f"{name}_rs", [P, 2, 2], F32))
        part = ctx.enter_context(nc.sbuf_tensor(f"{name}_part", [P, P], F32))
        slots = ctx.enter_context(nc.sbuf_tensor(f"{name}_slots", [P, 2, P], F32))
        aff = ctx.enter_context(nc.sbuf_tensor(f"{name}_aff", [P, 2, P], F32))
        LB = [ctx.enter_context(nc.psum_tensor(f"{name}_L{i}", [P, 512], F32)) for i in range(NK)]
        TB = [ctx.enter_context(nc.psum_tensor(f"{name}_T{i}", [P, 4, P], F32)) for i in range(2)]
        SL = [ctx.enter_context(nc.psum_tensor(f"{name}_S{i}", [P, 512], F32)) for i in range(2)]
        logits, maxed, max_parts, exped = sem("logits"), sem("maxed"), sem("max_parts"), sem("exped")
        transposed, hi_ready, lo_ready, summed = sem("transposed"), sem("hi_ready"), sem("lo_ready"), sem("summed")
        total_ready, inverse_ready, part_ready = sem("total_ready"), sem("inverse_ready"), sem("part_ready")
        slots_ready = sem("slots_ready")
        slots_transposed, slots_out = sem("slots_transposed"), sem("slots_out")
        slots_low = sem("slots_low")
        block = ctx.enter_context(nc.Block(no_gpsimd_drain=True))
        STEPS = 2 * SB

        def step(r, q):
            return 2 * r + q, r + q // 2, q % 2

        @block.tensor
        def _(pe):
            def logit(r, q, banks=range(NK)):
                i, j, b = step(r, q)
                jj = bass.ds(j * P, P)
                for k in banks:
                    wait(pe, exped, 4 * i - 3 + k)
                    cols = slice(b * SEQ + k * 512, b * SEQ + (k + 1) * 512)
                    nc.tensor.matmul(LB[k][:, :], c.seh[:, jj], xT[:, 0, cols], start=True, stop=False)
                    nc.tensor.matmul(LB[k][:, :], c.seh[:, jj], xT[:, 1, cols], start=False, stop=False)
                    nc.tensor.matmul(LB[k][:, :], c.sel[:, jj], xT[:, 0, cols], start=False, stop=True)\
                        .then_inc(logits, 1)

            def transpose(r, q, g):
                i, j, b = step(r, q)
                pe.wait_ge(exped, 4 * i + g + 1)
                wait(pe, lo_ready, 4 * i + g - 1)
                for k in range(4):
                    col = (4 * g + k) * P
                    last = nc.tensor.transpose(TB[g % 2][:, k, :], e32[:, b, col:col + P], c.ident[:, :])
                last.then_inc(transposed, 1)

            def collect(r, q, g):
                i, j, b = step(r, q)
                pe.wait_ge(lo_ready, 4 * i + g + 1)
                if g == 0:
                    wait(pe, slots_out, i - 1)
                for k in range(4):
                    t = b * TILES + 4 * g + k
                    first, final = g == 0 and k == 0, g == NK - 1 and k == 3
                    nc.tensor.matmul(SL[b][:, 0:2 * P], eh[:, g, k, :],
                                     xh[:, t, :, :].rearrange("p h d -> p (h d)"),
                                     start=first, stop=False, skip_group_check=True)
                    last = nc.tensor.matmul(SL[b][:, 0:P], el[:, g, k, :], xh[:, t, 0, :],
                                            start=False, stop=final, skip_group_check=True)
                last.then_inc(summed, 1)

            def slot_transpose(r, q):
                i, j, b = step(r, q)
                pe.wait_ge(slots_ready, i + 1)
                nc.tensor.transpose(SL[b][:, 2 * P:3 * P], slots[:, b, :], c.ident[:, :]).then_inc(slots_transposed, 1)

            def body(r, q, first=False, final=False):
                def ahead(bank):
                    if not final:
                        logit(r, q + 1, [bank])

                for k in range(NK):
                    ahead(k)
                transpose(r, q, 0)
                transpose(r, q, 1)
                if not first:
                    collect(r, q - 1, 2)
                    collect(r, q - 1, 3)
                transpose(r, q, 2)
                collect(r, q, 0)
                if not first:
                    slot_transpose(r, q - 1)
                transpose(r, q, 3)
                collect(r, q, 1)

            logit(0, 0)
            body(0, 0, first=True)
            body(0, 1)
            body(0, 2)
            with pe.Fori(1, SB - 1) as r:
                body(r, 1)
                body(r, 2)
            body(SB - 1, 1, final=True)
            collect(SB - 1, 1, 2)
            collect(SB - 1, 1, 3)
            slot_transpose(SB - 1, 1)

        @block.vector
        def _(dve):
            def peak(r, q, k):
                i, j, b = step(r, q)
                dve.wait_ge(logits, 4 * i + k + 1)
                if k < NK - 1:
                    nc.vector.tensor_reduce(mx[:, b, k:k + 1], LB[k][:, :], AX.X, ALU.max)
                else:
                    chain(dve, max_parts, nc.vector.tensor_reduce(mx[:, b, k:k + 1], LB[k][:, :], AX.X, ALU.max), i + 1)
                    nc.vector.tensor_reduce(nmx[:, b:b + 1], mx[:, b, :], AX.X, ALU.max, negate=True).then_inc(maxed, 1)

            def low(r, q, g):
                i, j, b = step(r, q)
                dve.wait_ge(hi_ready, 4 * i + g + 1)
                nc.vector.tensor_tensor(el[:, g, :, :], TB[g % 2][:, :, :], eh[:, g, :, :], ALU.subtract)\
                    .then_inc(lo_ready, 1)

            def inverse(r, q):
                i, j, b = step(r, q)
                dve.wait_ge(exped, 4 * i + 4)
                chain(dve, total_ready, nc.vector.tensor_reduce(rs[:, b, 0:1], sums[:, b, :], AX.X, ALU.add), i + 1)
                chain(dve, inverse_ready, nc.vector.reciprocal(rs[:, b, 1:2], rs[:, b, 0:1]), i + 1)

            def normalise(r, q):
                i, j, b = step(r, q)
                dve.wait_ge(summed, 4 * i + 4)
                chain(dve, part_ready, nc.vector.tensor_scalar(part[:, :], SL[b][:, P:2 * P], rs[:, b, 1:2], None,
                                                               ALU.mult), i + 1)
                nc.vector.scalar_tensor_tensor(out=slots[:, b, :], in0=SL[b][:, 0:P], scalar=rs[:, b, 1:2],
                                               in1=part[:, :], op0=ALU.mult, op1=ALU.add).then_inc(slots_ready, 1)

            def body(r, q, first=False, final=False):
                def ahead(k):
                    if not final:
                        peak(r, q + 1, k)

                for k in range(NK):
                    ahead(k)
                inverse(r, q)
                low(r, q, 0)
                low(r, q, 1)
                if not first:
                    normalise(r, q - 1)
                low(r, q, 2)
                low(r, q, 3)

            for k in range(NK):
                peak(0, 0, k)
            body(0, 0, first=True)
            with dve.Fori(0, SB - 1) as r:
                body(r, 1)
                body(r, 2)
            body(SB - 1, 1, final=True)
            normalise(SB - 1, 1)

        @block.scalar
        def _(act):
            def exponential(r, q, k):
                i, j, b = step(r, q)
                if k == 0:
                    act.wait_ge(maxed, i + 1)
                    wait(act, transposed, 4 * i - 4)
                    wait(act, total_ready, i - 1)
                nc.scalar.activation(e32[:, b, k * 512:(k + 1) * 512], LB[k][:, :], ACT.Exp,
                                     bias=nmx[:, b:b + 1], accum_out=sums[:, b, k:k + 1]).then_inc(exped, 1)

            def high(r, q, g):
                i, j, b = step(r, q)
                act.wait_ge(transposed, 4 * i + g + 1)
                wait(act, summed, 4 * i + g - 3)
                nc.scalar.copy(eh[:, g, :, :], TB[g % 2][:, :, :]).then_inc(hi_ready, 1)

            def affine(r, q):
                i, j, b = step(r, q)
                act.wait_ge(slots_transposed, i + 1)
                wait(act, slots_low, i - 1)
                ps = SL[b][:, 2 * P:3 * P]
                nc.scalar.activation(aff[:, b, :], ps, ACT.Identity, scale=c.gcol[:, 0:1], bias=c.bcol[:, 0:1])
                nc.scalar.activation(sT[:, bass.ds(j, 1), 0, b, :], ps, ACT.Identity,
                                     scale=c.gcol[:, 0:1], bias=c.bcol[:, 0:1]).then_inc(slots_out, 1)

            def body(r, q, first=False, final=False):
                def ahead(k):
                    if not final:
                        exponential(r, q + 1, k)

                high(r, q, 0)
                high(r, q, 1)
                ahead(0)
                ahead(1)
                high(r, q, 2)
                ahead(2)
                high(r, q, 3)
                if not first:
                    affine(r, q - 1)
                ahead(3)

            for k in range(NK):
                exponential(0, 0, k)
            body(0, 0, first=True)
            body(0, 1)
            body(0, 2)
            with act.Fori(1, SB - 1) as r:
                body(r, 1)
                body(r, 2)
            body(SB - 1, 1, final=True)
            affine(SB - 1, 1)

        @block.gpsimd
        def _(pool):
            def low(r, q):
                i, j, b = step(r, q)
                pool.wait_ge(slots_out, i + 1)
                nc.gpsimd.tensor_tensor(sT[:, bass.ds(j, 1), 1, b, :], aff[:, b, :].unsqueeze(1),
                                        sT[:, bass.ds(j, 1), 0, b, :], ALU.subtract).then_inc(slots_low, 1)

            with pool.Fori(0, SB) as r:
                low(r, 0)
                low(r, 1)
            pool.wait_ge(slots_low, STEPS)


def moe_experts(nc, c, name, sT, eo):
    with ExitStack() as ctx:
        def sem(what):
            return nc.alloc_semaphore(f"{name}_{what}")

        def sb(what, shape, dt=F32):
            return ctx.enter_context(nc.sbuf_tensor(f"{name}_{what}", shape, dt))

        def pb(what):
            return ctx.enter_context(nc.psum_tensor(f"{name}_{what}", [P, 512], F32))

        FB = FF // P
        gate, hid = sb("gate", [P, 2, 2, FB, P]), sb("hid", [P, 2, 2, FB, P])
        hh, hl = sb("hh", [P, 2, 2, FB, P], F16), sb("hl", [P, 2, 2, FB, P], F16)
        oT = sb("oT", [P, 2, BATCH, P])
        HB = [[pb(f"H{pj}{e2}").ap().rearrange("p (w k s) -> p w k s", w=2, k=FB) for e2 in range(2)]
              for pj in range(2)]
        DB = [pb(f"D{pj}").ap()[:, 0:2 * P].rearrange("p (e s) -> p e s", e=2) for pj in range(2)]
        OB = [pb(f"O{pj}").ap()[:, 0:2 * P].rearrange("p (b o) -> p b o", b=BATCH) for pj in range(2)]
        up_done, gate_ready, hid_ready, down_done = sem("up_done"), sem("gate_ready"), sem("hid_ready"), sem("down_done")
        hid_hi, hid_lo, biased, out_transposed = sem("hid_hi"), sem("hid_lo"), sem("biased"), sem("out_transposed")
        out_hi, out_lo = sem("out_hi"), sem("out_lo")
        block = ctx.enter_context(nc.Block(no_gpsimd_drain=True))

        def periods(eng, body):
            body(-1, 1)
            body(0, 0)
            body(1, 1)
            body(2, 0)
            with eng.Fori(1, SB // 2 - 1) as r:
                body(2 * r + 1, 1)
                body(2 * r + 2, 0)
            body(SB - 1, 1)
            body(SB, 0)

        def exists(j, ahead):
            return not isinstance(j, int) or 0 <= j + ahead < SB

        @block.tensor
        def _(pe):
            def split_product(out, whole_w, whole_x, first, final):
                (wh, wl), (xh, xl) = whole_w, whole_x
                nc.tensor.matmul(out, wh, xh, start=first, stop=False)
                nc.tensor.matmul(out, wh, xl, start=False, stop=False)
                return nc.tensor.matmul(out, wl, xh, start=False, stop=final)

            def weights(e, col):
                return [w[:, bass.ds(e, 1), col:col + P].rearrange("p a m -> p (a m)") for w in (c.ewh, c.ewl)]

            def up(j, pj, e2):
                e = 2 * j + e2
                wait(pe, hid_ready, e - 3)
                rows = [sT[:, bass.ds(j, 1), half, :, e2 * SLOTS:(e2 + 1) * SLOTS] for half in range(2)]
                for which in range(2):
                    for k in range(FB):
                        last = split_product(HB[pj][e2][:, which, k, :], weights(e, which * FF + k * P), rows, True, True)
                last.then_inc(up_done, 1)

            def down(j, pj, e2):
                e = 2 * j + e2
                pe.wait_ge(hid_lo, e + 1)
                if e2 == 0:
                    wait(pe, biased, j - 1)
                for k in range(FB):
                    last = split_product(DB[pj][:, e2, :], weights(e, 2 * FF + k * P),
                                         (hh[:, pj, e2, k, :], hl[:, pj, e2, k, :]), k == 0, k == FB - 1)
                last.then_inc(down_done, 1)

            def to_slots(j, pj):
                pe.wait_ge(biased, j + 1)
                wait(pe, out_lo, j - 1)
                for b in range(BATCH):
                    last = nc.tensor.transpose(OB[pj][:, b, :], oT[:, pj, b, :], c.ident[:, :])
                last.then_inc(out_transposed, 1)

            def body(j, pj):
                if exists(j, 1):
                    up(j + 1, 1 - pj, 0)
                    up(j + 1, 1 - pj, 1)
                if exists(j, -1):
                    to_slots(j - 1, 1 - pj)
                if exists(j, 0):
                    down(j, pj, 0)
                    down(j, pj, 1)

            periods(pe, body)

        @block.scalar
        def _(act):
            def gelu(j, pj, e2):
                e = 2 * j + e2
                act.wait_ge(up_done, e + 1)
                wait(act, hid_ready, e - 3)
                for k in range(FB):
                    last = nc.scalar.activation(gate[:, pj, e2, k, :], HB[pj][e2][:, 0, k, :], ACT.Gelu,
                                                bias=c.bgT[:, k, bass.ds(e, 1)])
                last.then_inc(gate_ready, 1)

            def high(j, pj, e2):
                e = 2 * j + e2
                act.wait_ge(hid_ready, e + 1)
                wait(act, down_done, e - 3)
                nc.scalar.copy(hh[:, pj, e2, :, :], hid[:, pj, e2, :, :]).then_inc(hid_hi, 1)

            def out_high(j, pj):
                act.wait_ge(out_transposed, j + 1)
                nc.scalar.copy(eo[:, :, bass.ds(j, 1), 0, :], OB[pj][:, :, :]).then_inc(out_hi, 1)

            def body(j, pj):
                if exists(j, 1):
                    gelu(j + 1, 1 - pj, 0)
                    gelu(j + 1, 1 - pj, 1)
                if exists(j, -1):
                    out_high(j - 1, 1 - pj)
                if exists(j, 1):
                    high(j + 1, 1 - pj, 0)
                    high(j + 1, 1 - pj, 1)

            periods(act, body)

        @block.gpsimd
        def _(pool):
            def low(j, pj, e2):
                e = 2 * j + e2
                pool.wait_ge(hid_hi, e + 1)
                wait(pool, down_done, e - 3)
                nc.gpsimd.tensor_tensor(hl[:, pj, e2, :, :], hid[:, pj, e2, :, :], hh[:, pj, e2, :, :], ALU.subtract)\
                    .then_inc(hid_lo, 1)

            def body(j, pj):
                if exists(j, 1):
                    low(j + 1, 1 - pj, 0)
                    low(j + 1, 1 - pj, 1)

            periods(pool, body)
            pool.wait_ge(hid_lo, NE)

        @block.vector
        def _(dve):
            def hidden(j, pj, e2):
                e = 2 * j + e2
                dve.wait_ge(gate_ready, e + 1)
                wait(dve, hid_lo, e - 3)
                for k in range(FB):
                    last = nc.vector.scalar_tensor_tensor(out=hid[:, pj, e2, k, :], in0=HB[pj][e2][:, 1, k, :],
                                                          scalar=c.buT[:, k, bass.ds(e, 1)], in1=gate[:, pj, e2, k, :],
                                                          op0=ALU.add, op1=ALU.mult)
                last.then_inc(hid_ready, 1)

            def bias(j, pj):
                dve.wait_ge(down_done, 2 * j + 2)
                wait(dve, out_transposed, j - 1)
                by_expert = oT[:, pj, :, :].rearrange("p b (e s) -> p e b s", e=2)
                for e2 in range(2):
                    last = nc.vector.tensor_scalar(by_expert[:, e2, :, :], DB[pj][:, e2, :]
                                                   .rearrange("p (b s) -> p b s", b=BATCH),
                                                   c.bdT[:, bass.ds(2 * j + e2, 1)], None, ALU.add)
                last.then_inc(biased, 1)

            def out_low(j, pj):
                dve.wait_ge(out_hi, j + 1)
                nc.vector.tensor_tensor(eo[:, :, bass.ds(j, 1), 1, :].rearrange("p b a o -> p (b a) o"), OB[pj][:, :, :],
                                        eo[:, :, bass.ds(j, 1), 0, :].rearrange("p b a o -> p (b a) o"), ALU.subtract)\
                    .then_inc(out_lo, 1)

            def body(j, pj):
                if exists(j, 1):
                    hidden(j + 1, 1 - pj, 0)
                    hidden(j + 1, 1 - pj, 1)
                if exists(j, -1):
                    out_low(j - 1, 1 - pj)
                if exists(j, 0):
                    bias(j, pj)

            periods(dve, body)


def moe_combine(nc, c, name, xT, eo, store):
    with ExitStack() as ctx:
        def sem(what):
            return nc.alloc_semaphore(f"{name}_{what}")

        NK = NS // 512
        e32 = ctx.enter_context(nc.sbuf_tensor(f"{name}_e32", [P, 2, NS], F32))
        eh = ctx.enter_context(nc.sbuf_tensor(f"{name}_eh", [P, 2, SB, P], F16))
        el = ctx.enter_context(nc.sbuf_tensor(f"{name}_el", [P, 2, SB, P], F16))
        nmx = ctx.enter_context(nc.sbuf_tensor(f"{name}_nmx", [P, 2], F32))
        rs = ctx.enter_context(nc.sbuf_tensor(f"{name}_rs", [P, 2, 2], F32))
        part = ctx.enter_context(nc.sbuf_tensor(f"{name}_part", [P, P], F32))
        LB = [ctx.enter_context(nc.psum_tensor(f"{name}_L{i}", [P, NS], F32)) for i in range(2)]
        TB = [ctx.enter_context(nc.psum_tensor(f"{name}_T{i}", [P, 4, P], F32)) for i in range(2)]
        OB = [ctx.enter_context(nc.psum_tensor(f"{name}_O{i}", [P, 512], F32)) for i in range(2)]
        logits, maxed, exped, transposed = sem("logits"), sem("maxed"), sem("exped"), sem("transposed")
        hi_ready, lo_ready, summed = sem("hi_ready"), sem("lo_ready"), sem("summed")
        inverse_ready, part_ready, x_ready, stored = sem("inverse_ready"), sem("part_ready"), sem("x_ready"), sem("stored")
        block = ctx.enter_context(nc.Block())
        STEPS = 2 * TILES

        def step(r, q):
            return 2 * r + q, r + q // 2, q % 2

        @block.tensor
        def _(pe):
            def logit(r, q):
                i, t, b = step(r, q)
                wait(pe, exped, i - 1)
                tok = bass.ds(b * SEQ + t * P, P)
                for k in range(NK):
                    out, sl = LB[b][:, k * 512:(k + 1) * 512], slice(k * 512, (k + 1) * 512)
                    nc.tensor.matmul(out, xT[:, 0, tok], c.seh[:, sl], start=True, stop=False)
                    nc.tensor.matmul(out, xT[:, 0, tok], c.sel[:, sl], start=False, stop=False)
                    last = nc.tensor.matmul(out, xT[:, 1, tok], c.seh[:, sl], start=False, stop=True)
                last.then_inc(logits, 1)

            def transpose(r, q):
                i, t, b = step(r, q)
                pe.wait_ge(exped, i + 1)
                for g in range(2):
                    wait(pe, lo_ready, 2 * i + g - 1)
                    for k in range(4):
                        col = (4 * g + k) * P
                        last = nc.tensor.transpose(TB[g][:, k, :], e32[:, b, col:col + P], c.ident[:, :])
                    last.then_inc(transposed, 1)

            def collect(r, q):
                i, t, b = step(r, q)
                wait(pe, x_ready, i - 1)
                for k in range(SB):
                    if k % 4 == 0:
                        pe.wait_ge(lo_ready, 2 * i + k // 4 + 1)
                    nc.tensor.matmul(OB[b][:, 0:2 * P], eh[:, b, k, :], eo[:, b, k, :, :].rearrange("p h d -> p (h d)"),
                                     start=(k == 0), stop=False, skip_group_check=True)
                    last = nc.tensor.matmul(OB[b][:, 0:P], el[:, b, k, :], eo[:, b, k, 0, :],
                                            start=False, stop=(k == SB - 1), skip_group_check=True)
                last.then_inc(summed, 1)

            def body(r, q, first=False, final=False):
                if not final:
                    logit(r, q + 1)
                transpose(r, q)
                if not first:
                    collect(r, q - 1)

            logit(0, 0)
            body(0, 0, first=True)
            body(0, 1)
            body(0, 2)
            with pe.Fori(1, TILES - 1) as r:
                body(r, 1)
                body(r, 2)
            body(TILES - 1, 1, final=True)
            collect(TILES - 1, 1)

        @block.vector
        def _(dve):
            def peak(r, q):
                i, t, b = step(r, q)
                dve.wait_ge(logits, i + 1)
                nc.vector.tensor_reduce(nmx[:, b:b + 1], LB[b][:, :], AX.X, ALU.max, negate=True).then_inc(maxed, 1)

            def low(r, q, g):
                i, t, b = step(r, q)
                dve.wait_ge(hi_ready, 2 * i + g + 1)
                sl = slice(4 * g, 4 * g + 4)
                nc.vector.tensor_tensor(el[:, b, sl, :], TB[g][:, :, :], eh[:, b, sl, :], ALU.subtract)\
                    .then_inc(lo_ready, 1)

            def add(r, q):
                i, t, b = step(r, q)
                chain(dve, inverse_ready, nc.vector.reciprocal(rs[:, b, 1:2], rs[:, b, 0:1]), i + 1)
                dve.wait_ge(summed, i + 1)
                xt = c.x[:, b, bass.ds(t, 1), :]
                chain(dve, part_ready, nc.vector.scalar_tensor_tensor(
                    out=part[:, :], in0=OB[b][:, P:2 * P], scalar=rs[:, b, 1:2], in1=xt,
                    op0=ALU.mult, op1=ALU.add), i + 1)
                nc.vector.scalar_tensor_tensor(out=xt, in0=OB[b][:, 0:P], scalar=rs[:, b, 1:2], in1=part[:, :],
                                               op0=ALU.mult, op1=ALU.add).then_inc(x_ready, 1)

            def stats(r, q):
                i, t, b = step(r, q)
                dve.wait_ge(x_ready, i + 1)
                nc.vector.bn_stats(c.st[:, bass.ds(b * TILES + t, 1), :], c.x[:, b, bass.ds(t, 1), :])

            def body(r, q, first=False, final=False):
                if not final:
                    peak(r, q + 1)
                low(r, q, 0)
                low(r, q, 1)
                if not first:
                    add(r, q - 1)
                    if not store:
                        stats(r, q - 1)

            peak(0, 0)
            body(0, 0, first=True)
            with dve.Fori(0, TILES - 1) as r:
                body(r, 1)
                body(r, 2)
            body(TILES - 1, 1, final=True)
            add(TILES - 1, 1)
            if not store:
                stats(TILES - 1, 1)

        @block.scalar
        def _(act):
            def exponential(r, q):
                i, t, b = step(r, q)
                act.wait_ge(maxed, i + 1)
                wait(act, transposed, 2 * i - 2)
                wait(act, inverse_ready, i - 1)
                nc.scalar.activation(e32[:, b, :], LB[b][:, :], ACT.Exp, bias=nmx[:, b:b + 1],
                                     accum_out=rs[:, b, 0:1]).then_inc(exped, 1)

            def high(r, q, g):
                i, t, b = step(r, q)
                act.wait_ge(transposed, 2 * i + g + 1)
                wait(act, summed, i - 1)
                nc.scalar.copy(eh[:, b, 4 * g:4 * g + 4, :], TB[g][:, :, :]).then_inc(hi_ready, 1)

            def body(r, q, final=False):
                high(r, q, 0)
                high(r, q, 1)
                if not final:
                    exponential(r, q + 1)

            exponential(0, 0)
            body(0, 0)
            body(0, 1)
            body(0, 2)
            with act.Fori(1, TILES - 1) as r:
                body(r, 1)
                body(r, 2)
            body(TILES - 1, 1, final=True)

        if store:
            @block.sync
            def _(sp):
                def save(r, q):
                    i, t, b = step(r, q)
                    sp.wait_ge(x_ready, i + 1)
                    dst = c.out_dram[b].rearrange("(t p) d -> p t d", p=P)
                    sp.dma_start(dst[:, bass.ds(t, 1), :], c.x[:, b, bass.ds(t, 1), :]).then_inc(stored, 16)

                with sp.Fori(0, TILES) as r:
                    save(r, 0)
                    save(r, 1)
                sp.wait_ge(stored, 16 * STEPS)


def save_x(nc, c):
    with ExitStack() as ctx:
        stored = nc.alloc_semaphore("x_stored")
        block = ctx.enter_context(nc.Block())

        @block.sync
        def _(sp):
            for b in range(BATCH):
                sp.dma_start(c.out_dram[b].rearrange("(t p) d -> p t d", p=P), c.x[:, b, :, :]).then_inc(stored, 16)
            sp.wait_ge(stored, 16 * BATCH)


def moe(nc, c, name, store=False):
    row_scales(nc, c, f"{name}_rows", [(c.s, 1 + LN_EPS, LN_EPS * LN_EPS)])
    with ExitStack() as ctx:
        xT = ctx.enter_context(nc.sbuf_tensor(f"{name}_xT", [P, 2, BATCH * SEQ], F16))
        sT = ctx.enter_context(nc.sbuf_tensor(f"{name}_sT", [P, SB, 2, BATCH, P], F16))
        eo = ctx.enter_context(nc.sbuf_tensor(f"{name}_eo", [P, BATCH, SB, 2, DM], F16))
        with ExitStack() as tokens:
            xh = tokens.enter_context(nc.sbuf_tensor(f"{name}_xh", [P, NT, 2, DM], F16))
            moe_normalise(nc, c, f"{name}_norm", xh, xT)
            moe_dispatch(nc, c, f"{name}_disp", xh, xT, sT)
        moe_experts(nc, c, f"{name}_exp", sT, eo)
        moe_combine(nc, c, f"{name}_comb", xT, eo, store)


def ssm_inputs(nc, c, name, xT, dt_half, a, ecum, etot):
    with ExitStack() as ctx:
        def sem(what):
            return nc.alloc_semaphore(f"{name}_{what}")

        def sb(what, shape):
            return ctx.enter_context(nc.sbuf_tensor(f"{name}_{what}", shape, F32))

        G, NG = 4, NT // 4
        xn, xl, xa = sb("xn", [P, 2, G, DM]), sb("xl", [P, 2, G, DM]), sb("xa", [P, 2, G * P])
        raw, neg, ex, up, lg, rc = (sb(n, [P, NT, NH]) for n in ("raw", "neg", "ex", "up", "lg", "rc"))
        ea = sb("ea", [P, NH])
        ps = [ctx.enter_context(nc.psum_tensor(f"{name}_ps{i}", [P, G * P], F32)) for i in range(2)]
        DT = ctx.enter_context(nc.psum_tensor(f"{name}_DT", [P, 512], F32))
        CU = ctx.enter_context(nc.psum_tensor(f"{name}_CU", [P, 512], F32))
        xn_ready, xl_ready, x_added, transposed = sem("xn_ready"), sem("xl_ready"), sem("x_added"), sem("transposed")
        xa_ready, xT_ready, dt_done = sem("xa_ready"), sem("xT_ready"), sem("dt_done")
        dve_step, neg_ready, act_step, a_ready, sums_done = (
            sem("dve_step"), sem("neg_ready"), sem("act_step"), sem("a_ready"), sem("sums_done"))
        xf = c.x[:, :, :, :].rearrange("p b t d -> p (b t) d")
        dts = DT[:, 0:NT * NH].rearrange("p (t h) -> p t h", h=NH)
        block = ctx.enter_context(nc.Block(no_gpsimd_drain=True))

        @block.vector
        def _(dve):
            def normalise(g, pp):
                wait(dve, transposed, g - 1)
                wait(dve, x_added, g - 1)
                for q in range(G):
                    t = bass.ds(g * G + q, 1)
                    last = nc.vector.tensor_scalar(xn[:, pp, q, :], xf[:, t, :], c.mean[:, t], c.s[:, t],
                                                   ALU.subtract, ALU.mult)
                last.then_inc(xn_ready, 1)
                for q in range(G):
                    t = bass.ds(g * G + q, 1)
                    last = nc.vector.tensor_scalar(xl[:, pp, q, :], xf[:, t, :], c.mean[:, t], c.r1[:, t],
                                                   ALU.subtract, ALU.mult)
                last.then_inc(xl_ready, 1)

            def keep(g, pp):
                dve.wait_ge(xa_ready, g + 1)
                nc.vector.tensor_copy(xT[:, bass.ds(g * (G * P), G * P)], xa[:, pp, :]).then_inc(xT_ready, 1)

            normalise(0, 0)
            normalise(1, 1)
            keep(0, 0)
            with dve.Fori(0, NG // 2 - 1) as r:
                g = 2 * r + 1
                for q in range(2):
                    normalise(g + q + 1, q % 2)
                    keep(g + q, (q + 1) % 2)
            keep(NG - 1, 1)
            dve.wait_ge(dt_done, NG)
            bias = c.dtb[:, :].unsqueeze(1).broadcast_to([P, NT, NH])
            chain(dve, dve_step, nc.vector.tensor_tensor(raw[:, :, :], dts, bias, ALU.add), 1)
            nc.vector.scalar_tensor_tensor(out=neg[:, :, :], in0=raw[:, :, :], scalar=-1.0, in1=raw[:, :, :],
                                           op0=ALU.mult, op1=ALU.min).then_inc(neg_ready, 1)
            dve.wait_ge(act_step, 2)
            chain(dve, dve_step, nc.vector.tensor_scalar(up[:, :, :], ex[:, :, :], 1.0, None, ALU.add), 2)
            nc.vector.reciprocal(rc[:, :, :], up[:, :, :]).then_inc(neg_ready, 1)
            chain(dve, dve_step, nc.vector.tensor_scalar(neg[:, :, :], up[:, :, :], -1.0, None, ALU.add), 3)
            chain(dve, dve_step, nc.vector.tensor_tensor(ex[:, :, :], ex[:, :, :], neg[:, :, :], ALU.subtract), 4)
            chain(dve, dve_step, nc.vector.tensor_tensor(ex[:, :, :], ex[:, :, :], rc[:, :, :], ALU.mult), 5)
            dve.wait_ge(act_step, 3)
            chain(dve, dve_step, nc.vector.tensor_tensor(lg[:, :, :], lg[:, :, :], ex[:, :, :], ALU.add), 6)
            chain(dve, dve_step, nc.vector.scalar_tensor_tensor(out=raw[:, :, :], in0=raw[:, :, :], scalar=0.0,
                                                                in1=lg[:, :, :], op0=ALU.max, op1=ALU.add), 7)
            nc.vector.tensor_scalar(dt_half[:, :, :], raw[:, :, :], 0.5, None, ALU.mult)
            nc.vector.scalar_tensor_tensor(out=a[:, :, :], in0=raw[:, :, :], scalar=-1.0,
                                           in1=ea[:, :].unsqueeze(1).broadcast_to([P, NT, NH]),
                                           op0=ALU.mult, op1=ALU.mult).then_inc(a_ready, 1)

        @block.gpsimd
        def _(pool):
            def add(g, pp):
                pool.wait_ge(xl_ready, g + 1)
                t = bass.ds(g * G, G)
                nc.gpsimd.tensor_tensor(xf[:, t, :], xf[:, t, :], xl[:, pp, :, :], ALU.add).then_inc(x_added, 1)

            with pool.Fori(0, NG // 2) as r:
                add(2 * r, 0)
                add(2 * r + 1, 1)
            pool.wait_ge(x_added, NG)

        @block.tensor
        def _(pe):
            def transpose(g, pp):
                pe.wait_ge(xn_ready, g + 1)
                wait(pe, xa_ready, g - 1)
                for q in range(G):
                    last = nc.tensor.transpose(ps[pp][:, q * P:(q + 1) * P], xn[:, pp, q, :], c.ident[:, :])
                last.then_inc(transposed, 1)

            def project(g, pp):
                pe.wait_ge(xa_ready, g + 1)
                for q in range(G):
                    last = nc.tensor.matmul(DT[:, bass.ds((g * G + q) * NH, NH)], xa[:, pp, q * P:(q + 1) * P],
                                            c.wpT[:, PROJ:PROJ + NH], start=True, stop=True)
                last.then_inc(dt_done, 1)

            transpose(0, 0)
            transpose(1, 1)
            with pe.Fori(1, NG // 2) as r:
                for q in range(2):
                    project(2 * r + q - 2, q)
                    transpose(2 * r + q, q)
            project(NG - 2, 0)
            project(NG - 1, 1)
            pe.wait_ge(a_ready, 1)
            av = a[:, :, :].rearrange("p t h -> p (t h)")
            nc.tensor.matmul(CU[:, 0:P], c.upto[:, :], av, start=True, stop=True)
            nc.tensor.matmul(CU[:, P:2 * P], c.ones[:, :], av, start=True, stop=True).then_inc(sums_done, 1)

        @block.scalar
        def _(act):
            def evacuate(g, pp):
                act.wait_ge(transposed, g + 1)
                wait(act, xT_ready, g - 1)
                wait(act, dt_done, g - 1)
                nc.scalar.copy(xa[:, pp, :], ps[pp][:, :]).then_inc(xa_ready, 1)

            evacuate(0, 0)
            evacuate(1, 1)
            with act.Fori(1, NG // 2) as r:
                for q in range(2):
                    evacuate(2 * r + q, q)
            nc.scalar.activation(ea[:, :], c.alog[:, :], ACT.Exp).then_inc(act_step, 1)
            act.wait_ge(neg_ready, 1)
            nc.scalar.activation(ex[:, :, :], neg[:, :, :], ACT.Exp).then_inc(act_step, 1)
            act.wait_ge(neg_ready, 2)
            nc.scalar.activation(lg[:, :, :], up[:, :, :], ACT.Ln).then_inc(act_step, 1)
            act.wait_ge(sums_done, 1)
            nc.scalar.activation(ecum[:, :, :].rearrange("p t h -> p (t h)"), CU[:, 0:P], ACT.Exp)
            nc.scalar.activation(etot[:, :, :].rearrange("p t h -> p (t h)"), CU[:, P:2 * P], ACT.Exp)


def ssm_scan(nc, c, name, xT, dt_half, a, ecum, etot):
    with ExitStack() as ctx:
        def sem(what):
            return nc.alloc_semaphore(f"{name}_{what}")

        def sb(what, shape):
            return ctx.enter_context(nc.sbuf_tensor(f"{name}_{what}", shape, F32))

        HALO = TAPS - 1
        xs = sb("xs", [P, 2, 2, BATCH, HALO + P])
        bc = sb("bc", [P, 2, 2, BATCH, P])
        zt, zg = sb("zt", [P, 2, BATCH, P]), sb("zg", [P, 2, 2, BATCH, P])
        cv, th = sb("cv", [P, 2, BATCH, P]), sb("th", [P, 2, BATCH, P])
        xg = sb("xg", [P, 2, 2, BATCH, P])
        am, dd = sb("am", [P, BATCH, NH, P]), sb("dd", [P, BATCH, NH, P])
        gm, pr = sb("gm", [P, BATCH, P]), sb("pr", [P, BATCH, NH, P])
        xt, xw = sb("xt", [P, BATCH, NH, HD]), sb("xw", [P, BATCH, NH, HD])
        bt = sb("bt", [P, BATCH, P])
        st = sb("st", [P, BATCH, NH, HD])
        yo, y = sb("yo", [P, BATCH, NH, HD]), sb("y", [P, BATCH, CH])
        gd, gt = sb("gd", [P, 2, BATCH, P]), sb("gt", [P, 2, BATCH, P])
        ew = sb("ew", [P, 2, EW])

        def pb(what, shape):
            return ctx.enter_context(nc.psum_tensor(f"{name}_{what}", shape, F32))

        ZB, XB, CB = pb("ZB", [P, 2, BATCH, P]), pb("XB", [P, 2, BATCH, P]), pb("CB", [P, 2, BATCH, P])
        DB = [pb("DB0", [P, NH, P]), pb("DB1", [P, NH, P])]
        GB = pb("GB", [P, 512])
        TB = pb("TB", [P, 512])
        YB = pb("YB", [P, 512])
        x_proj, bc_proj, z_proj, decay_done = sem("x_proj"), sem("bc_proj"), sem("z_proj"), sem("decay_done")
        cb_done, xt_done, y_done, st_done = sem("cb_done"), sem("xt_done"), sem("y_done"), sem("st_done")
        yT_done, out_done = sem("yT_done"), sem("out_done")
        xs_ready, bc_ready, zt_ready, tap_ready = sem("xs_ready"), sem("bc_ready"), sem("zt_ready"), sem("tap_ready")
        th_ready, dd_ready, bt_ready = sem("th_ready"), sem("dd_ready"), sem("bt_ready")
        gm_ready, xt_ready, xw_ready, x_added = sem("gm_ready"), sem("xt_ready"), sem("xw_ready"), sem("x_added")
        tap_step, cv_ready, xg_ready, zg_ready = sem("tap_step"), sem("cv_ready"), sem("xg_ready"), sem("zg_ready")
        yo_ready, y_ready, st_step, st_ready = sem("yo_ready"), sem("y_ready"), sem("st_step"), sem("st_ready")
        gd_ready, gt_ready = sem("gd_ready"), sem("gt_ready")
        am_ready, pr_ready = sem("am_ready"), sem("pr_ready")
        zeroed = sem("zeroed")
        ew_in, ew_hi, ew_split = [sem("ew_in0"), sem("ew_in1")], sem("ew_hi"), sem("ew_split")
        K = TILES
        xTb = xT[:, :].rearrange("p (b l) -> p b l", b=BATCH)

        def of_tile(v, k):
            return v[:, :, :].rearrange("p (b t) h -> p b t h", b=BATCH)[:, :, bass.ds(k, 1), :]\
                .rearrange("p b a h -> p (b a) h")

        block = ctx.enter_context(nc.Block(no_gpsimd_drain=True))

        def periods(eng, body):
            body(0, 0, first=True)
            body(1, 1)
            with eng.Fori(1, K // 2 - 1) as r:
                body(2 * r, 0)
                body(2 * r + 1, 1)
            body(K - 2, 0)
            body(K - 1, 1, final=True)

        @block.tensor
        def _(pe):
            def project(k, pp):
                tok = xTb[:, :, bass.ds(k * P, P)]
                for bank, col, free, done in ((XB, CH, xs_ready, x_proj), (CB, 2 * CH, bc_ready, bc_proj),
                                              (ZB, 0, zg_ready, z_proj)):
                    wait(pe, free, k)
                    for n in range(2):
                        last = nc.tensor.matmul(bank[:, n, :, :], c.wpT[:, col + n * P:col + (n + 1) * P], tok,
                                                start=True, stop=True)
                    last.then_inc(done, 1)

            def decay(k):
                pe.wait_ge(am_ready, k + 1)
                wait(pe, dd_ready, k)
                for b in range(BATCH):
                    last = nc.tensor.matmul(DB[b][:, :, :], c.after[:, :], am[:, b, :, :], start=True, stop=True)
                last.then_inc(decay_done, 1)

            def products(k, pp):
                pe.wait_ge(bc_ready, k + 1)
                wait(pe, y_ready, k)
                for b in range(BATCH):
                    nc.tensor.matmul(GB[:, b * P:(b + 1) * P], bc[:, pp, 0, b, :], bc[:, pp, 1, b, :],
                                     start=True, stop=True)
                for b in range(BATCH):
                    last = nc.tensor.transpose(GB[:, (2 + b) * P:(3 + b) * P], bc[:, pp, 0, b, :], c.ident[:, :])
                last.then_inc(cb_done, 1)
                pe.wait_ge(xg_ready, k + 1)
                wait(pe, st_ready, k)
                for b in range(BATCH):
                    for n in range(2):
                        last = nc.tensor.transpose(TB[:, (2 * b + n) * P:(2 * b + n + 1) * P], xg[:, pp, n, b, :],
                                                   c.ident[:, :])
                last.then_inc(xt_done, 1)

            def outputs(k, pp):
                pe.wait_ge(pr_ready, k + 1)
                pe.wait_ge(xt_ready, k + 1)
                wait(pe, x_added, k)
                for b in range(BATCH):
                    for h in range(NH):
                        col = b * CH + h * HD
                        nc.tensor.matmul(YB[:, col:col + HD], pr[:, b, h, :], xt[:, b, h, :], start=True, stop=True)
                pe.wait_ge(bt_ready, k + 1)
                wait(pe, st_ready, k)
                pe.wait_ge(zeroed, 2)
                for b in range(BATCH):
                    last = nc.tensor.matmul(GB[:, b * CH:(b + 1) * CH], bc[:, pp, 1, b, :], st[:, b, :, :],
                                            start=True, stop=True)
                last.then_inc(y_done, 1)
                pe.wait_ge(xw_ready, k + 1)
                for b in range(BATCH):
                    last = nc.tensor.matmul(TB[:, b * CH:(b + 1) * CH], bt[:, b, :], xw[:, b, :, :],
                                            start=True, stop=True)
                last.then_inc(st_done, 1)

            def y_transpose(k):
                pe.wait_ge(y_ready, k + 1)
                for n in range(2):
                    for b in range(BATCH):
                        last = nc.tensor.transpose(YB[:, (2 * n + b) * P:(2 * n + b + 1) * P],
                                                   y[:, b, n * P:(n + 1) * P], c.ident[:, :])
                last.then_inc(yT_done, 1)

            def project_out(k):
                pe.wait_ge(gt_ready, k + 1)
                for b in range(BATCH):
                    for n in range(2):
                        last = nc.tensor.matmul(YB[:, b * P:(b + 1) * P], gt[:, n, b, :], c.woutT[:, n, :],
                                                start=(n == 0), stop=(n == 1))
                last.then_inc(out_done, 1)

            def body(k, pp, first=False, final=False):
                products(k, pp)
                if not first:
                    project_out(k - 1)
                if not final:
                    project(k + 1, 1 - pp)
                outputs(k, pp)
                if not final:
                    decay(k + 1)
                y_transpose(k)

            project(0, 0)
            decay(0)
            periods(pe, body)
            project_out(K - 1)

        @block.scalar
        def _(act):
            def ahead(k, pp):
                act.wait_ge(x_proj, k + 1)
                wait(act, cv_ready, k - 1)
                if isinstance(k, int) and k == 0:
                    act.wait_ge(zeroed, 2)
                else:
                    nc.scalar.copy(xs[:, pp, :, :, 0:HALO], xs[:, 1 - pp, :, :, P:P + HALO])
                chain(act, xs_ready, nc.scalar.copy(xs[:, pp, :, :, HALO:HALO + P], XB[:, :, :, :]), k + 1)
                wait(act, xg_ready, k)
                for n in range(2):
                    last = nc.scalar.activation(cv[:, n, :, :], xs[:, pp, n, :, 0:P], ACT.Identity,
                                                scale=c.convw[:, n, 0:1], bias=c.convb[:, n:n + 1])
                last.then_inc(tap_ready, 1)
                act.wait_ge(bc_proj, k + 1)
                wait(act, y_done, k - 1)
                nc.scalar.copy(bc[:, pp, :, :, :], CB[:, :, :, :]).then_inc(bc_ready, 1)
                act.wait_ge(z_proj, k + 1)
                nc.scalar.activation(zt[:, :, :, :], ZB[:, :, :, :], ACT.Tanh, scale=0.5).then_inc(zt_ready, 1)
                act.wait_ge(cv_ready, k + 1)
                nc.scalar.activation(th[:, :, :, :], cv[:, :, :, :], ACT.Tanh, scale=0.5).then_inc(th_ready, 1)
                act.wait_ge(decay_done, k + 1)
                wait(act, pr_ready, k)
                wait(act, xw_ready, k)
                for b in range(BATCH):
                    last = nc.scalar.activation(dd[:, b, :, :], DB[b][:, :, :], ACT.Exp)
                last.then_inc(dd_ready, 1)

            def body(k, pp, first=False, final=False):
                act.wait_ge(gm_ready, k + 1)
                wait(act, st_done, k)
                nc.scalar.copy(bt[:, :, :].rearrange("p b n -> p (b n)"), GB[:, 2 * P:4 * P]).then_inc(bt_ready, 1)
                if not final:
                    ahead(k + 1, 1 - pp)

            ahead(0, 0)
            periods(act, body)

        @block.gpsimd
        def _(pool):
            def decays(k):
                wait(pool, decay_done, k)
                at = of_tile(a, k).unsqueeze(3).broadcast_to([P, BATCH, NH, P])
                upto = c.upto[:, :].unsqueeze(1).unsqueeze(1).broadcast_to([P, BATCH, NH, P])
                nc.gpsimd.tensor_tensor(am[:, :, :, :], upto, at, ALU.mult).then_inc(am_ready, 1)

            def masked(k):
                pool.wait_ge(dd_ready, k + 1)
                pool.wait_ge(gm_ready, k + 1)
                wait(pool, y_done, k)
                nc.gpsimd.tensor_tensor(pr[:, :, :, :], dd[:, :, :, :],
                                        gm[:, :, :].unsqueeze(2).broadcast_to([P, BATCH, NH, P]), ALU.mult)\
                    .then_inc(pr_ready, 1)

            def split_weights(e, pp):
                pool.wait_ge(ew_in[pp], 24 * (e - pp) + 48)
                ones = c.ones[:, :].unsqueeze(1).broadcast_to([P, EW // P, P])
                hi = c.ewh[:, bass.ds(e, 1), :].rearrange("p a (k m) -> p (a k) m", m=P)
                lo = c.ewl[:, bass.ds(e, 1), :].rearrange("p a (k m) -> p (a k) m", m=P)
                w = ew[:, pp, :].rearrange("p (k m) -> p k m", m=P)
                nc.gpsimd.tensor_tensor(hi, w, ones, ALU.mult).then_inc(ew_hi, 1)
                pool.wait_ge(ew_hi, e + 1)
                nc.gpsimd.tensor_tensor(lo, w, hi, ALU.subtract).then_inc(ew_split, 1)

            def body(k, pp, first=False, final=False):
                masked(k)
                if not final:
                    decays(k + 1)
                split_weights(k, pp)

            nc.gpsimd.memset(xs[:, 0, :, :, 0:HALO], 0.0).then_inc(zeroed, 1)
            nc.gpsimd.memset(st[:, :, :, :], 0.0).then_inc(zeroed, 1)
            decays(0)
            periods(pool, body)
            pool.wait_ge(pr_ready, K)
            pool.wait_ge(ew_split, NE)

        @block.sync
        def _(sp):
            def load(e, pp):
                wait(sp, ew_split, e - 1)
                ee = bass.ds(e, 1)
                gate, up, down = (ew[:, pp, k * FF:(k + 1) * FF] for k in range(3))
                sp.dma_start(gate, c.Wg[ee, :, :].rearrange("a d f -> d (a f)")).then_inc(ew_in[pp], 16)
                sp.dma_start(up, c.Wu[ee, :, :].rearrange("a d f -> d (a f)")).then_inc(ew_in[pp], 16)
                sp.dma_start(down.rearrange("p (k o) -> p k o", o=DM),
                             c.Wd[ee, :, :].rearrange("a (k p) o -> p (a k) o", p=P)).then_inc(ew_in[pp], 16)

            load(0, 0)
            load(1, 1)
            with sp.Fori(1, NE // 2) as r:
                load(2 * r, 0)
                load(2 * r + 1, 1)

        @block.vector
        def _(dve):
            def inside(k, pp):
                dve.wait_ge(cb_done, k + 1)
                wait(dve, pr_ready, k)
                nc.vector.tensor_tensor(gm[:, :, :], GB[:, 0:BATCH * P].rearrange("p (b t) -> p b t", b=BATCH),
                                        c.upto[:, :].unsqueeze(1).broadcast_to([P, BATCH, P]), ALU.mult)\
                    .then_inc(gm_ready, 1)
                dve.wait_ge(xt_done, k + 1)
                wait(dve, y_done, k)
                chain(dve, xt_ready, nc.vector.tensor_tensor(
                    xt[:, :, :, :], TB[:, :].rearrange("p (b h e) -> p b h e", b=BATCH, h=NH),
                    of_tile(dt_half, k).unsqueeze(3).broadcast_to([P, BATCH, NH, HD]), ALU.mult), k + 1)
                dve.wait_ge(dd_ready, k + 1)
                wait(dve, st_done, k)
                nc.vector.tensor_tensor(xw[:, :, :, :], xt[:, :, :, :],
                                        dd[:, :, :, P - 1:P].broadcast_to([P, BATCH, NH, HD]), ALU.mult)\
                    .then_inc(xw_ready, 1)

            def residual(k):
                dve.wait_ge(out_done, k + 1)
                xk = c.x[:, :, bass.ds(k, 1), :].rearrange("p b a d -> p (b a) d")
                nc.vector.tensor_tensor(xk, YB[:, 0:BATCH * P].rearrange("p (b d) -> p b d", b=BATCH), xk, ALU.add)\
                    .then_inc(x_added, 1)

            def stats(k):
                dve.wait_ge(x_added, k + 1)
                for b in range(BATCH):
                    nc.vector.bn_stats(c.st[:, bass.ds(b * TILES + k, 1), :], c.x[:, b, bass.ds(k, 1), :])

            def ahead(k, pp):
                dve.wait_ge(tap_ready, k + 1)
                for tap in range(1, TAPS):
                    for n in range(2):
                        last = nc.vector.scalar_tensor_tensor(
                            out=cv[:, n, :, :], in0=xs[:, pp, n, :, tap:tap + P], scalar=c.convw[:, n, tap:tap + 1],
                            in1=cv[:, n, :, :], op0=ALU.mult, op1=ALU.add)
                    if tap < TAPS - 1:
                        chain(dve, tap_step, last, (TAPS - 2) * k + tap)
                last.then_inc(cv_ready, 1)
                dve.wait_ge(zt_ready, k + 1)
                nc.vector.scalar_tensor_tensor(out=zg[:, pp, :, :, :].rearrange("p n b t -> p (n b t)"),
                                               in0=zt[:, :, :, :].rearrange("p n b t -> p (n b t)"), scalar=1.0,
                                               in1=ZB[:, :, :, :].rearrange("p n b t -> p (n b t)"),
                                               op0=ALU.add, op1=ALU.mult).then_inc(zg_ready, 1)
                dve.wait_ge(th_ready, k + 1)
                wait(dve, xt_done, k - 1)
                nc.vector.scalar_tensor_tensor(out=xg[:, pp, :, :, :].rearrange("p n b t -> p (n b t)"),
                                               in0=th[:, :, :, :].rearrange("p n b t -> p (n b t)"), scalar=1.0,
                                               in1=cv[:, :, :, :].rearrange("p n b t -> p (n b t)"),
                                               op0=ALU.add, op1=ALU.mult).then_inc(xg_ready, 1)

            def combine(k, pp):
                dve.wait_ge(y_done, k + 1)
                wait(dve, yT_done, k)
                chain(dve, yo_ready, nc.vector.tensor_tensor(
                    yo[:, :, :, :], GB[:, :].rearrange("p (b h e) -> p b h e", b=BATCH, h=NH),
                    of_tile(ecum, k).unsqueeze(3).broadcast_to([P, BATCH, NH, HD]), ALU.mult), k + 1)
                nc.vector.tensor_tensor(y[:, :, :].rearrange("p b e -> p (b e)"), YB[:, :],
                                        yo[:, :, :, :].rearrange("p b h e -> p (b h e)"), ALU.add).then_inc(y_ready, 1)
                chain(dve, st_step, nc.vector.tensor_tensor(
                    st[:, :, :, :], st[:, :, :, :],
                    of_tile(etot, k).unsqueeze(3).broadcast_to([P, BATCH, NH, HD]), ALU.mult), k + 1)
                dve.wait_ge(st_done, k + 1)
                nc.vector.tensor_tensor(st[:, :, :, :].rearrange("p b h e -> p (b h e)"),
                                        st[:, :, :, :].rearrange("p b h e -> p (b h e)"), TB[:, :], ALU.add)\
                    .then_inc(st_ready, 1)
                dve.wait_ge(yT_done, k + 1)
                for n in range(2):
                    last = nc.vector.scalar_tensor_tensor(
                        out=gd[:, n, :, :].rearrange("p b t -> p (b t)"),
                        in0=xg[:, pp, n, :, :].rearrange("p b t -> p (b t)"), scalar=c.dcol[:, n:n + 1],
                        in1=YB[:, n * BATCH * P:(n + 1) * BATCH * P], op0=ALU.mult, op1=ALU.add)
                chain(dve, gd_ready, last, k + 1)
                wait(dve, out_done, k)
                nc.vector.tensor_tensor(gt[:, :, :, :], gd[:, :, :, :], zg[:, pp, :, :, :], ALU.mult)\
                    .then_inc(gt_ready, 1)

            def body(k, pp, first=False, final=False):
                inside(k, pp)
                if not first:
                    residual(k - 1)
                if not final:
                    ahead(k + 1, 1 - pp)
                combine(k, pp)
                if not first:
                    stats(k - 1)

            dve.wait_ge(zeroed, 2)
            ahead(0, 0)
            periods(dve, body)
            residual(K - 1)
            stats(K - 1)


def ssm(nc, c):
    row_scales(nc, c, "ssm_rows", [(c.r1, 1.0, LN_EPS), (c.s, 1 + RMS_EPS, LN_EPS * RMS_EPS)])
    with ExitStack() as ctx:
        def sb(what, shape):
            return ctx.enter_context(nc.sbuf_tensor(f"ssm_{what}", shape, F32))

        xT = sb("xT", [P, BATCH * SEQ])
        tables = [sb(n, [P, NT, NH]) for n in ("dt_half", "a", "ecum", "etot")]
        ssm_inputs(nc, c, "ssm_in", xT, *tables)
        ssm_scan(nc, c, "ssm", xT, *tables)


def linear_attention(nc, c):
    row_scales(nc, c, "att_rows", [(c.r1, 1.0, LN_EPS)])
    with ExitStack() as ctx:
        def sem(what):
            return nc.alloc_semaphore(f"att_{what}")

        def sb(what, shape):
            return ctx.enter_context(nc.sbuf_tensor(f"att_{what}", shape, F32))

        KV = AH * AE * AD
        HE = AH * AE
        xn, xT = sb("xn", [P, 2, DM]), sb("xT", [P, 2, P])
        ex, qk = sb("ex", [P, 2, 2 * DM]), sb("qk", [P, 2, 2 * DM])
        neg = sb("neg", [P, 2 * DM])
        vx, kv = sb("vx", [P, 2, AH, AE]), sb("kv", [P, 2, KV])
        qT, st = sb("qT", [P, 2, P]), sb("st", [P, BATCH, HE])
        w, inter, num, inc = sb("w", [P, KV]), sb("inter", [P, HE]), sb("num", [P, AH, AE]), sb("inc", [P, HE])
        den, rden = sb("den", [P, AH]), sb("rden", [P, AH])
        o, oT = sb("o", [P, 2, DM]), sb("oT", [P, 2, P])

        def pb(what):
            return ctx.enter_context(nc.psum_tensor(f"att_{what}", [P, 512], F32))

        XB, QB, QT = pb("XB"), pb("QB"), pb("QT")
        CUM = ctx.enter_context(nc.psum_tensor("att_CUM", [P, 3 * 512], F32))
        SB_, OB = pb("SB"), pb("OB")
        xn_ready, x_transposed, xT_ready, qkv_done = sem("xn_ready"), sem("x_transposed"), sem("xT_ready"), sem("qkv_done")
        ex_ready, v_ready, negative_ready, qk_ready = sem("ex_ready"), sem("v_ready"), sem("negative_ready"), sem("qk_ready")
        kv_ready, q_transposed, qT_ready, inc_done = sem("kv_ready"), sem("q_transposed"), sem("qT_ready"), sem("inc_done")
        cum_done, w_ready, inter_ready, num_step = sem("cum_done"), sem("w_ready"), sem("inter_ready"), sem("num_step")
        o_ready, o_transposed, oT_ready, out_done = sem("o_ready"), sem("o_transposed"), sem("oT_ready"), sem("out_done")
        x_added, inc_masked, st_ready, zeroed = sem("x_added"), sem("inc_masked"), sem("st_ready"), sem("zeroed")
        STEPS = 2 * TILES
        block = ctx.enter_context(nc.Block(no_gpsimd_drain=True))

        def at(r, q):
            return 2 * r + q, r + q // 2, q % 2

        def exists(r, q):
            return not isinstance(r, int) or 0 <= 2 * r + q < STEPS

        def periods(eng, body):
            for i in range(-4, 4):
                body(0, i)
            with eng.Fori(2, TILES - 2) as r:
                body(r, 0)
                body(r, 1)
            for i in range(STEPS - 4, STEPS + 1):
                body(0, i)

        @block.tensor
        def _(pe):
            def x_transpose(r, q):
                i, t, b = at(r, q)
                pe.wait_ge(xn_ready, i + 1)
                wait(pe, xT_ready, i)
                nc.tensor.transpose(XB[:, 0:P], xn[:, b, :], c.ident[:, :]).then_inc(x_transposed, 1)

            def project(r, q):
                i, t, b = at(r, q)
                pe.wait_ge(xT_ready, i + 1)
                wait(pe, qk_ready, i)
                nc.tensor.matmul(QB[:, 0:3 * DM], xT[:, b, :], c.wqkvT[:, :], start=True, stop=True)\
                    .then_inc(qkv_done, 1)

            def q_transpose(r, q):
                i, t, b = at(r, q)
                pe.wait_ge(qk_ready, i + 1)
                wait(pe, qT_ready, i)
                nc.tensor.transpose(QT[:, 0:P], qk[:, b, 0:DM], c.ident[:, :]).then_inc(q_transposed, 1)

            def increment(r, q):
                i, t, b = at(r, q)
                pe.wait_ge(v_ready, i + 1)
                wait(pe, st_ready, i)
                nc.tensor.matmul(SB_[:, 0:HE], qk[:, b, DM:2 * DM], vx[:, b, :, :], start=True, stop=True)\
                    .then_inc(inc_done, 1)

            def add_up(r, q):
                i, t, b = at(r, q)
                pe.wait_ge(kv_ready, i + 1)
                wait(pe, inter_ready, i)
                for col in range(0, KV, 512):
                    end = min(KV, col + 512)
                    nc.tensor.matmul(CUM[:, col:end], c.upto[:, :], kv[:, b, col:end], start=True, stop=True)
                pe.wait_ge(qT_ready, i + 1)
                wait(pe, st_ready, i - 1)
                nc.tensor.matmul(CUM[:, KV:KV + HE], qT[:, b, :], st[:, b, :], start=True, stop=True)\
                    .then_inc(cum_done, 1)

            def o_transpose(r, q):
                i, t, b = at(r, q)
                pe.wait_ge(o_ready, i + 1)
                wait(pe, x_added, i)
                nc.tensor.transpose(OB[:, 0:P], o[:, b, :], c.ident[:, :]).then_inc(o_transposed, 1)

            def project_out(r, q):
                i, t, b = at(r, q)
                pe.wait_ge(oT_ready, i + 1)
                nc.tensor.matmul(OB[:, P:2 * P], oT[:, b, :], c.waoT[:, :], start=True, stop=True).then_inc(out_done, 1)

            def body(r, q):
                if exists(r, q - 1):
                    o_transpose(r, q - 1)
                if exists(r, q + 1):
                    add_up(r, q + 1)
                if exists(r, q - 1):
                    project_out(r, q - 1)
                if exists(r, q + 2):
                    q_transpose(r, q + 2)
                    increment(r, q + 2)
                if exists(r, q + 3):
                    x_transpose(r, q + 3)
                    project(r, q + 3)

            pe.wait_ge(zeroed, 2)
            periods(pe, body)

        @block.scalar
        def _(act):
            def o_copy(r, q):
                i, t, b = at(r, q)
                act.wait_ge(o_transposed, i + 1)
                wait(act, out_done, i - 1)
                nc.scalar.copy(oT[:, b, :], OB[:, 0:P]).then_inc(oT_ready, 1)

            def q_copy(r, q):
                i, t, b = at(r, q)
                act.wait_ge(q_transposed, i + 1)
                wait(act, cum_done, i - 1)
                nc.scalar.copy(qT[:, b, :], QT[:, 0:P]).then_inc(qT_ready, 1)

            def inputs(r, q):
                i, t, b = at(r, q)
                act.wait_ge(x_transposed, i + 1)
                wait(act, qkv_done, i - 1)
                nc.scalar.copy(xT[:, b, :], XB[:, 0:P]).then_inc(xT_ready, 1)
                act.wait_ge(qkv_done, i + 1)
                wait(act, qk_ready, i - 1)
                chain(act, negative_ready, nc.scalar.activation(neg[:, :], QB[:, 0:2 * DM], ACT.Relu, scale=-1.0), i + 1)
                nc.scalar.activation(ex[:, b, :], neg[:, :], ACT.Exp, scale=-1.0).then_inc(ex_ready, 1)
                wait(act, kv_ready, i - 1)
                wait(act, inc_done, i - 1)
                nc.scalar.copy(vx[:, b, :, 0:AD], QB[:, 2 * DM:3 * DM].rearrange("p (h e) -> p h e", e=AD))\
                    .then_inc(v_ready, 1)

            def body(r, q):
                if exists(r, q - 1):
                    o_copy(r, q - 1)
                if exists(r, q + 2):
                    q_copy(r, q + 2)
                if exists(r, q + 3):
                    inputs(r, q + 3)

            act.wait_ge(zeroed, 2)
            periods(act, body)

        @block.gpsimd
        def _(pool):
            def products(r, q):
                i, t, b = at(r, q)
                pool.wait_ge(qk_ready, i + 1)
                wait(pool, cum_done, i - 1)
                k = qk[:, b, DM:2 * DM].rearrange("p (h d) -> p h d", d=AD).unsqueeze(2)\
                    .broadcast_to([P, AH, AE, AD])
                v = vx[:, b, :, :].unsqueeze(3).broadcast_to([P, AH, AE, AD])
                nc.gpsimd.tensor_tensor(kv[:, b, :].rearrange("p (h e d) -> p h e d", h=AH, e=AE), k, v, ALU.mult)\
                    .then_inc(kv_ready, 1)

            def body(r, q):
                if exists(r, q + 2):
                    products(r, q + 2)

            nc.gpsimd.memset(vx[:, :, :, :], 1.0).then_inc(zeroed, 1)
            nc.gpsimd.memset(st[:, :, :], 0.0).then_inc(zeroed, 1)
            periods(pool, body)
            pool.wait_ge(kv_ready, STEPS)

        @block.vector
        def _(dve):
            mask = c.mask_blk[:, :, :].rearrange("p h e -> p (h e)")

            def normalise(r, q):
                i, t, b = at(r, q)
                wait(dve, x_transposed, i - 1)
                tt = bass.ds(b * TILES + t, 1)
                nc.vector.tensor_scalar(xn[:, b, :], c.x[:, b, bass.ds(t, 1), :].rearrange("p a d -> p (a d)"),
                                        c.mean[:, tt], c.r1[:, tt], ALU.subtract, ALU.mult).then_inc(xn_ready, 1)

            def features(r, q):
                i, t, b = at(r, q)
                dve.wait_ge(ex_ready, i + 1)
                dve.wait_ge(v_ready, i + 1)
                wait(dve, w_ready, i - 1)
                wait(dve, kv_ready, i - 1)
                wait(dve, inc_done, i - 1)
                wait(dve, q_transposed, i - 1)
                nc.vector.scalar_tensor_tensor(out=qk[:, b, :], in0=QB[:, 0:2 * DM], scalar=0.0, in1=ex[:, b, :],
                                               op0=ALU.max, op1=ALU.add).then_inc(qk_ready, 1)

            def read(r, q):
                i, t, b = at(r, q)
                dve.wait_ge(cum_done, i + 1)
                qb = qk[:, b, 0:DM].rearrange("p (h d) -> p h d", d=AD).unsqueeze(2).broadcast_to([P, AH, AE, AD])
                nc.vector.tensor_tensor(w[:, :].rearrange("p (h e d) -> p h e d", h=AH, e=AE),
                                        CUM[:, 0:KV].rearrange("p (h e d) -> p h e d", h=AH, e=AE), qb, ALU.mult)\
                    .then_inc(w_ready, 1)
                nc.vector.tensor_copy(inter[:, :], CUM[:, KV:KV + HE]).then_inc(inter_ready, 1)

            def finish(r, q):
                i, t, b = at(r, q)
                numf = num[:, :, :].rearrange("p h e -> p (h e)")
                dve.wait_ge(w_ready, i + 1)
                chain(dve, num_step, nc.vector.tensor_reduce(
                    numf, w[:, :].rearrange("p (m d) -> p m d", d=AD), AX.X, ALU.add), 4 * i + 1)
                chain(dve, num_step, nc.vector.tensor_tensor(numf, numf, inter[:, :], ALU.add), 4 * i + 2)
                chain(dve, num_step, nc.vector.tensor_scalar(den[:, :], num[:, :, AD], ATT_EPS, None, ALU.add), 4 * i + 3)
                chain(dve, num_step, nc.vector.reciprocal(rden[:, :], den[:, :]), 4 * i + 4)
                wait(dve, o_transposed, i - 1)
                nc.vector.tensor_tensor(o[:, b, :].rearrange("p (h e) -> p h e", e=AD), num[:, :, 0:AD],
                                        rden[:, :].unsqueeze(2).broadcast_to([P, AH, AD]), ALU.mult).then_inc(o_ready, 1)

            def update(r, q):
                i, t, b = at(r, q)
                dve.wait_ge(inc_done, i + 1)
                chain(dve, inc_masked, nc.vector.tensor_tensor(inc[:, :], SB_[:, 0:HE], mask, ALU.mult), i + 1)
                dve.wait_ge(cum_done, i + 1)
                nc.vector.tensor_tensor(st[:, b, :], st[:, b, :], inc[:, :], ALU.add).then_inc(st_ready, 1)

            def residual(r, q):
                i, t, b = at(r, q)
                dve.wait_ge(out_done, i + 1)
                xt = c.x[:, b, bass.ds(t, 1), :].rearrange("p a d -> p (a d)")
                nc.vector.tensor_tensor(xt, OB[:, P:2 * P], xt, ALU.add).then_inc(x_added, 1)

            def stats(r, q):
                i, t, b = at(r, q)
                dve.wait_ge(x_added, i + 1)
                nc.vector.bn_stats(c.st[:, bass.ds(b * TILES + t, 1), :], c.x[:, b, bass.ds(t, 1), :])

            def body(r, q):
                if exists(r, q):
                    read(r, q)
                if exists(r, q + 2):
                    features(r, q + 2)
                if exists(r, q):
                    finish(r, q)
                if exists(r, q + 1):
                    update(r, q + 1)
                if exists(r, q - 1):
                    residual(r, q - 1)
                if exists(r, q + 4):
                    normalise(r, q + 4)
                if exists(r, q - 1):
                    stats(r, q - 1)

            dve.wait_ge(zeroed, 2)
            periods(dve, body)


STAGES = [ssm, lambda nc, c: moe(nc, c, "moe1"), linear_attention, lambda nc, c: moe(nc, c, "moe2", store=True)]


def build(nc, c, stages):
    with ExitStack() as ctx:
        def sb(name, shape, dt=F32):
            return ctx.enter_context(nc.sbuf_tensor(name, shape, dt))

        c.x = sb("x_res", [P, BATCH, TILES, DM])
        c.ident, c.ones = sb("ident", [P, P]), sb("ones", [P, P])
        c.upto, c.after = sb("upto", [P, P]), sb("after", [P, P])
        c.st = sb("st", [P, NT, 6])
        c.mask_blk = sb("mask_blk", [P, AH, AE])
        c.wpT, c.woutT = sb("wpT", [P, PROJ + NH]), sb("woutT", [P, 2, DM])
        c.wqkvT, c.waoT = sb("wqkvT", [P, 3 * DM]), sb("waoT", [P, DM])
        c.seh, c.sel = sb("seh", [P, NS], F16), sb("sel", [P, NS], F16)
        c.bgT, c.buT, c.bdT = sb("bgT", [P, 2, NE]), sb("buT", [P, 2, NE]), sb("bdT", [P, NE])
        c.ewh, c.ewl = sb("ewh", [P, NE, EW], F16), sb("ewl", [P, NE, EW], F16)
        c.gcol, c.bcol = sb("gcol", [P, 1]), sb("bcol", [P, 1])
        c.convw, c.convb, c.dcol = sb("convw", [P, 2, TAPS]), sb("convb", [P, 2]), sb("dcol", [P, 2])
        c.alog, c.dtb = sb("alog", [P, NH]), sb("dtb", [P, NH])
        c.mean, c.r1, c.s = sb("mean", [P, NT]), sb("r1", [P, NT]), sb("s", [P, NT])
        prepare(nc, c)
        for stage in stages[:-1]:
            with nc.cleanup_on_exit():
                stage(nc, c)
        stages[-1](nc, c)


NAMES = dict(L0_attn_a_x="x_dram", L0_attn_a_norm_w="norm_w", L0_attn_a_in_proj_w="in_proj_w",
             L0_attn_a_conv_w="conv_w", L0_attn_a_conv_b="conv_b", L0_attn_a_A_log="A_log", L0_attn_a_D="D_skip",
             L0_attn_a_dt_bias="dt_bias", L0_attn_a_out_proj_w="out_proj_w", L0_attn_b_Wq="Wq", L0_attn_b_Wk="Wk",
             L0_attn_b_Wv="Wv", L0_attn_b_Wo="Wo", L0_ffn_norm_g="norm_g", L0_ffn_norm_b="norm_b",
             L0_ffn_slot_g="slot_g", L0_ffn_slot_b="slot_b", L0_ffn_scale="scale", L0_ffn_slot_embeds="slot_embeds",
             L0_ffn_Wg="Wg", L0_ffn_bg="bg", L0_ffn_Wu="Wu", L0_ffn_bu="bu", L0_ffn_Wd="Wd", L0_ffn_bd="bd")


def kernel(**inputs):
    import numpy as _np
    import concourse.bacc as _bacc
    from concourse import mybir as _mybir
    from concourse.bass_utils import run_bass_kernel_spmd as _run

    nc = _bacc.Bacc("TRN2", target_bir_lowering=False, num_devices=1)
    core, arrays = Core(), {}
    args = {}
    for name, short in NAMES.items():
        a = _np.ascontiguousarray(inputs[name])
        arrays[f"in_{short}"] = a
        args[short] = nc.dram_tensor(f"in_{short}", a.shape, _mybir.dt.from_np(a.dtype), kind="ExternalInput").ap()
    core.__dict__.update(args)
    core.out_dram = nc.dram_tensor("out", (BATCH, SEQ, DM), _mybir.dt.float32, kind="ExternalOutput").ap()
    build(nc, core, STAGES)
    r = _run(nc, [arrays], core_ids=[0])
    return r.results[0]["out"]
```

```python
import concourse.bass as bass
from concourse import mybir
from contextlib import ExitStack

F32 = mybir.dt.float32
F16 = mybir.dt.float16
ACT = mybir.ActivationFunctionType
ALU = mybir.AluOpType
AX = mybir.AxisListType

P = 128
BATCH, SEQ, DM = 2, 2048, 128
TILES = SEQ // P
NT = BATCH * TILES
LN_EPS, RMS_EPS, ATT_EPS = 1e-5, 1e-6, 1e-8
CH = 256
NH, HD = 4, 64
TAPS = 4
PROJ = 2 * CH + 2 * P
NE, SLOTS, FF = 16, 64, 256
NS = NE * SLOTS
EW = 3 * FF
SB = NS // P
AH, AD = 16, 8
AE = AD + 1


def wait(eng, sem, value):
    if isinstance(value, int) and value <= 0:
        return
    eng.wait_ge(sem, value)


def chain(eng, sem, ins, value):
    ins.then_inc(sem, 1)
    eng.wait_ge(sem, value)


def periods(eng, plan, steps, start=2, unroll=2):
    aheads = [ahead for piece, ahead in plan]

    def body(r, q):
        for piece, ahead in plan:
            if not isinstance(r, int) or 0 <= 2 * r + q + ahead < steps:
                piece(r, q + ahead)

    first = 2 * start // unroll
    end = (steps - unroll - max(aheads)) // unroll + 1
    for i in range(-max(aheads), unroll * first):
        body(0, i)
    with eng.Fori(first, end) as r:
        for q in range(unroll):
            body(r if unroll == 2 else unroll // 2 * r, q)
    for i in range(unroll * end, steps - min(aheads)):
        body(0, i)


def split_product(nc, out, left, right, first=True, final=True):
    (lh, ll), (rh, rl) = left, right
    nc.tensor.matmul(out, lh, rh, start=first, stop=False)
    nc.tensor.matmul(out, lh, rl, start=False, stop=False)
    return nc.tensor.matmul(out, ll, rh, start=False, stop=final)


class Core:
    pass


def prepare(nc, c):
    with ExitStack() as ctx:
        def sb(name, shape, dt=F32):
            return ctx.enter_context(nc.sbuf_tensor(name, shape, dt))

        def sem(name):
            return nc.alloc_semaphore(name)

        wp_nat = sb("wp_nat", [P, PROJ // P, DM])
        wdt_nat = sb("wdt_nat", [NH, DM])
        wpT = sb("wpT", [P, PROJ + NH])
        wout_nat = sb("wout_nat", [DM, CH])
        wa_nat = sb("wa_nat", [P, 4, DM])
        se_nat = sb("se_nat", [P, SB, DM])
        b_nat = sb("b_nat", [NE, 2, FF])
        bd_nat = sb("bd_nat", [NE, DM])
        se_st = sb("se_st", [P, SB, 6])
        se_half = sb("se_half", [P, 4, SB])
        se_v, se_sd, se_y, se_t = (sb(f"se_{w}", [P, 1, SB]) for w in ("v", "sd", "y", "t"))
        se_mean, se_scale = sb("se_mean", [P, SB]), sb("se_scale", [P, SB])
        cols = sb("cols", [P, 8])
        dskip = sb("dskip", [P, 2])
        tb = [ctx.enter_context(nc.psum_tensor(f"prep_ps{i}", [P, 512], F32)) for i in range(8)]

        x_in = [sem("x_in0"), sem("x_in1")]
        w_in = sem("w_in")
        cols_in = sem("cols_in")
        se_in = sem("se_in")
        masks_zero = sem("masks_zero")
        masks_ready = sem("masks_ready")
        se_dve = sem("se_dve")
        se_root = sem("se_root")
        se_var = sem("se_var")
        se_scaled = sem("se_scaled")
        tr_done = sem("tr_done")
        ev_act = sem("ev_act")
        wp_hi = sem("wp_hi")

        jobs = []
        for k in range(PROJ // P):
            jobs.append((wp_nat[:, k, :], P, wpT[:, k * P:(k + 1) * P], "norm"))
        jobs.append((wdt_nat[:, :], NH, wpT[:, PROJ:PROJ + NH], "norm"))
        for k in range(2):
            jobs.append((wout_nat[:, k * P:(k + 1) * P], P, c.woutT[:, k, :], "half"))
        for k in range(3):
            jobs.append((wa_nat[:, k, :], P, c.wqkvT[:, k * P:(k + 1) * P], "copy"))
        jobs.append((wa_nat[:, 3, :], P, c.waoT[:, :], "copy"))
        for which, dst in ((0, c.bgT), (1, c.buT)):
            for k in range(2):
                jobs.append((b_nat[:, which, k * P:(k + 1) * P], NE, dst[:, k, :], "copy"))
        jobs.append((bd_nat[:, :], NE, c.bdT[:, :], "copy"))
        for j in range(SB):
            jobs.append((se_nat[:, j, :], P, c.se32[:, j * P:(j + 1) * P], "slot"))
        first_se = len(jobs) - SB

        block = ctx.enter_context(nc.Block(no_gpsimd_drain=True))

        @block.sync
        def _(sp):
            sp.dma_start(wp_nat[:, :, :], c.in_proj_w[0:PROJ, :].rearrange("(k p) d -> p k d", p=P)).then_inc(w_in, 16)
            sp.dma_start(wdt_nat[:, :], c.in_proj_w[PROJ:PROJ + NH, :]).then_inc(w_in, 16)
            sp.dma_start(wout_nat[:, :], c.out_proj_w).then_inc(w_in, 16)
            for k, w in enumerate((c.Wq, c.Wk, c.Wv, c.Wo)):
                sp.dma_start(wa_nat[:, k, :], w).then_inc(w_in, 16)
            sp.dma_start(b_nat[:, 0, :], c.bg).then_inc(w_in, 16)
            sp.dma_start(b_nat[:, 1, :], c.bu).then_inc(w_in, 16)
            sp.dma_start(bd_nat[:, :], c.bd).then_inc(w_in, 16)
            for dst, v in ((c.gcol, c.norm_g), (c.bcol, c.norm_b)):
                sp.dma_start(dst[:, :], v.rearrange("(p a) -> p a", a=1)).then_inc(cols_in, 16)
            sp.dma_start(c.alog[:, :], c.A_log.rearrange("(a h) -> a h", a=1).broadcast_to([P, NH])).then_inc(cols_in, 16)
            sp.dma_start(c.dtb[:, :], c.dt_bias.rearrange("(a h) -> a h", a=1).broadcast_to([P, NH])).then_inc(cols_in, 16)
            for h in range(2):
                src = c.D_skip.rearrange("(k h) -> h k", h=2)[h:h + 1, :]
                sp.dma_start(dskip[h * HD:(h + 1) * HD, :], src.broadcast_to([HD, 2]),
                             allow_slow_non_contiguous=True).then_inc(cols_in, 16)

        @block.scalar
        def _(act):
            act.dma_start(se_nat[:, :, :], c.slot_embeds.rearrange("e s d -> (e s) d")
                          .rearrange("(j p) d -> p j d", p=P)).then_inc(se_in, 16)
            for k, v in enumerate((c.norm_w, c.slot_g, c.slot_b)):
                act.dma_start(cols[:, k:k + 1], v.rearrange("(p a) -> p a", a=1)).then_inc(cols_in, 16)
            act.dma_start(cols[:, 3:4], c.scale.rearrange("(p a) -> p a", a=1).broadcast_to([P, 1])).then_inc(cols_in, 16)
            act.dma_start(c.convw[:, :, :], c.conv_w.rearrange("(k p) t -> p k t", p=P)).then_inc(cols_in, 16)
            act.dma_start(c.convb[:, :], c.conv_b.rearrange("(k p) -> p k", p=P),
                          allow_slow_non_contiguous=True).then_inc(cols_in, 16)
            act.wait_ge(se_var, 1)
            nc.scalar.activation(se_sd[:, :, :], se_v[:, :, :], ACT.Sqrt).then_inc(se_root, 1)
            act.wait_ge(cols_in, 16 * 12)
            for n, (src, rows, dst, how) in enumerate(jobs):
                act.wait_ge(tr_done, n + 1)
                if n == first_se:
                    act.wait_ge(ev_act, n)
                    nc.scalar.copy(c.wph[:, :], wpT[:, :]).then_inc(wp_hi, 1)
                    act.wait_ge(se_dve, 9)
                ps = tb[n % 8][:, 0:rows]
                if how == "norm":
                    nc.scalar.activation(dst, ps, ACT.Copy, scale=cols[:, 0:1]).then_inc(ev_act, 1)
                elif how == "slot":
                    nc.scalar.activation(dst, ps, ACT.Identity, scale=cols[:, 4:5], bias=cols[:, 5:6]).then_inc(ev_act, 1)
                elif how == "half":
                    nc.scalar.activation(dst, ps, ACT.Copy, scale=0.5).then_inc(ev_act, 1)
                else:
                    nc.scalar.copy(dst, ps).then_inc(ev_act, 1)
            act.wait_ge(ev_act, len(jobs))
            nc.scalar.copy(c.seh[:, :], c.se32[:, :])

        @block.gpsimd
        def _(pool):
            for b in range(BATCH):
                pool.dma_start(c.x[:, b, :, :], c.x_dram[b].rearrange("(t p) d -> p t d", p=P)).then_inc(x_in[b], 16)
            nc.gpsimd.memset(c.ident[:, :], 0.0).then_inc(masks_zero, 1)
            nc.gpsimd.memset(c.ones[:, :], 1.0).then_inc(masks_zero, 1)
            nc.gpsimd.memset(c.mask_blk[:, :, :], 1.0).then_inc(masks_zero, 1)
            pool.wait_ge(masks_zero, 3)
            nc.gpsimd.affine_select(out=c.ident[:, :], in_=c.ident[:, :], compare_op=ALU.not_equal, fill=1.0,
                                    base=0, pattern=[[-1, P]], channel_multiplier=1).then_inc(masks_ready, 1)
            nc.gpsimd.affine_select(out=c.upto[:, :], in_=c.ones[:, :], compare_op=ALU.is_ge, fill=0.0,
                                    base=0, pattern=[[1, P]], channel_multiplier=-1).then_inc(masks_ready, 1)
            nc.gpsimd.affine_select(out=c.after[:, :], in_=c.ones[:, :], compare_op=ALU.is_gt, fill=0.0,
                                    base=0, pattern=[[-1, P]], channel_multiplier=1).then_inc(masks_ready, 1)
            nc.gpsimd.affine_select(out=c.mask_blk[:, :, :], in_=c.mask_blk[:, :, :], compare_op=ALU.is_ge, fill=0.0,
                                    base=0, pattern=[[-AD, AH], [0, AE]], channel_multiplier=1).then_inc(masks_zero, 1)
            pool.wait_ge(masks_zero, 4)
            nc.gpsimd.affine_select(out=c.mask_blk[:, :, :], in_=c.mask_blk[:, :, :], compare_op=ALU.is_ge, fill=0.0,
                                    base=AD - 1, pattern=[[AD, AH], [0, AE]], channel_multiplier=-1).then_inc(masks_ready, 1)
            pool.wait_ge(masks_ready, 4)

        @block.vector
        def _(dve):
            def stats(b):
                dve.wait_ge(x_in[b], 16)
                for t in range(TILES):
                    nc.vector.bn_stats(c.st[:, b * TILES + t, :], c.x[:, b, t, :])

            dve.wait_ge(se_in, 16)
            for j in range(SB):
                last = nc.vector.bn_stats(se_st[:, j, :], se_nat[:, j, :])
            chain(dve, se_dve, last, 1)
            variance(nc, dve, se_st, se_half, se_mean[:, :], se_dve, 1)
            nc.vector.tensor_scalar(se_v[:, 0, :], se_half[:, 3, :], LN_EPS, None, ALU.add).then_inc(se_var, 1)
            dve.wait_ge(se_root, 1)
            chain(dve, se_dve, inverse_root(nc, dve, se_v[:, :, :], se_sd[:, :, :], se_y[:, :, :], se_t[:, :, :],
                                            [(se_scale[:, :], 0)], se_dve, 4), 8)
            for j in range(SB):
                nc.vector.tensor_scalar(se_nat[:, j, :], se_nat[:, j, :], se_mean[:, j:j + 1], se_scale[:, j:j + 1],
                                        ALU.subtract, ALU.mult).then_inc(se_scaled, 1)
            stats(0)
            dve.wait_ge(cols_in, 16 * 12)
            nc.vector.tensor_scalar(cols[:, 4:6], cols[:, 1:3], cols[:, 3:4], None, ALU.mult).then_inc(se_dve, 1)
            dve.wait_ge(se_dve, 9)
            nc.vector.tensor_scalar(c.dcol[:, :], dskip[:, :], 0.5, None, ALU.mult)
            stats(1)
            dve.wait_ge(wp_hi, 1)
            nc.vector.tensor_tensor(c.wpl[:, :], wpT[:, :], c.wph[:, :], ALU.subtract)

        @block.tensor
        def _(pe):
            pe.wait_ge(masks_ready, 1)
            pe.wait_ge(w_in, 16 * 10)
            for n, (src, rows, dst, how) in enumerate(jobs):
                if n >= 8:
                    m = n - 8
                    pe.wait_ge(ev_act, m + 1)
                if how == "slot":
                    pe.wait_ge(se_scaled, n - first_se + 1)
                nc.tensor.transpose(tb[n % 8][:, 0:rows], src, c.ident[0:rows, 0:rows]).then_inc(tr_done, 1)



def variance(nc, dve, st, tmp, mean, sem, n):
    nc.vector.tensor_tensor(tmp[:, 0, :], st[:, :, 1], st[:, :, 4], ALU.add)
    nc.vector.tensor_tensor(tmp[:, 2, :], st[:, :, 2], st[:, :, 5], ALU.add)
    chain(dve, sem, nc.vector.tensor_tensor(tmp[:, 1, :], st[:, :, 1], st[:, :, 4], ALU.subtract), n + 1)
    nc.vector.tensor_scalar(mean, tmp[:, 0, :], 0.5, None, ALU.mult)
    chain(dve, sem, nc.vector.scalar_tensor_tensor(out=tmp[:, 1, :], in0=tmp[:, 1, :], scalar=0.25,
                                                   in1=tmp[:, 1, :], op0=ALU.mult, op1=ALU.mult), n + 2)
    chain(dve, sem, nc.vector.scalar_tensor_tensor(out=tmp[:, 3, :], in0=tmp[:, 2, :], scalar=1.0 / DM,
                                                   in1=tmp[:, 1, :], op0=ALU.mult, op1=ALU.add), n + 3)


def inverse_root(nc, dve, v, sd, y, t, outs, sem, n):
    chain(dve, sem, nc.vector.reciprocal(y, sd), n + 1)
    chain(dve, sem, nc.vector.tensor_tensor(t, y, y, ALU.mult), n + 2)
    chain(dve, sem, nc.vector.scalar_tensor_tensor(out=t, in0=t, scalar=-0.5, in1=v, op0=ALU.mult, op1=ALU.mult), n + 3)
    for out, k in outs:
        last = nc.vector.scalar_tensor_tensor(out=out, in0=t[:, k, :], scalar=1.5, in1=y[:, k, :],
                                              op0=ALU.add, op1=ALU.mult)
    return last
class RowScales:

    def __init__(self, nc, c, ctx, name, norms):
        n = len(norms)
        self.nc, self.c, self.norms = nc, c, norms
        self.half = ctx.enter_context(nc.sbuf_tensor(f"{name}_half", [P, 4, NT], F32))
        self.v, self.sd, self.y, self.t = (ctx.enter_context(nc.sbuf_tensor(f"{name}_{w}", [P, n, NT], F32))
                                           for w in ("v", "sd", "y", "t"))
        self.step = nc.alloc_semaphore(f"{name}_dve_step")
        self.var_ready = nc.alloc_semaphore(f"{name}_var_ready")
        self.root_ready = nc.alloc_semaphore(f"{name}_root_ready")
        self.scales_ready = nc.alloc_semaphore(f"{name}_scales_ready")

    def on_vector(self, dve):
        nc, v = self.nc, self.v
        variance(nc, dve, self.c.st, self.half, self.c.mean[:, :], self.step, 0)
        for k, (out, a, b) in enumerate(self.norms):
            last = nc.vector.tensor_scalar(v[:, k, :], self.half[:, 3, :], a, b, ALU.mult, ALU.add)
        last.then_inc(self.var_ready, 1)
        dve.wait_ge(self.root_ready, 1)
        last = inverse_root(nc, dve, v[:, :, :], self.sd[:, :, :], self.y[:, :, :], self.t[:, :, :],
                            [(out[:, :], k) for k, (out, a, b) in enumerate(self.norms)], self.step, 3)
        chain(dve, self.scales_ready, last, 1)

    def on_scalar(self, act):
        act.wait_ge(self.var_ready, 1)
        self.nc.scalar.activation(self.sd[:, :, :], self.v[:, :, :], ACT.Sqrt).then_inc(self.root_ready, 1)


class Normalise:

    G = 4
    NG = NT // G

    def __init__(self, nc, c, ctx, name, xh, xT, ps):
        self.nc, self.c, self.xh, self.xT, self.ps = nc, c, xh, xT, ps
        self.xn = ctx.enter_context(nc.sbuf_tensor(f"{name}_xn", [P, 2, self.G, DM], F32))
        self.xa = ctx.enter_context(nc.sbuf_tensor(f"{name}_xa", [P, 2, self.G * P], F32))
        self.xn_ready, self.xn_hi, self.xn_split, self.transposed, self.affine, self.xT_ready = (
            nc.alloc_semaphore(f"{name}_{what}")
            for what in ("xn_ready", "xn_hi", "xn_split", "x_transposed", "x_affine", "xT_ready"))
        self.rows = RowScales(nc, c, ctx, name, [(c.s, 1 + LN_EPS, LN_EPS * LN_EPS)])

    def group(self, r, q):
        g = 2 * r + q
        return g, q % 2, bass.ds(g * self.G, self.G), bass.ds(g * (self.G * P), self.G * P)

    def on_vector(self, dve, before_last):
        nc, c = self.nc, self.c
        xf = c.x[:, :, :, :].rearrange("p b t d -> p (b t) d")

        def normalise(r, q):
            g, pp, tiles, cols = self.group(r, q)
            wait(dve, self.transposed, g - 1)
            wait(dve, self.xn_split, g - 1)
            for n in range(self.G):
                t = bass.ds(g * self.G + n, 1)
                last = nc.vector.tensor_scalar(self.xn[:, pp, n, :], xf[:, t, :], c.mean[:, t], c.s[:, t],
                                               ALU.subtract, ALU.mult)
            last.then_inc(self.xn_ready, 1)

        def low(r, q):
            g, pp, tiles, cols = self.group(r, q)
            if isinstance(g, int) and g == self.NG - 2:
                before_last()
            dve.wait_ge(self.affine, g + 1)
            nc.vector.tensor_tensor(self.xT[:, 1, cols], self.xa[:, pp, :], self.xT[:, 0, cols], ALU.subtract)\
                .then_inc(self.xT_ready, 1)

        self.rows.on_vector(dve)
        periods(dve, ((normalise, 2), (low, 0)), self.NG, 1)

    def on_gpsimd(self, pool):
        def low(r, q):
            g, pp, tiles, cols = self.group(r, q)
            pool.wait_ge(self.xn_hi, g + 1)
            self.nc.gpsimd.tensor_tensor(self.xh[:, tiles, 1, :], self.xn[:, pp, :, :], self.xh[:, tiles, 0, :],
                                         ALU.subtract).then_inc(self.xn_split, 1)

        with pool.Fori(0, self.NG // 2) as r:
            low(r, 0)
            low(r, 1)

    def transpose(self, pe, g):
        pp = g % 2
        pe.wait_ge(self.xn_ready, g + 1)
        wait(pe, self.affine, g - 1)
        for n in range(self.G):
            last = self.nc.tensor.transpose(self.ps[pp][:, n, :], self.xn[:, pp, n, :], self.c.ident[:, :])
        last.then_inc(self.transposed, 1)

    def on_scalar(self, act):
        nc, c = self.nc, self.c

        def high(r, q):
            g, pp, tiles, cols = self.group(r, q)
            act.wait_ge(self.xn_ready, g + 1)
            nc.scalar.copy(self.xh[:, tiles, 0, :], self.xn[:, pp, :, :]).then_inc(self.xn_hi, 1)

        def apply(r, q):
            g, pp, tiles, cols = self.group(r, q)
            act.wait_ge(self.transposed, g + 1)
            wait(act, self.xT_ready, g - 1)
            src = self.ps[pp][:, :, :].rearrange("p n t -> p (n t)")
            nc.scalar.activation(self.xa[:, pp, :], src, ACT.Identity, scale=c.gcol[:, 0:1], bias=c.bcol[:, 0:1])
            nc.scalar.activation(self.xT[:, 0, cols], src, ACT.Identity,
                                 scale=c.gcol[:, 0:1], bias=c.bcol[:, 0:1]).then_inc(self.affine, 1)

        self.rows.on_scalar(act)
        periods(act, ((high, 1), (apply, 0)), self.NG, 1)


def moe_dispatch(nc, c, name, xh, xT, sT):
    with ExitStack() as ctx:
        def sem(what):
            return nc.alloc_semaphore(f"{name}_{what}")

        NK = SEQ // 512
        RING = 4
        e32 = ctx.enter_context(nc.sbuf_tensor(f"{name}_e32", [P, 2, SEQ], F32))
        eh = ctx.enter_context(nc.sbuf_tensor(f"{name}_eh", [P, RING, 4, P], F16))
        el = ctx.enter_context(nc.sbuf_tensor(f"{name}_el", [P, RING, 4, P], F16))
        mx = ctx.enter_context(nc.sbuf_tensor(f"{name}_mx", [P, 2, NK], F32))
        nmx = ctx.enter_context(nc.sbuf_tensor(f"{name}_nmx", [P, 2], F32))
        sums = ctx.enter_context(nc.sbuf_tensor(f"{name}_sums", [P, 2, NK], F32))
        rs = ctx.enter_context(nc.sbuf_tensor(f"{name}_rs", [P, 2, 2], F32))
        part = ctx.enter_context(nc.sbuf_tensor(f"{name}_part", [P, P], F32))
        slots = ctx.enter_context(nc.sbuf_tensor(f"{name}_slots", [P, 2, P], F32))
        aff = ctx.enter_context(nc.sbuf_tensor(f"{name}_aff", [P, 2, P], F32))
        LB = [ctx.enter_context(nc.psum_tensor(f"{name}_L{i}", [P, 512], F32)) for i in range(NK)]
        TB = [ctx.enter_context(nc.psum_tensor(f"{name}_T{i}", [P, 4, P], F32)) for i in range(2)]
        SL = [ctx.enter_context(nc.psum_tensor(f"{name}_S{i}", [P, 512], F32)) for i in range(2)]
        logits, maxed, max_parts, exped = sem("logits"), sem("maxed"), sem("max_parts"), sem("exped")
        transposed, hi_ready, lo_ready, summed = sem("transposed"), sem("hi_ready"), sem("lo_ready"), sem("summed")
        total_ready, inverse_ready, part_ready = sem("total_ready"), sem("inverse_ready"), sem("part_ready")
        slots_ready = sem("slots_ready")
        slots_transposed, slots_out = sem("slots_transposed"), sem("slots_out")
        slots_low = sem("slots_low")
        tokens = Normalise(nc, c, ctx, f"{name}_norm", xh, xT, TB)
        block = ctx.enter_context(nc.Block(no_gpsimd_drain=True))
        STEPS = 2 * SB

        def step(r, q):
            return 2 * r + q, r + q // 2, q % 2

        @block.tensor
        def _(pe):
            def logit(r, q, banks=range(NK)):
                i, j, b = step(r, q)
                jj = bass.ds(j * P, P)
                for k in banks:
                    wait(pe, exped, 4 * i - 3 + k)
                    cols = slice(b * SEQ + k * 512, b * SEQ + (k + 1) * 512)
                    nc.tensor.matmul(LB[k][:, :], c.seh[:, jj], xT[:, 0, cols], start=True, stop=False)
                    nc.tensor.matmul(LB[k][:, :], c.seh[:, jj], xT[:, 1, cols], start=False, stop=False)
                    nc.tensor.matmul(LB[k][:, :], c.sel[:, jj], xT[:, 0, cols], start=False, stop=True)\
                        .then_inc(logits, 1)

            def transpose(r, q, g):
                i, j, b = step(r, q)
                pe.wait_ge(exped, 4 * i + g + 1)
                wait(pe, lo_ready, 4 * i + g - 1)
                for k in range(4):
                    col = (4 * g + k) * P
                    last = nc.tensor.transpose(TB[g % 2][:, k, :], e32[:, b, col:col + P], c.ident[:, :])
                last.then_inc(transposed, 1)

            def collect(r, q, g):
                i, j, b = step(r, q)
                pe.wait_ge(lo_ready, 4 * i + g + 1)
                if g == 0:
                    wait(pe, slots_out, i - 1)
                for k in range(4):
                    t = b * TILES + 4 * g + k
                    first, final = g == 0 and k == 0, g == NK - 1 and k == 3
                    nc.tensor.matmul(SL[b][:, 0:2 * P], eh[:, g, k, :],
                                     xh[:, t, :, :].rearrange("p h d -> p (h d)"),
                                     start=first, stop=False, skip_group_check=True)
                    last = nc.tensor.matmul(SL[b][:, 0:P], el[:, g, k, :], xh[:, t, 0, :],
                                            start=False, stop=final, skip_group_check=True)
                last.then_inc(summed, 1)

            def slot_transpose(r, q):
                i, j, b = step(r, q)
                pe.wait_ge(slots_ready, i + 1)
                nc.tensor.transpose(SL[b][:, 2 * P:3 * P], slots[:, b, :], c.ident[:, :]).then_inc(slots_transposed, 1)

            def body(r, q, first=False, final=False):
                def ahead(bank):
                    if not final:
                        logit(r, q + 1, [bank])

                for k in range(NK):
                    if first:
                        pe.wait_ge(tokens.xT_ready, NK + k + 1)
                    ahead(k)
                if first:
                    pe.wait_ge(tokens.xn_split, tokens.NG)
                transpose(r, q, 0)
                transpose(r, q, 1)
                if not first:
                    collect(r, q - 1, 2)
                    collect(r, q - 1, 3)
                transpose(r, q, 2)
                collect(r, q, 0)
                if not first:
                    slot_transpose(r, q - 1)
                transpose(r, q, 3)
                collect(r, q, 1)

            for g in range(tokens.NG):
                tokens.transpose(pe, g)
                if 2 <= g < 2 + NK:
                    pe.wait_ge(tokens.xT_ready, g - 1)
                    logit(0, 0, [g - 2])
            body(0, 0, first=True)
            body(0, 1)
            body(0, 2)
            with pe.Fori(1, SB - 1) as r:
                body(r, 1)
                body(r, 2)
            body(SB - 1, 1, final=True)
            collect(SB - 1, 1, 2)
            collect(SB - 1, 1, 3)
            slot_transpose(SB - 1, 1)

        @block.vector
        def _(dve):
            def peak(r, q, k):
                i, j, b = step(r, q)
                dve.wait_ge(logits, 4 * i + k + 1)
                if k < NK - 1:
                    nc.vector.tensor_reduce(mx[:, b, k:k + 1], LB[k][:, :], AX.X, ALU.max)
                else:
                    chain(dve, max_parts, nc.vector.tensor_reduce(mx[:, b, k:k + 1], LB[k][:, :], AX.X, ALU.max), i + 1)
                    nc.vector.tensor_reduce(nmx[:, b:b + 1], mx[:, b, :], AX.X, ALU.max, negate=True).then_inc(maxed, 1)

            def low(r, q, g):
                i, j, b = step(r, q)
                dve.wait_ge(hi_ready, 4 * i + g + 1)
                nc.vector.tensor_tensor(el[:, g, :, :], TB[g % 2][:, :, :], eh[:, g, :, :], ALU.subtract)\
                    .then_inc(lo_ready, 1)

            def inverse(r, q):
                i, j, b = step(r, q)
                dve.wait_ge(exped, 4 * i + 4)
                chain(dve, total_ready, nc.vector.tensor_reduce(rs[:, b, 0:1], sums[:, b, :], AX.X, ALU.add), i + 1)
                chain(dve, inverse_ready, nc.vector.reciprocal(rs[:, b, 1:2], rs[:, b, 0:1]), i + 1)

            def normalise(r, q):
                i, j, b = step(r, q)
                dve.wait_ge(summed, 4 * i + 4)
                chain(dve, part_ready, nc.vector.tensor_scalar(part[:, :], SL[b][:, P:2 * P], rs[:, b, 1:2], None,
                                                               ALU.mult), i + 1)
                nc.vector.scalar_tensor_tensor(out=slots[:, b, :], in0=SL[b][:, 0:P], scalar=rs[:, b, 1:2],
                                               in1=part[:, :], op0=ALU.mult, op1=ALU.add).then_inc(slots_ready, 1)

            def body(r, q, first=False, final=False):
                def ahead(k):
                    if not final:
                        peak(r, q + 1, k)

                for k in range(NK):
                    ahead(k)
                inverse(r, q)
                low(r, q, 0)
                low(r, q, 1)
                if not first:
                    normalise(r, q - 1)
                low(r, q, 2)
                low(r, q, 3)

            def first_peaks():
                for k in range(NK):
                    peak(0, 0, k)

            tokens.on_vector(dve, first_peaks)
            body(0, 0, first=True)
            with dve.Fori(0, SB - 1) as r:
                body(r, 1)
                body(r, 2)
            body(SB - 1, 1, final=True)
            normalise(SB - 1, 1)

        @block.scalar
        def _(act):
            def exponential(r, q, k):
                i, j, b = step(r, q)
                if k == 0:
                    act.wait_ge(maxed, i + 1)
                    wait(act, transposed, 4 * i - 4)
                    wait(act, total_ready, i - 1)
                nc.scalar.activation(e32[:, b, k * 512:(k + 1) * 512], LB[k][:, :], ACT.Exp,
                                     bias=nmx[:, b:b + 1], accum_out=sums[:, b, k:k + 1]).then_inc(exped, 1)

            def high(r, q, g):
                i, j, b = step(r, q)
                act.wait_ge(transposed, 4 * i + g + 1)
                wait(act, summed, 4 * i + g - 3)
                nc.scalar.copy(eh[:, g, :, :], TB[g % 2][:, :, :]).then_inc(hi_ready, 1)

            def affine(r, q):
                i, j, b = step(r, q)
                act.wait_ge(slots_transposed, i + 1)
                wait(act, slots_low, i - 1)
                ps = SL[b][:, 2 * P:3 * P]
                nc.scalar.activation(aff[:, b, :], ps, ACT.Identity, scale=c.gcol[:, 0:1], bias=c.bcol[:, 0:1])
                nc.scalar.activation(sT[:, bass.ds(j, 1), 0, b, :], ps, ACT.Identity,
                                     scale=c.gcol[:, 0:1], bias=c.bcol[:, 0:1]).then_inc(slots_out, 1)

            def body(r, q, first=False, final=False):
                def ahead(k):
                    if not final:
                        exponential(r, q + 1, k)

                high(r, q, 0)
                high(r, q, 1)
                ahead(0)
                ahead(1)
                high(r, q, 2)
                ahead(2)
                high(r, q, 3)
                if not first:
                    affine(r, q - 1)
                ahead(3)

            tokens.on_scalar(act)
            for k in range(NK):
                exponential(0, 0, k)
            body(0, 0, first=True)
            body(0, 1)
            body(0, 2)
            with act.Fori(1, SB - 1) as r:
                body(r, 1)
                body(r, 2)
            body(SB - 1, 1, final=True)
            affine(SB - 1, 1)

        @block.gpsimd
        def _(pool):
            def low(r, q):
                i, j, b = step(r, q)
                pool.wait_ge(slots_out, i + 1)
                nc.gpsimd.tensor_tensor(sT[:, bass.ds(j, 1), 1, b, :], aff[:, b, :].unsqueeze(1),
                                        sT[:, bass.ds(j, 1), 0, b, :], ALU.subtract).then_inc(slots_low, 1)

            tokens.on_gpsimd(pool)
            with pool.Fori(0, SB) as r:
                low(r, 0)
                low(r, 1)
            pool.wait_ge(slots_low, STEPS)


def moe_experts(nc, c, name, sT, eo):
    with ExitStack() as ctx:
        def sem(what):
            return nc.alloc_semaphore(f"{name}_{what}")

        def sb(what, shape, dt=F32):
            return ctx.enter_context(nc.sbuf_tensor(f"{name}_{what}", shape, dt))

        def pb(what):
            return ctx.enter_context(nc.psum_tensor(f"{name}_{what}", [P, 512], F32))

        FB = FF // P
        gate, hid = sb("gate", [P, 2, 2, FB, P]), sb("hid", [P, 2, 2, FB, P])
        hh, hl = sb("hh", [P, 2, 2, FB, P], F16), sb("hl", [P, 2, 2, FB, P], F16)
        oT = sb("oT", [P, 2, BATCH, P])
        HB = [[pb(f"H{pj}{e2}").ap().rearrange("p (w k s) -> p w k s", w=2, k=FB) for e2 in range(2)]
              for pj in range(2)]
        DB = [pb(f"D{pj}").ap()[:, 0:2 * P].rearrange("p (e s) -> p e s", e=2) for pj in range(2)]
        OB = [pb(f"O{pj}").ap()[:, 0:2 * P].rearrange("p (b o) -> p b o", b=BATCH) for pj in range(2)]
        up_done, gate_ready, hid_ready, down_done = sem("up_done"), sem("gate_ready"), sem("hid_ready"), sem("down_done")
        hid_hi, hid_lo, biased, out_transposed = sem("hid_hi"), sem("hid_lo"), sem("biased"), sem("out_transposed")
        out_hi, out_lo = sem("out_hi"), sem("out_lo")
        block = ctx.enter_context(nc.Block(no_gpsimd_drain=True))

        def all_pairs(body):
            for j in range(-1, SB + 1):
                body(j, j % 2)

        def exists(j, ahead):
            return 0 <= j + ahead < SB

        @block.tensor
        def _(pe):
            def weights(e, col):
                return [w[:, bass.ds(e, 1), col:col + P].rearrange("p a m -> p (a m)") for w in (c.ewh, c.ewl)]

            def up(j, pj, e2):
                e = 2 * j + e2
                wait(pe, hid_ready, e - 3)
                rows = [sT[:, bass.ds(j, 1), half, :, e2 * SLOTS:(e2 + 1) * SLOTS] for half in range(2)]
                for which in range(2):
                    for k in range(FB):
                        last = split_product(nc, HB[pj][e2][:, which, k, :], weights(e, which * FF + k * P), rows)
                last.then_inc(up_done, 1)

            def down(j, pj, e2):
                e = 2 * j + e2
                pe.wait_ge(hid_lo, e + 1)
                if e2 == 0:
                    wait(pe, biased, j - 1)
                for k in range(FB):
                    last = split_product(nc, DB[pj][:, e2, :], weights(e, 2 * FF + k * P),
                                         (hh[:, pj, e2, k, :], hl[:, pj, e2, k, :]), k == 0, k == FB - 1)
                last.then_inc(down_done, 1)

            def to_slots(j, pj):
                pe.wait_ge(biased, j + 1)
                wait(pe, out_lo, j - 1)
                for b in range(BATCH):
                    last = nc.tensor.transpose(OB[pj][:, b, :], oT[:, pj, b, :], c.ident[:, :])
                last.then_inc(out_transposed, 1)

            def body(j, pj):
                if exists(j, 1):
                    up(j + 1, 1 - pj, 0)
                    up(j + 1, 1 - pj, 1)
                if exists(j, -1):
                    to_slots(j - 1, 1 - pj)
                if exists(j, 0):
                    down(j, pj, 0)
                    down(j, pj, 1)

            all_pairs(body)

        @block.scalar
        def _(act):
            def gelu(j, pj, e2):
                e = 2 * j + e2
                act.wait_ge(up_done, e + 1)
                wait(act, hid_ready, e - 3)
                for k in range(FB):
                    last = nc.scalar.activation(gate[:, pj, e2, k, :], HB[pj][e2][:, 0, k, :], ACT.Gelu,
                                                bias=c.bgT[:, k, bass.ds(e, 1)])
                last.then_inc(gate_ready, 1)

            def high(j, pj, e2):
                e = 2 * j + e2
                act.wait_ge(hid_ready, e + 1)
                wait(act, down_done, e - 3)
                nc.scalar.copy(hh[:, pj, e2, :, :], hid[:, pj, e2, :, :]).then_inc(hid_hi, 1)

            def out_high(j, pj):
                act.wait_ge(out_transposed, j + 1)
                nc.scalar.copy(eo[:, :, bass.ds(j, 1), 0, :], OB[pj][:, :, :]).then_inc(out_hi, 1)

            def body(j, pj):
                if exists(j, 1):
                    gelu(j + 1, 1 - pj, 0)
                    gelu(j + 1, 1 - pj, 1)
                if exists(j, -1):
                    out_high(j - 1, 1 - pj)
                if exists(j, 1):
                    high(j + 1, 1 - pj, 0)
                    high(j + 1, 1 - pj, 1)

            all_pairs(body)

        @block.gpsimd
        def _(pool):
            def low(j, pj, e2):
                e = 2 * j + e2
                pool.wait_ge(hid_hi, e + 1)
                wait(pool, down_done, e - 3)
                nc.gpsimd.tensor_tensor(hl[:, pj, e2, :, :], hid[:, pj, e2, :, :], hh[:, pj, e2, :, :], ALU.subtract)\
                    .then_inc(hid_lo, 1)

            def body(j, pj):
                if exists(j, 1):
                    low(j + 1, 1 - pj, 0)
                    low(j + 1, 1 - pj, 1)

            all_pairs(body)
            pool.wait_ge(hid_lo, NE)

        @block.vector
        def _(dve):
            def hidden(j, pj, e2):
                e = 2 * j + e2
                dve.wait_ge(gate_ready, e + 1)
                wait(dve, hid_lo, e - 3)
                for k in range(FB):
                    last = nc.vector.scalar_tensor_tensor(out=hid[:, pj, e2, k, :], in0=HB[pj][e2][:, 1, k, :],
                                                          scalar=c.buT[:, k, bass.ds(e, 1)], in1=gate[:, pj, e2, k, :],
                                                          op0=ALU.add, op1=ALU.mult)
                last.then_inc(hid_ready, 1)

            def bias(j, pj):
                dve.wait_ge(down_done, 2 * j + 2)
                wait(dve, out_transposed, j - 1)
                by_expert = oT[:, pj, :, :].rearrange("p b (e s) -> p e b s", e=2)
                for e2 in range(2):
                    last = nc.vector.tensor_scalar(by_expert[:, e2, :, :], DB[pj][:, e2, :]
                                                   .rearrange("p (b s) -> p b s", b=BATCH),
                                                   c.bdT[:, bass.ds(2 * j + e2, 1)], None, ALU.add)
                last.then_inc(biased, 1)

            def out_low(j, pj):
                dve.wait_ge(out_hi, j + 1)
                nc.vector.tensor_tensor(eo[:, :, bass.ds(j, 1), 1, :].rearrange("p b a o -> p (b a) o"), OB[pj][:, :, :],
                                        eo[:, :, bass.ds(j, 1), 0, :].rearrange("p b a o -> p (b a) o"), ALU.subtract)\
                    .then_inc(out_lo, 1)

            def body(j, pj):
                if exists(j, 1):
                    hidden(j + 1, 1 - pj, 0)
                    hidden(j + 1, 1 - pj, 1)
                if exists(j, -1):
                    out_low(j - 1, 1 - pj)
                if exists(j, 0):
                    bias(j, pj)

            all_pairs(body)


def moe_combine(nc, c, name, xT, eo, store):
    with ExitStack() as ctx:
        def sem(what):
            return nc.alloc_semaphore(f"{name}_{what}")

        NK = NS // 512
        e32 = ctx.enter_context(nc.sbuf_tensor(f"{name}_e32", [P, 2, NS], F32))
        eh = ctx.enter_context(nc.sbuf_tensor(f"{name}_eh", [P, 2, SB, P], F16))
        el = ctx.enter_context(nc.sbuf_tensor(f"{name}_el", [P, 2, SB, P], F16))
        nmx = ctx.enter_context(nc.sbuf_tensor(f"{name}_nmx", [P, 2], F32))
        rs = ctx.enter_context(nc.sbuf_tensor(f"{name}_rs", [P, 2, 2], F32))
        part = ctx.enter_context(nc.sbuf_tensor(f"{name}_part", [P, 2, P], F32))
        LB = [ctx.enter_context(nc.psum_tensor(f"{name}_L{i}", [P, NS], F32)) for i in range(2)]
        TB = [ctx.enter_context(nc.psum_tensor(f"{name}_T{i}", [P, 4, P], F32)) for i in range(2)]
        OB = [ctx.enter_context(nc.psum_tensor(f"{name}_O{i}", [P, 512], F32)) for i in range(2)]
        logits, maxed, exped, transposed = sem("logits"), sem("maxed"), sem("exped"), sem("transposed")
        hi_ready, lo_ready, summed = sem("hi_ready"), sem("lo_ready"), sem("summed")
        inverse_ready, part_ready, main_added = sem("inverse_ready"), sem("part_ready"), sem("main_added")
        x_ready, stored = sem("x_ready"), sem("stored")
        block = ctx.enter_context(nc.Block(no_gpsimd_drain=True))
        STEPS = 2 * TILES

        def step(r, q):
            return 2 * r + q, r + q // 2, q % 2

        @block.tensor
        def _(pe):
            def logit(r, q):
                i, t, b = step(r, q)
                wait(pe, exped, i - 1)
                tok = bass.ds(b * SEQ + t * P, P)
                for k in range(NK):
                    out, sl = LB[b][:, k * 512:(k + 1) * 512], slice(k * 512, (k + 1) * 512)
                    nc.tensor.matmul(out, xT[:, 0, tok], c.seh[:, sl], start=True, stop=False)
                    nc.tensor.matmul(out, xT[:, 0, tok], c.sel[:, sl], start=False, stop=False)
                    last = nc.tensor.matmul(out, xT[:, 1, tok], c.seh[:, sl], start=False, stop=True)
                last.then_inc(logits, 1)

            def transpose(r, q):
                i, t, b = step(r, q)
                pe.wait_ge(exped, i + 1)
                for g in range(2):
                    wait(pe, lo_ready, 2 * i + g - 1)
                    for k in range(4):
                        col = (4 * g + k) * P
                        last = nc.tensor.transpose(TB[g][:, k, :], e32[:, b, col:col + P], c.ident[:, :])
                    last.then_inc(transposed, 1)

            def collect(r, q):
                i, t, b = step(r, q)
                wait(pe, main_added, i - 1)
                for k in range(SB):
                    if k % 4 == 0:
                        pe.wait_ge(lo_ready, 2 * i + k // 4 + 1)
                    nc.tensor.matmul(OB[b][:, 0:2 * P], eh[:, b, k, :], eo[:, b, k, :, :].rearrange("p h d -> p (h d)"),
                                     start=(k == 0), stop=False, skip_group_check=True)
                    last = nc.tensor.matmul(OB[b][:, 0:P], el[:, b, k, :], eo[:, b, k, 0, :],
                                            start=False, stop=(k == SB - 1), skip_group_check=True)
                last.then_inc(summed, 1)

            periods(pe, ((logit, 1), (transpose, 0), (collect, -1)), STEPS)

        @block.vector
        def _(dve):
            def peak(r, q):
                i, t, b = step(r, q)
                dve.wait_ge(logits, i + 1)
                wait(dve, exped, i - 1)
                nc.vector.tensor_reduce(nmx[:, b:b + 1], LB[b][:, :], AX.X, ALU.max, negate=True).then_inc(maxed, 1)

            def low(g):
                def piece(r, q):
                    i, t, b = step(r, q)
                    dve.wait_ge(hi_ready, 2 * i + g + 1)
                    sl = slice(4 * g, 4 * g + 4)
                    nc.vector.tensor_tensor(el[:, b, sl, :], TB[g][:, :, :], eh[:, b, sl, :], ALU.subtract)\
                        .then_inc(lo_ready, 1)
                return piece

            def inverse(r, q):
                i, t, b = step(r, q)
                dve.wait_ge(exped, i + 1)
                wait(dve, main_added, i - 1)
                wait(dve, part_ready, i - 1)
                nc.vector.reciprocal(rs[:, b, 1:2], rs[:, b, 0:1]).then_inc(inverse_ready, 1)

            def add(r, q):
                i, t, b = step(r, q)
                dve.wait_ge(part_ready, i + 1)
                xt = c.x[:, b, bass.ds(t, 1), :]
                nc.vector.scalar_tensor_tensor(out=xt, in0=OB[b][:, 0:P], scalar=rs[:, b, 1:2], in1=xt,
                                               op0=ALU.mult, op1=ALU.add).then_inc(main_added, 1)

            def stats(r, q):
                i, t, b = step(r, q)
                dve.wait_ge(x_ready, i + 1)
                nc.vector.bn_stats(c.st[:, bass.ds(b * TILES + t, 1), :], c.x[:, b, bass.ds(t, 1), :])

            plan = ((peak, 1), (add, -2), (inverse, 0), (low(0), 0), (low(1), 0))
            periods(dve, plan if store else plan + ((stats, -3),), STEPS)

        @block.gpsimd
        def _(pool):
            def add(r, q):
                i, t, b = step(r, q)
                pool.wait_ge(main_added, i + 1)
                xt = c.x[:, b, bass.ds(t, 1), :].rearrange("p a d -> p (a d)")
                nc.gpsimd.tensor_tensor(xt, xt, part[:, b, :], ALU.add).then_inc(x_ready, 1)

            periods(pool, ((add, -2),), STEPS)
            pool.wait_ge(x_ready, STEPS)

        @block.scalar
        def _(act):
            def exponential(r, q):
                i, t, b = step(r, q)
                act.wait_ge(maxed, i + 1)
                wait(act, transposed, 2 * i - 2)
                wait(act, inverse_ready, i - 1)
                nc.scalar.activation(e32[:, b, :], LB[b][:, :], ACT.Exp, bias=nmx[:, b:b + 1],
                                     accum_out=rs[:, b, 0:1]).then_inc(exped, 1)

            def high(g):
                def piece(r, q):
                    i, t, b = step(r, q)
                    act.wait_ge(transposed, 2 * i + g + 1)
                    wait(act, summed, i - 1)
                    nc.scalar.copy(eh[:, b, 4 * g:4 * g + 4, :], TB[g][:, :, :]).then_inc(hi_ready, 1)
                return piece

            def partial(r, q):
                i, t, b = step(r, q)
                act.wait_ge(summed, i + 1)
                act.wait_ge(inverse_ready, i + 1)
                wait(act, x_ready, i - 1)
                nc.scalar.activation(part[:, b, :], OB[b][:, P:2 * P], ACT.Copy, scale=rs[:, b, 1:2])\
                    .then_inc(part_ready, 1)

            periods(act, ((partial, -2), (high(0), 0), (high(1), 0), (exponential, 1)), STEPS)

        if store:
            @block.sync
            def _(sp):
                def save(r, q):
                    i, t, b = step(r, q)
                    sp.wait_ge(x_ready, i + 1)
                    dst = c.out_dram[b].rearrange("(t p) d -> p t d", p=P)
                    sp.dma_start(dst[:, bass.ds(t, 1), :], c.x[:, b, bass.ds(t, 1), :]).then_inc(stored, 16)

                with sp.Fori(0, TILES) as r:
                    save(r, 0)
                    save(r, 1)
                sp.wait_ge(stored, 16 * STEPS)


def moe(nc, c, name, store=False):
    with ExitStack() as ctx:
        xT = ctx.enter_context(nc.sbuf_tensor(f"{name}_xT", [P, 2, BATCH * SEQ], F16))
        sT = ctx.enter_context(nc.sbuf_tensor(f"{name}_sT", [P, SB, 2, BATCH, P], F16))
        eo = ctx.enter_context(nc.sbuf_tensor(f"{name}_eo", [P, BATCH, SB, 2, DM], F16))
        with ExitStack() as tokens:
            xh = tokens.enter_context(nc.sbuf_tensor(f"{name}_xh", [P, NT, 2, DM], F16))
            moe_dispatch(nc, c, f"{name}_disp", xh, xT, sT)
        moe_experts(nc, c, f"{name}_exp", sT, eo)
        moe_combine(nc, c, f"{name}_comb", xT, eo, store)


def ssm_inputs(nc, c, name, xT, dt_half, a, ecum, etot):
    with ExitStack() as ctx:
        def sem(what):
            return nc.alloc_semaphore(f"{name}_{what}")

        def sb(what, shape):
            return ctx.enter_context(nc.sbuf_tensor(f"{name}_{what}", shape, F32))

        G, NG = 4, NT // 4
        xn = sb("xn", [P, 2, G, DM])
        gain, shift = sb("gain", [P, NT]), sb("shift", [P, NT])
        raw, neg, ex, up, lg, rc = (sb(n, [P, NT, NH]) for n in ("raw", "neg", "ex", "up", "lg", "rc"))
        ea = sb("ea", [P, NH])
        ps = [ctx.enter_context(nc.psum_tensor(f"{name}_ps{i}", [P, G * P], F32)) for i in range(2)]
        DT = ctx.enter_context(nc.psum_tensor(f"{name}_DT", [P, 512], F32))
        CU = ctx.enter_context(nc.psum_tensor(f"{name}_CU", [P, 512], F32))
        sel_ready = sem("sel_ready")
        xn_ready, gain_ready, transposed = sem("xn_ready"), sem("gain_ready"), sem("transposed")
        xh_ready, xT_ready, dt_done = sem("xh_ready"), sem("xT_ready"), sem("dt_done")
        dve_step, neg_ready, act_step, a_ready, sums_done = (
            sem("dve_step"), sem("neg_ready"), sem("act_step"), sem("a_ready"), sem("sums_done"))
        xf = c.x[:, :, :, :].rearrange("p b t d -> p (b t) d")
        dts = DT[:, 0:NT * NH].rearrange("p (t h) -> p t h", h=NH)
        rows = RowScales(nc, c, ctx, "ssm_rows", [(c.r1, 1.0, LN_EPS), (c.s, 1 + RMS_EPS, LN_EPS * RMS_EPS)])
        block = ctx.enter_context(nc.Block(no_gpsimd_drain=True))

        @block.vector
        def _(dve):
            def normalise(r, q):
                g, pp = 2 * r + q, q % 2
                wait(dve, transposed, g - 1)
                for n in range(G):
                    t = bass.ds(g * G + n, 1)
                    last = nc.vector.tensor_scalar(xn[:, pp, n, :], xf[:, t, :], c.mean[:, t], c.s[:, t],
                                                   ALU.subtract, ALU.mult)
                last.then_inc(xn_ready, 1)

            def low(r, q):
                g, pp = 2 * r + q, q % 2
                dve.wait_ge(xh_ready, g + 1)
                cols = bass.ds(g * (G * P), G * P)
                nc.vector.tensor_tensor(xT[:, 1, cols], ps[pp][:, :], xT[:, 0, cols], ALU.subtract).then_inc(xT_ready, 1)

            rows.on_vector(dve)
            nc.vector.tensor_scalar(gain[:, :], c.r1[:, :], 1.0, None, ALU.add)
            nc.vector.scalar_tensor_tensor(out=shift[:, :], in0=c.mean[:, :], scalar=-1.0, in1=c.r1[:, :],
                                           op0=ALU.mult, op1=ALU.mult).then_inc(gain_ready, 1)
            periods(dve, ((normalise, 2), (low, 0)), NG, 1)
            dve.wait_ge(dt_done, NG)
            bias = c.dtb[:, :].unsqueeze(1).broadcast_to([P, NT, NH])
            chain(dve, dve_step, nc.vector.tensor_tensor(raw[:, :, :], dts, bias, ALU.add), 1)
            nc.vector.scalar_tensor_tensor(out=neg[:, :, :], in0=raw[:, :, :], scalar=-1.0, in1=raw[:, :, :],
                                           op0=ALU.mult, op1=ALU.min).then_inc(neg_ready, 1)
            dve.wait_ge(act_step, 2)
            chain(dve, dve_step, nc.vector.tensor_scalar(up[:, :, :], ex[:, :, :], 1.0, None, ALU.add), 2)
            nc.vector.reciprocal(rc[:, :, :], up[:, :, :]).then_inc(neg_ready, 1)
            chain(dve, dve_step, nc.vector.tensor_scalar(neg[:, :, :], up[:, :, :], -1.0, None, ALU.add), 3)
            chain(dve, dve_step, nc.vector.tensor_tensor(ex[:, :, :], ex[:, :, :], neg[:, :, :], ALU.subtract), 4)
            chain(dve, dve_step, nc.vector.tensor_tensor(ex[:, :, :], ex[:, :, :], rc[:, :, :], ALU.mult), 5)
            dve.wait_ge(act_step, 3)
            chain(dve, dve_step, nc.vector.tensor_tensor(lg[:, :, :], lg[:, :, :], ex[:, :, :], ALU.add), 6)
            chain(dve, dve_step, nc.vector.scalar_tensor_tensor(out=raw[:, :, :], in0=raw[:, :, :], scalar=0.0,
                                                                in1=lg[:, :, :], op0=ALU.max, op1=ALU.add), 7)
            nc.vector.tensor_scalar(dt_half[:, :, :], raw[:, :, :], 0.5, None, ALU.mult)
            nc.vector.scalar_tensor_tensor(out=a[:, :, :], in0=raw[:, :, :], scalar=-1.0,
                                           in1=ea[:, :].unsqueeze(1).broadcast_to([P, NT, NH]),
                                           op0=ALU.mult, op1=ALU.mult).then_inc(a_ready, 1)

        @block.gpsimd
        def _(pool):
            nc.gpsimd.tensor_tensor(c.sel[:, :], c.se32[:, :], c.seh[:, :], ALU.subtract).then_inc(sel_ready, 1)
            pool.wait_ge(sel_ready, 1)

        @block.tensor
        def _(pe):
            def transpose(r, q):
                g, pp = 2 * r + q, q % 2
                pe.wait_ge(xn_ready, g + 1)
                wait(pe, xT_ready, g - 1)
                for n in range(G):
                    last = nc.tensor.transpose(ps[pp][:, n * P:(n + 1) * P], xn[:, pp, n, :], c.ident[:, :])
                last.then_inc(transposed, 1)

            def project(r, q):
                g = 2 * r + q
                pe.wait_ge(xT_ready, g + 1)
                for n in range(G):
                    tok = bass.ds((g * G + n) * P, P)
                    last = split_product(nc, DT[:, bass.ds((g * G + n) * NH, NH)], (xT[:, 0, tok], xT[:, 1, tok]),
                                         (c.wph[:, PROJ:PROJ + NH], c.wpl[:, PROJ:PROJ + NH]))
                last.then_inc(dt_done, 1)

            periods(pe, ((transpose, 1), (project, -1)), NG, 1)
            pe.wait_ge(a_ready, 1)
            av = a[:, :, :].rearrange("p t h -> p (t h)")
            nc.tensor.matmul(CU[:, 0:P], c.upto[:, :], av, start=True, stop=True)
            nc.tensor.matmul(CU[:, P:2 * P], c.ones[:, :], av, start=True, stop=True).then_inc(sums_done, 1)

        @block.scalar
        def _(act):
            def high(r, q):
                g, pp = 2 * r + q, q % 2
                act.wait_ge(transposed, g + 1)
                nc.scalar.copy(xT[:, 0, bass.ds(g * (G * P), G * P)], ps[pp][:, :]).then_inc(xh_ready, 1)

            def add(r, q):
                g = 2 * r + q
                act.wait_ge(xn_ready, g + 1)
                for n in range(G):
                    t = bass.ds(g * G + n, 1)
                    nc.scalar.activation(xf[:, t, :], xf[:, t, :], ACT.Identity, scale=gain[:, t], bias=shift[:, t])

            rows.on_scalar(act)
            nc.scalar.activation(ea[:, :], c.alog[:, :], ACT.Exp).then_inc(act_step, 1)
            act.wait_ge(gain_ready, 1)
            periods(act, ((high, 0), (add, 0)), NG, 1)
            act.wait_ge(neg_ready, 1)
            nc.scalar.activation(ex[:, :, :], neg[:, :, :], ACT.Exp).then_inc(act_step, 1)
            act.wait_ge(neg_ready, 2)
            nc.scalar.activation(lg[:, :, :], up[:, :, :], ACT.Ln).then_inc(act_step, 1)
            act.wait_ge(sums_done, 1)
            nc.scalar.activation(ecum[:, :, :].rearrange("p t h -> p (t h)"), CU[:, 0:P], ACT.Exp)
            nc.scalar.activation(etot[:, :, :].rearrange("p t h -> p (t h)"), CU[:, P:2 * P], ACT.Exp)


def ssm_scan(nc, c, name, xT, dt_half, a, ecum, etot):
    with ExitStack() as ctx:
        def sem(what):
            return nc.alloc_semaphore(f"{name}_{what}")

        def sb(what, shape):
            return ctx.enter_context(nc.sbuf_tensor(f"{name}_{what}", shape, F32))

        HALO = TAPS - 1
        xs = sb("xs", [P, 2, 2, BATCH, HALO + P])
        bc = sb("bc", [P, 2, 2, BATCH, P])
        zt, zg = sb("zt", [P, 2, BATCH, P]), sb("zg", [P, 2, 2, BATCH, P])
        cv, th = sb("cv", [P, 2, BATCH, P]), sb("th", [P, 2, BATCH, P])
        xg = sb("xg", [P, 2, 2, BATCH, P])
        am, dd = sb("am", [P, BATCH, NH, P]), sb("dd", [P, BATCH, NH, P])
        gm, pr = sb("gm", [P, BATCH, P]), sb("pr", [P, BATCH, NH, P])
        xt, xw = sb("xt", [P, BATCH, NH, HD]), sb("xw", [P, BATCH, NH, HD])
        bt = sb("bt", [P, 2, BATCH, P])
        st = sb("st", [P, BATCH, NH, HD])
        yo, y = sb("yo", [P, BATCH, NH, HD]), sb("y", [P, BATCH, CH])
        gd, gt = sb("gd", [P, 2, BATCH, P]), sb("gt", [P, 2, BATCH, P])
        ew = sb("ew", [P, 2, EW])

        def pb(what, shape):
            return ctx.enter_context(nc.psum_tensor(f"{name}_{what}", shape, F32))

        ZB, XB, CB = pb("ZB", [P, 2, BATCH, P]), pb("XB", [P, 2, BATCH, P]), pb("CB", [P, 2, BATCH, P])
        DB = [pb("DB0", [P, NH, P]), pb("DB1", [P, NH, P])]
        GB = pb("GB", [P, 512])
        TB = pb("TB", [P, 512])
        YB = pb("YB", [P, 512])
        x_proj, bc_proj, z_proj, decay_done = sem("x_proj"), sem("bc_proj"), sem("z_proj"), sem("decay_done")
        cb_done, xt_done, y_done, st_done = sem("cb_done"), sem("xt_done"), sem("y_done"), sem("st_done")
        yT_done, out_done = sem("yT_done"), sem("out_done")
        xs_ready, bc_ready, zt_ready, tap_ready = sem("xs_ready"), sem("bc_ready"), sem("zt_ready"), sem("tap_ready")
        th_ready, dd_ready, bt_ready = sem("th_ready"), sem("dd_ready"), sem("bt_ready")
        gm_ready, xt_ready, xw_ready, x_added = sem("gm_ready"), sem("xt_ready"), sem("xw_ready"), sem("x_added")
        tap_step, cv_ready, xg_ready, zg_ready = sem("tap_step"), sem("cv_ready"), sem("xg_ready"), sem("zg_ready")
        yo_ready, y_ready, st_step, st_ready = sem("yo_ready"), sem("y_ready"), sem("st_step"), sem("st_ready")
        gd_ready, gt_ready = sem("gd_ready"), sem("gt_ready")
        am_ready, pr_ready = sem("am_ready"), sem("pr_ready")
        zeroed, from_state_done = sem("zeroed"), sem("from_state_done")
        CBf = CB[:, :, :, :].rearrange("p n b t -> p (n b t)")
        ew_in, ew_hi, ew_split = [sem("ew_in0"), sem("ew_in1")], sem("ew_hi"), sem("ew_split")
        K = TILES
        xTb = xT[:, :, :].rearrange("p s (b l) -> p s b l", b=BATCH)

        def of_tile(v, k):
            return v[:, :, :].rearrange("p (b t) h -> p b t h", b=BATCH)[:, :, bass.ds(k, 1), :]\
                .rearrange("p b a h -> p (b a) h")

        block = ctx.enter_context(nc.Block(no_gpsimd_drain=True))

        def at(r, q):
            return 2 * r + q, q % 2

        @block.tensor
        def _(pe):
            def project(bank, col, frees, done):
                def piece(r, q):
                    k, pp = at(r, q)
                    for free in frees:
                        wait(pe, free, k)
                    tokens = [xTb[:, half, :, bass.ds(k * P, P)] for half in range(2)]
                    for n in range(2):
                        cols = slice(col + n * P, col + (n + 1) * P)
                        last = split_product(nc, bank[:, n, :, :], (c.wph[:, cols], c.wpl[:, cols]), tokens)
                    last.then_inc(done, 1)
                return piece

            def decay(r, q):
                k, pp = at(r, q)
                pe.wait_ge(am_ready, k + 1)
                wait(pe, dd_ready, k)
                for b in range(BATCH):
                    last = nc.tensor.matmul(DB[b][:, :, :], c.after[:, :], am[:, b, :, :], start=True, stop=True)
                last.then_inc(decay_done, 1)

            def products(r, q):
                k, pp = at(r, q)
                pe.wait_ge(bc_ready, k + 1)
                for b in range(BATCH):
                    nc.tensor.matmul(CBf[:, b * P:(b + 1) * P], bc[:, pp, 0, b, :], bc[:, pp, 1, b, :],
                                     start=True, stop=True)
                for b in range(BATCH):
                    last = nc.tensor.transpose(CBf[:, (2 + b) * P:(3 + b) * P], bc[:, pp, 0, b, :], c.ident[:, :])
                last.then_inc(cb_done, 1)

            def x_transpose(r, q):
                k, pp = at(r, q)
                pe.wait_ge(xg_ready, k + 1)
                wait(pe, st_ready, k)
                for b in range(BATCH):
                    for n in range(2):
                        last = nc.tensor.transpose(TB[:, (2 * b + n) * P:(2 * b + n + 1) * P], xg[:, pp, n, b, :],
                                                   c.ident[:, :])
                last.then_inc(xt_done, 1)

            def from_state(r, q):
                k, pp = at(r, q)
                pe.wait_ge(bc_ready, k + 1)
                wait(pe, yo_ready, k)
                wait(pe, st_ready, k)
                for b in range(BATCH):
                    last = nc.tensor.matmul(GB[:, b * CH:(b + 1) * CH], bc[:, pp, 1, b, :], st[:, b, :, :],
                                            start=True, stop=True)
                last.then_inc(from_state_done, 1)

            def within(r, q):
                k, pp = at(r, q)
                pe.wait_ge(pr_ready, k + 1)
                pe.wait_ge(xt_ready, k + 1)
                wait(pe, x_added, k)
                for b in range(BATCH):
                    for h in range(NH):
                        col = b * CH + h * HD
                        last = nc.tensor.matmul(YB[:, col:col + HD], pr[:, b, h, :], xt[:, b, h, :], start=True, stop=True)
                last.then_inc(y_done, 1)

            def increment(r, q):
                k, pp = at(r, q)
                pe.wait_ge(bt_ready, k + 1)
                pe.wait_ge(xw_ready, k + 1)
                for b in range(BATCH):
                    last = nc.tensor.matmul(TB[:, b * CH:(b + 1) * CH], bt[:, pp, b, :], xw[:, b, :, :],
                                            start=True, stop=True)
                last.then_inc(st_done, 1)

            def y_transpose(r, q):
                k, pp = at(r, q)
                pe.wait_ge(y_ready, k + 1)
                for n in range(2):
                    for b in range(BATCH):
                        last = nc.tensor.transpose(YB[:, (2 * n + b) * P:(2 * n + b + 1) * P],
                                                   y[:, b, n * P:(n + 1) * P], c.ident[:, :])
                last.then_inc(yT_done, 1)

            def project_out(r, q):
                k, pp = at(r, q)
                pe.wait_ge(gt_ready, k + 1)
                for b in range(BATCH):
                    for n in range(2):
                        last = nc.tensor.matmul(YB[:, b * P:(b + 1) * P], gt[:, n, b, :], c.woutT[:, n, :],
                                                start=(n == 0), stop=(n == 1))
                last.then_inc(out_done, 1)

            pe.wait_ge(zeroed, 2)
            periods(pe, ((x_transpose, 0), (project(XB, CH, (xs_ready,), x_proj), 2), (from_state, 0),
                         (project_out, -1), (decay, 1), (within, 0), (products, 1), (increment, 0), (y_transpose, 0),
                         (project(ZB, 0, (zg_ready,), z_proj), 2),
                         (project(CB, 2 * CH, (bc_ready, gm_ready, bt_ready), bc_proj), 2)), K)

        @block.scalar
        def _(act):
            def x_copy(r, q):
                k, pp = at(r, q)
                act.wait_ge(x_proj, k + 1)
                wait(act, cv_ready, k - 1)
                if not (isinstance(k, int) and k == 0):
                    nc.scalar.copy(xs[:, pp, :, :, 0:HALO], xs[:, 1 - pp, :, :, P:P + HALO])
                chain(act, xs_ready, nc.scalar.copy(xs[:, pp, :, :, HALO:HALO + P], XB[:, :, :, :]), k + 1)

            def first_tap(r, q):
                k, pp = at(r, q)
                wait(act, xg_ready, k)
                for n in range(2):
                    last = nc.scalar.activation(cv[:, n, :, :], xs[:, pp, n, :, 0:P], ACT.Identity,
                                                scale=c.convw[:, n, 0:1], bias=c.convb[:, n:n + 1])
                last.then_inc(tap_ready, 1)

            def bc_copy(r, q):
                k, pp = at(r, q)
                act.wait_ge(bc_proj, k + 1)
                wait(act, from_state_done, k - 1)
                nc.scalar.copy(bc[:, pp, :, :, :], CB[:, :, :, :]).then_inc(bc_ready, 1)

            def z_tanh(r, q):
                k, pp = at(r, q)
                act.wait_ge(z_proj, k + 1)
                wait(act, zg_ready, k)
                nc.scalar.activation(zt[:, :, :, :], ZB[:, :, :, :], ACT.Tanh, scale=0.5).then_inc(zt_ready, 1)

            def state_part(r, q):
                k, pp = at(r, q)
                act.wait_ge(from_state_done, k + 1)
                wait(act, y_ready, k)
                for b in range(BATCH):
                    for h in range(NH):
                        col = b * CH + h * HD
                        last = nc.scalar.activation(yo[:, b, h, :], GB[:, col:col + HD], ACT.Copy,
                                                    scale=ecum[:, bass.ds(b * TILES + k, 1), h])
                last.then_inc(yo_ready, 1)

            def x_tanh(r, q):
                k, pp = at(r, q)
                act.wait_ge(cv_ready, k + 1)
                nc.scalar.activation(th[:, :, :, :], cv[:, :, :, :], ACT.Tanh, scale=0.5).then_inc(th_ready, 1)

            def decay_exp(r, q):
                k, pp = at(r, q)
                act.wait_ge(decay_done, k + 1)
                wait(act, pr_ready, k)
                wait(act, xw_ready, k)
                for b in range(BATCH):
                    last = nc.scalar.activation(dd[:, b, :, :], DB[b][:, :, :], ACT.Exp)
                last.then_inc(dd_ready, 1)

            def b_copy(r, q):
                k, pp = at(r, q)
                act.wait_ge(gm_ready, k + 1)
                wait(act, st_done, k - 1)
                nc.scalar.copy(bt[:, pp, :, :].rearrange("p b n -> p (b n)"), CBf[:, 2 * P:4 * P]).then_inc(bt_ready, 1)

            def high_weights(r, q):
                e, pp = at(r, q)
                act.wait_ge(ew_in[pp], 24 * (e - pp) + 48)
                nc.scalar.copy(c.ewh[:, bass.ds(e, 1), :], ew[:, pp, :].unsqueeze(1)).then_inc(ew_hi, 1)

            act.wait_ge(zeroed, 2)
            periods(act, ((x_copy, 1), (first_tap, 1), (bc_copy, 1), (z_tanh, 1), (state_part, 0), (x_tanh, 1),
                          (decay_exp, 1), (b_copy, 1), (high_weights, 1)), K)

        @block.gpsimd
        def _(pool):
            def decays(r, q):
                k, pp = at(r, q)
                wait(pool, decay_done, k)
                each = of_tile(a, k).unsqueeze(3).broadcast_to([P, BATCH, NH, P])
                upto = c.upto[:, :].unsqueeze(1).unsqueeze(1).broadcast_to([P, BATCH, NH, P])
                nc.gpsimd.tensor_tensor(am[:, :, :, :], upto, each, ALU.mult).then_inc(am_ready, 1)

            def masked(r, q):
                k, pp = at(r, q)
                pool.wait_ge(dd_ready, k + 1)
                pool.wait_ge(gm_ready, k + 1)
                wait(pool, y_done, k)
                nc.gpsimd.tensor_tensor(pr[:, :, :, :], dd[:, :, :, :],
                                        gm[:, :, :].unsqueeze(2).broadcast_to([P, BATCH, NH, P]), ALU.mult)\
                    .then_inc(pr_ready, 1)

            def weigh(r, q):
                k, pp = at(r, q)
                pool.wait_ge(xt_ready, k + 1)
                wait(pool, st_done, k)
                nc.gpsimd.tensor_tensor(xw[:, :, :, :], xt[:, :, :, :],
                                        dd[:, :, :, P - 1:P].broadcast_to([P, BATCH, NH, HD]), ALU.mult)\
                    .then_inc(xw_ready, 1)

            def fade(r, q):
                k, pp = at(r, q)
                pool.wait_ge(from_state_done, k + 1)
                wait(pool, st_ready, k)
                nc.gpsimd.tensor_tensor(st[:, :, :, :], st[:, :, :, :],
                                        of_tile(etot, k).unsqueeze(3).broadcast_to([P, BATCH, NH, HD]), ALU.mult)\
                    .then_inc(st_step, 1)

            def gate(r, q):
                k, pp = at(r, q)
                pool.wait_ge(gd_ready, k + 1)
                wait(pool, out_done, k)
                nc.gpsimd.tensor_tensor(gt[:, :, :, :], gd[:, :, :, :], zg[:, pp, :, :, :], ALU.mult)\
                    .then_inc(gt_ready, 1)

            def low_weights(r, q):
                e, pp = at(r, q)
                pool.wait_ge(ew_hi, e + 1)
                nc.gpsimd.tensor_tensor(c.ewl[:, bass.ds(e, 1), :], ew[:, pp, :].unsqueeze(1),
                                        c.ewh[:, bass.ds(e, 1), :], ALU.subtract).then_inc(ew_split, 1)

            nc.gpsimd.memset(xs[:, 0, :, :, 0:HALO], 0.0).then_inc(zeroed, 1)
            nc.gpsimd.memset(st[:, :, :, :], 0.0).then_inc(zeroed, 1)
            periods(pool, ((weigh, 0), (fade, 0), (decays, 2), (masked, 1), (gate, 0), (low_weights, 0)), K)
            pool.wait_ge(pr_ready, K)
            pool.wait_ge(st_step, K)
            pool.wait_ge(gt_ready, K)
            pool.wait_ge(ew_split, NE)

        @block.sync
        def _(sp):
            def load(e, pp):
                wait(sp, ew_split, e - 1)
                ee = bass.ds(e, 1)
                gate, up, down = (ew[:, pp, k * FF:(k + 1) * FF] for k in range(3))
                sp.dma_start(gate, c.Wg[ee, :, :].rearrange("a d f -> d (a f)")).then_inc(ew_in[pp], 16)
                sp.dma_start(up, c.Wu[ee, :, :].rearrange("a d f -> d (a f)")).then_inc(ew_in[pp], 16)
                sp.dma_start(down.rearrange("p (k o) -> p k o", o=DM),
                             c.Wd[ee, :, :].rearrange("a (k p) o -> p (a k) o", p=P)).then_inc(ew_in[pp], 16)

            load(0, 0)
            load(1, 1)
            with sp.Fori(1, NE // 2) as r:
                load(2 * r, 0)
                load(2 * r + 1, 1)

        @block.vector
        def _(dve):
            def flat(v):
                return v.rearrange("p n b t -> p (n b t)")

            def weighted_x(r, q):
                k, pp = at(r, q)
                dve.wait_ge(xt_done, k + 1)
                wait(dve, y_done, k)
                wait(dve, xw_ready, k)
                nc.vector.tensor_tensor(
                    xt[:, :, :, :], TB[:, :].rearrange("p (b h e) -> p b h e", b=BATCH, h=NH),
                    of_tile(dt_half, k).unsqueeze(3).broadcast_to([P, BATCH, NH, HD]), ALU.mult).then_inc(xt_ready, 1)

            def residual(r, q):
                k, pp = at(r, q)
                dve.wait_ge(out_done, k + 1)
                xk = c.x[:, :, bass.ds(k, 1), :].rearrange("p b a d -> p (b a) d")
                nc.vector.tensor_tensor(xk, YB[:, 0:BATCH * P].rearrange("p (b d) -> p b d", b=BATCH), xk, ALU.add)\
                    .then_inc(x_added, 1)

            def stats(r, q):
                k, pp = at(r, q)
                dve.wait_ge(x_added, k + 1)
                for b in range(BATCH):
                    nc.vector.bn_stats(c.st[:, bass.ds(b * TILES + k, 1), :], c.x[:, b, bass.ds(k, 1), :])

            def taps(r, q):
                k, pp = at(r, q)
                dve.wait_ge(tap_ready, k + 1)
                for tap in range(1, TAPS):
                    for n in range(2):
                        last = nc.vector.scalar_tensor_tensor(
                            out=cv[:, n, :, :], in0=xs[:, pp, n, :, tap:tap + P], scalar=c.convw[:, n, tap:tap + 1],
                            in1=cv[:, n, :, :], op0=ALU.mult, op1=ALU.add)
                    if tap < TAPS - 1:
                        chain(dve, tap_step, last, (TAPS - 2) * k + tap)
                last.then_inc(cv_ready, 1)

            def z_gate(r, q):
                k, pp = at(r, q)
                dve.wait_ge(zt_ready, k + 1)
                nc.vector.scalar_tensor_tensor(out=flat(zg[:, pp, :, :, :]), in0=flat(zt[:, :, :, :]), scalar=1.0,
                                               in1=flat(ZB[:, :, :, :]), op0=ALU.add, op1=ALU.mult).then_inc(zg_ready, 1)

            def x_gate(r, q):
                k, pp = at(r, q)
                dve.wait_ge(th_ready, k + 1)
                wait(dve, xt_done, k - 1)
                nc.vector.scalar_tensor_tensor(out=flat(xg[:, pp, :, :, :]), in0=flat(th[:, :, :, :]), scalar=1.0,
                                               in1=flat(cv[:, :, :, :]), op0=ALU.add, op1=ALU.mult).then_inc(xg_ready, 1)

            def causal(r, q):
                k, pp = at(r, q)
                dve.wait_ge(cb_done, k + 1)
                wait(dve, pr_ready, k)
                nc.vector.tensor_tensor(gm[:, :, :], CBf[:, 0:BATCH * P].rearrange("p (b t) -> p b t", b=BATCH),
                                        c.upto[:, :].unsqueeze(1).broadcast_to([P, BATCH, P]), ALU.mult)\
                    .then_inc(gm_ready, 1)

            def add_up(r, q):
                k, pp = at(r, q)
                dve.wait_ge(y_done, k + 1)
                dve.wait_ge(yo_ready, k + 1)
                wait(dve, yT_done, k)
                nc.vector.tensor_tensor(y[:, :, :].rearrange("p b e -> p (b e)"), YB[:, :],
                                        yo[:, :, :, :].rearrange("p b h e -> p (b h e)"), ALU.add).then_inc(y_ready, 1)

            def update(r, q):
                k, pp = at(r, q)
                dve.wait_ge(st_step, k + 1)
                dve.wait_ge(st_done, k + 1)
                nc.vector.tensor_tensor(st[:, :, :, :].rearrange("p b h e -> p (b h e)"),
                                        st[:, :, :, :].rearrange("p b h e -> p (b h e)"), TB[:, :], ALU.add)\
                    .then_inc(st_ready, 1)

            def skip(r, q):
                k, pp = at(r, q)
                dve.wait_ge(yT_done, k + 1)
                wait(dve, gt_ready, k)
                for n in range(2):
                    last = nc.vector.scalar_tensor_tensor(
                        out=gd[:, n, :, :].rearrange("p b t -> p (b t)"),
                        in0=xg[:, pp, n, :, :].rearrange("p b t -> p (b t)"), scalar=c.dcol[:, n:n + 1],
                        in1=YB[:, n * BATCH * P:(n + 1) * BATCH * P], op0=ALU.mult, op1=ALU.add)
                last.then_inc(gd_ready, 1)

            dve.wait_ge(zeroed, 2)
            periods(dve, ((weighted_x, 0), (taps, 1), (residual, -1), (z_gate, 1), (x_gate, 1), (add_up, 0),
                          (causal, 1), (update, 0), (skip, 0), (stats, -1)), K)


def ssm(nc, c):
    with ExitStack() as ctx:
        def sb(what, shape, dt=F32):
            return ctx.enter_context(nc.sbuf_tensor(f"ssm_{what}", shape, dt))

        xT = sb("xT", [P, 2, BATCH * SEQ], F16)
        tables = [sb(n, [P, NT, NH]) for n in ("dt_half", "a", "ecum", "etot")]
        ssm_inputs(nc, c, "ssm_in", xT, *tables)
        ssm_scan(nc, c, "ssm", xT, *tables)


def linear_attention(nc, c):
    with ExitStack() as ctx:
        def sem(what):
            return nc.alloc_semaphore(f"att_{what}")

        def sb(what, shape):
            return ctx.enter_context(nc.sbuf_tensor(f"att_{what}", shape, F32))

        KV = AH * AE * AD
        HE = AH * AE
        HEADS = ((0, 6), (6, 11), (11, 16))
        PARTS = len(HEADS)
        shift = sb("shift", [P, NT])
        xn, xT = sb("xn", [P, 2, DM]), sb("xT", [P, 2, P])
        ex, qk = sb("ex", [P, 2, 2 * DM]), sb("qk", [P, 2, 2 * DM])
        neg = sb("neg", [P, 2 * DM])
        vx, kv = sb("vx", [P, 2, AH, AE]), sb("kv", [P, 2, KV])
        qT, st = sb("qT", [P, 2, P]), sb("st", [P, BATCH, HE])
        w, half = sb("w", [P, 2, HE, AD]), sb("half", [P, 2, HE, AD // 2])
        inter, inc = sb("inter", [P, 2, HE]), sb("inc", [P, HE])
        own, num = sb("own", [P, AH, AE]), sb("num", [P, AH, AE])
        den, rden = sb("den", [P, AH]), sb("rden", [P, AH])
        o, oT = sb("o", [P, 2, DM]), sb("oT", [P, 2, P])

        def pb(what):
            return ctx.enter_context(nc.psum_tensor(f"att_{what}", [P, 512], F32))

        XB, QB, QT = pb("XB"), pb("QB"), pb("QT")
        CUM = [pb(f"CUM{n}") for n in range(PARTS)]
        IB, OB = pb("IB"), pb("OB")
        INTER = XB.ap()[:, 2 * P:2 * P + HE]
        xn_ready, x_transposed, xT_ready, qkv_done = sem("xn_ready"), sem("x_transposed"), sem("xT_ready"), sem("qkv_done")
        ex_ready, v_ready, negative_ready, qk_ready = sem("ex_ready"), sem("v_ready"), sem("negative_ready"), sem("qk_ready")
        kv_ready, q_transposed, qT_ready, inc_done = sem("kv_ready"), sem("q_transposed"), sem("qT_ready"), sem("inc_done")
        inter_done, inter_ready = sem("inter_done"), sem("inter_ready")
        cum_done, w_ready, folded = sem("cum_done"), sem("w_ready"), sem("folded")
        own_ready, num_ready, rden_ready = sem("own_ready"), sem("num_ready"), sem("rden_ready")
        o_ready, o_transposed, oT_ready, out_done = sem("o_ready"), sem("o_transposed"), sem("oT_ready"), sem("out_done")
        x_added, inc_masked, st_ready, zeroed = sem("x_added"), sem("inc_masked"), sem("st_ready"), sem("zeroed")
        shift_ready = sem("shift_ready")
        STEPS = 2 * TILES
        rows = RowScales(nc, c, ctx, "att_rows", [(c.r1, 1.0, LN_EPS)])
        block = ctx.enter_context(nc.Block(no_gpsimd_drain=True))

        def at(r, q):
            return 2 * r + q, r + q // 2, q % 2

        @block.tensor
        def _(pe):
            def x_transpose(r, q):
                i, t, b = at(r, q)
                pe.wait_ge(xn_ready, i + 1)
                wait(pe, xT_ready, i)
                nc.tensor.transpose(XB[:, 0:P], xn[:, b, :], c.ident[:, :]).then_inc(x_transposed, 1)

            def project(r, q):
                i, t, b = at(r, q)
                pe.wait_ge(xT_ready, i + 1)
                wait(pe, qk_ready, i)
                nc.tensor.matmul(QB[:, 0:3 * DM], xT[:, b, :], c.wqkvT[:, :], start=True, stop=True)\
                    .then_inc(qkv_done, 1)

            def q_transpose(r, q):
                i, t, b = at(r, q)
                pe.wait_ge(qk_ready, i + 1)
                wait(pe, qT_ready, i)
                nc.tensor.transpose(QT[:, 0:P], qk[:, b, 0:DM], c.ident[:, :]).then_inc(q_transposed, 1)

            def increment(r, q):
                i, t, b = at(r, q)
                pe.wait_ge(v_ready, i + 1)
                wait(pe, inc_masked, i)
                nc.tensor.matmul(IB[:, 0:HE], qk[:, b, DM:2 * DM], vx[:, b, :, :], start=True, stop=True)\
                    .then_inc(inc_done, 1)

            def from_state(r, q):
                i, t, b = at(r, q)
                pe.wait_ge(qT_ready, i + 1)
                wait(pe, st_ready, i - 1)
                wait(pe, inter_ready, i)
                nc.tensor.matmul(INTER, qT[:, b, :], st[:, b, :], start=True, stop=True).then_inc(inter_done, 1)

            def add_up(n):
                def piece(r, q):
                    i, t, b = at(r, q)
                    if n == 0:
                        pe.wait_ge(kv_ready, i + 1)
                    wait(pe, w_ready, PARTS * (i - 1) + n + 1)
                    lo, hi = (h * AE * AD for h in HEADS[n])
                    nc.tensor.matmul(CUM[n][:, 0:hi - lo], c.upto[:, :], kv[:, b, lo:hi], start=True, stop=True)\
                        .then_inc(cum_done, 1)
                return piece

            def o_transpose(r, q):
                i, t, b = at(r, q)
                pe.wait_ge(o_ready, i + 1)
                wait(pe, x_added, i)
                nc.tensor.transpose(OB[:, 0:P], o[:, b, :], c.ident[:, :]).then_inc(o_transposed, 1)

            def project_out(r, q):
                i, t, b = at(r, q)
                pe.wait_ge(oT_ready, i + 1)
                nc.tensor.matmul(OB[:, P:2 * P], oT[:, b, :], c.waoT[:, :], start=True, stop=True).then_inc(out_done, 1)

            pe.wait_ge(zeroed, 2)
            periods(pe, ((o_transpose, -2), (from_state, 1), (add_up(0), 1), (project_out, -2), (add_up(1), 1),
                         (x_transpose, 4), (add_up(2), 1), (q_transpose, 2), (increment, 2), (project, 3)),
                    STEPS, unroll=4)

        @block.scalar
        def _(act):
            def normalise(r, q):
                i, t, b = at(r, q)
                wait(act, x_transposed, i - 1)
                tt = bass.ds(b * TILES + t, 1)
                nc.scalar.activation(xn[:, b, :], c.x[:, b, bass.ds(t, 1), :].rearrange("p a d -> p (a d)"),
                                     ACT.Identity, scale=c.r1[:, tt], bias=shift[:, tt]).then_inc(xn_ready, 1)

            def o_copy(r, q):
                i, t, b = at(r, q)
                act.wait_ge(o_transposed, i + 1)
                wait(act, out_done, i - 1)
                nc.scalar.copy(oT[:, b, :], OB[:, 0:P]).then_inc(oT_ready, 1)

            def x_copy(r, q):
                i, t, b = at(r, q)
                act.wait_ge(x_transposed, i + 1)
                wait(act, qkv_done, i - 1)
                nc.scalar.copy(xT[:, b, :], XB[:, 0:P]).then_inc(xT_ready, 1)

            def q_copy(r, q):
                i, t, b = at(r, q)
                act.wait_ge(q_transposed, i + 1)
                wait(act, inter_done, i - 1)
                nc.scalar.copy(qT[:, b, :], QT[:, 0:P]).then_inc(qT_ready, 1)

            def exponential(r, q):
                i, t, b = at(r, q)
                act.wait_ge(qkv_done, i + 1)
                wait(act, qk_ready, i - 1)
                chain(act, negative_ready, nc.scalar.activation(neg[:, :], QB[:, 0:2 * DM], ACT.Relu, scale=-1.0), i + 1)
                nc.scalar.activation(ex[:, b, :], neg[:, :], ACT.Exp, scale=-1.0).then_inc(ex_ready, 1)
                wait(act, kv_ready, i - 1)
                wait(act, inc_done, i - 1)
                nc.scalar.copy(vx[:, b, :, 0:AD], QB[:, 2 * DM:3 * DM].rearrange("p (h e) -> p h e", e=AD))\
                    .then_inc(v_ready, 1)

            def inter_copy(r, q):
                i, t, b = at(r, q)
                act.wait_ge(inter_done, i + 1)
                wait(act, num_ready, i - 1)
                nc.scalar.copy(inter[:, b, :], INTER).then_inc(inter_ready, 1)

            rows.on_scalar(act)
            act.wait_ge(zeroed, 2)
            act.wait_ge(shift_ready, 1)
            periods(act, ((o_copy, -2), (normalise, 5), (x_copy, 4), (q_copy, 2), (inter_copy, 1), (exponential, 3)),
                    STEPS, unroll=4)

        @block.gpsimd
        def _(pool):
            def products(r, q):
                i, t, b = at(r, q)
                pool.wait_ge(qk_ready, i + 1)
                wait(pool, cum_done, PARTS * (i - 1))
                k = qk[:, b, DM:2 * DM].rearrange("p (h d) -> p h d", d=AD).unsqueeze(2)\
                    .broadcast_to([P, AH, AE, AD])
                v = vx[:, b, :, :].unsqueeze(3).broadcast_to([P, AH, AE, AD])
                nc.gpsimd.tensor_tensor(kv[:, b, :].rearrange("p (h e d) -> p h e d", h=AH, e=AE), k, v, ALU.mult)\
                    .then_inc(kv_ready, 1)

            def fold(r, q):
                i, t, b = at(r, q)
                pool.wait_ge(w_ready, PARTS * i + PARTS)
                wait(pool, own_ready, i - 1)
                nc.gpsimd.tensor_tensor(half[:, b, :, :], w[:, b, :, 0:AD // 2], w[:, b, :, AD // 2:AD], ALU.add)\
                    .then_inc(folded, 1)

            def update(r, q):
                i, t, b = at(r, q)
                pool.wait_ge(inc_masked, i + 1)
                pool.wait_ge(inter_done, i + 1)
                nc.gpsimd.tensor_tensor(st[:, b, :], st[:, b, :], inc[:, :], ALU.add).then_inc(st_ready, 1)

            nc.gpsimd.memset(vx[:, :, :, :], 1.0).then_inc(zeroed, 1)
            nc.gpsimd.memset(st[:, :, :], 0.0).then_inc(zeroed, 1)
            periods(pool, ((products, 2), (update, 1), (fold, 0)), STEPS, unroll=4)
            pool.wait_ge(kv_ready, STEPS)
            pool.wait_ge(folded, STEPS)
            pool.wait_ge(st_ready, STEPS)

        @block.vector
        def _(dve):
            def features(r, q):
                i, t, b = at(r, q)
                dve.wait_ge(ex_ready, i + 1)
                dve.wait_ge(v_ready, i + 1)
                wait(dve, w_ready, PARTS * (i - 1))
                wait(dve, kv_ready, i - 1)
                wait(dve, inc_done, i - 1)
                wait(dve, q_transposed, i - 1)
                nc.vector.scalar_tensor_tensor(out=qk[:, b, :], in0=QB[:, 0:2 * DM], scalar=0.0, in1=ex[:, b, :],
                                               op0=ALU.max, op1=ALU.add).then_inc(qk_ready, 1)

            def read(r, q):
                i, t, b = at(r, q)
                wait(dve, folded, i - 1)
                for n, (lo, hi) in enumerate(HEADS):
                    dve.wait_ge(cum_done, PARTS * i + n + 1)
                    qb = qk[:, b, lo * AD:hi * AD].rearrange("p (h d) -> p h d", d=AD).unsqueeze(2)\
                        .broadcast_to([P, hi - lo, AE, AD])
                    nc.vector.tensor_tensor(
                        w[:, b, lo * AE:hi * AE, :].rearrange("p (h e) d -> p h e d", e=AE),
                        CUM[n][:, 0:(hi - lo) * AE * AD].rearrange("p (h e d) -> p h e d", e=AE, d=AD),
                        qb, ALU.mult).then_inc(w_ready, 1)

            def reduce(r, q):
                i, t, b = at(r, q)
                dve.wait_ge(folded, i + 1)
                wait(dve, num_ready, i)
                nc.vector.tensor_reduce(own[:, :, :].rearrange("p h e -> p (h e)"), half[:, b, :, :], AX.X, ALU.add)\
                    .then_inc(own_ready, 1)

            def numerator(r, q):
                i, t, b = at(r, q)
                dve.wait_ge(own_ready, i + 1)
                dve.wait_ge(inter_ready, i + 1)
                wait(dve, o_ready, i)
                before = inter[:, b, :].rearrange("p (h e) -> p h e", e=AE)
                nc.vector.tensor_tensor(num[:, :, :], own[:, :, :], before, ALU.add)
                nc.vector.scalar_tensor_tensor(out=den[:, :], in0=own[:, :, AD], scalar=ATT_EPS, in1=before[:, :, AD],
                                               op0=ALU.add, op1=ALU.add).then_inc(num_ready, 1)

            def reciprocal(r, q):
                i, t, b = at(r, q)
                dve.wait_ge(num_ready, i + 1)
                nc.vector.reciprocal(rden[:, :], den[:, :]).then_inc(rden_ready, 1)

            def output(r, q):
                i, t, b = at(r, q)
                dve.wait_ge(rden_ready, i + 1)
                wait(dve, o_transposed, i - 1)
                nc.vector.tensor_tensor(o[:, b, :].rearrange("p (h e) -> p h e", e=AD), num[:, :, 0:AD],
                                        rden[:, :].unsqueeze(2).broadcast_to([P, AH, AD]), ALU.mult).then_inc(o_ready, 1)

            def mask_increment(r, q):
                i, t, b = at(r, q)
                dve.wait_ge(inc_done, i + 1)
                wait(dve, st_ready, i)
                nc.vector.tensor_tensor(inc[:, :], IB[:, 0:HE], c.mask_blk[:, :, :].rearrange("p h e -> p (h e)"),
                                        ALU.mult).then_inc(inc_masked, 1)

            def residual(r, q):
                i, t, b = at(r, q)
                dve.wait_ge(out_done, i + 1)
                xt = c.x[:, b, bass.ds(t, 1), :].rearrange("p a d -> p (a d)")
                nc.vector.tensor_tensor(xt, OB[:, P:2 * P], xt, ALU.add).then_inc(x_added, 1)

            def stats(r, q):
                i, t, b = at(r, q)
                dve.wait_ge(x_added, i + 1)
                nc.vector.bn_stats(c.st[:, bass.ds(b * TILES + t, 1), :], c.x[:, b, bass.ds(t, 1), :])

            rows.on_vector(dve)
            nc.vector.scalar_tensor_tensor(out=shift[:, :], in0=c.mean[:, :], scalar=-1.0, in1=c.r1[:, :],
                                           op0=ALU.mult, op1=ALU.mult).then_inc(shift_ready, 1)
            dve.wait_ge(zeroed, 2)
            periods(dve, ((read, 0), (features, 2), (reduce, -1), (mask_increment, 1), (numerator, -1),
                          (reciprocal, -1), (residual, -2), (output, -1), (stats, -2)), STEPS, unroll=4)


STAGES = [ssm, lambda nc, c: moe(nc, c, "moe1"), linear_attention, lambda nc, c: moe(nc, c, "moe2", store=True)]


def build(nc, c, stages):
    with ExitStack() as ctx:
        def sb(name, shape, dt=F32):
            return ctx.enter_context(nc.sbuf_tensor(name, shape, dt))

        c.x = sb("x_res", [P, BATCH, TILES, DM])
        c.ident, c.ones = sb("ident", [P, P]), sb("ones", [P, P])
        c.upto, c.after = sb("upto", [P, P]), sb("after", [P, P])
        c.st = sb("st", [P, NT, 6])
        c.mask_blk = sb("mask_blk", [P, AH, AE])
        c.wph, c.wpl = sb("wph", [P, PROJ + NH], F16), sb("wpl", [P, PROJ + NH], F16)
        c.woutT = sb("woutT", [P, 2, DM])
        c.wqkvT, c.waoT = sb("wqkvT", [P, 3 * DM]), sb("waoT", [P, DM])
        c.se32 = sb("se32", [P, NS])
        c.seh, c.sel = sb("seh", [P, NS], F16), sb("sel", [P, NS], F16)
        c.bgT, c.buT, c.bdT = sb("bgT", [P, 2, NE]), sb("buT", [P, 2, NE]), sb("bdT", [P, NE])
        c.ewh, c.ewl = sb("ewh", [P, NE, EW], F16), sb("ewl", [P, NE, EW], F16)
        c.gcol, c.bcol = sb("gcol", [P, 1]), sb("bcol", [P, 1])
        c.convw, c.convb, c.dcol = sb("convw", [P, 2, TAPS]), sb("convb", [P, 2]), sb("dcol", [P, 2])
        c.alog, c.dtb = sb("alog", [P, NH]), sb("dtb", [P, NH])
        c.mean, c.r1, c.s = sb("mean", [P, NT]), sb("r1", [P, NT]), sb("s", [P, NT])
        prepare(nc, c)
        for stage in stages[:-1]:
            with nc.cleanup_on_exit():
                stage(nc, c)
        stages[-1](nc, c)


NAMES = dict(L0_attn_a_x="x_dram", L0_attn_a_norm_w="norm_w", L0_attn_a_in_proj_w="in_proj_w",
             L0_attn_a_conv_w="conv_w", L0_attn_a_conv_b="conv_b", L0_attn_a_A_log="A_log", L0_attn_a_D="D_skip",
             L0_attn_a_dt_bias="dt_bias", L0_attn_a_out_proj_w="out_proj_w", L0_attn_b_Wq="Wq", L0_attn_b_Wk="Wk",
             L0_attn_b_Wv="Wv", L0_attn_b_Wo="Wo", L0_ffn_norm_g="norm_g", L0_ffn_norm_b="norm_b",
             L0_ffn_slot_g="slot_g", L0_ffn_slot_b="slot_b", L0_ffn_scale="scale", L0_ffn_slot_embeds="slot_embeds",
             L0_ffn_Wg="Wg", L0_ffn_bg="bg", L0_ffn_Wu="Wu", L0_ffn_bu="bu", L0_ffn_Wd="Wd", L0_ffn_bd="bd")


def kernel(**inputs):
    import numpy as _np
    import concourse.bacc as _bacc
    from concourse import mybir as _mybir
    from concourse.bass_utils import run_bass_kernel_spmd as _run

    nc = _bacc.Bacc("TRN2", target_bir_lowering=False, num_devices=1)
    core, arrays = Core(), {}
    args = {}
    for name, short in NAMES.items():
        a = _np.ascontiguousarray(inputs[name])
        arrays[f"in_{short}"] = a
        args[short] = nc.dram_tensor(f"in_{short}", a.shape, _mybir.dt.from_np(a.dtype), kind="ExternalInput").ap()
    core.__dict__.update(args)
    core.out_dram = nc.dram_tensor("out", (BATCH, SEQ, DM), _mybir.dt.float32, kind="ExternalOutput").ap()
    build(nc, core, STAGES)
    r = _run(nc, [arrays], core_ids=[0])
    return r.results[0]["out"]
```
